# Optimizing a Trainium2 kernel written in Bass

```python
import numpy as np
import jax
import jax.numpy as jnp

def _softmax(x, axis=-1):
    return jax.nn.softmax(x, axis=axis)

def _gelu(x):
    return jax.nn.gelu(x, approximate=True)

def _silu(x):
    return jax.nn.silu(x)

def _sigmoid(x):
    return jax.nn.sigmoid(x)

def _layernorm(x, axis=-1, eps=1e-05):
    m = jnp.mean(x, axis=axis, keepdims=True)
    v = jnp.var(x, axis=axis, keepdims=True)
    return (x - m) / jnp.sqrt(v + eps)

def _scatter_add(tgt, idx, src, axis=0):
    return tgt.at[idx].add(src)

def _segment_sum(src, seg, n):
    return jax.ops.segment_sum(src, seg, n)
kernel_name = 'mk_gnn_resnorm_d4_gnn_r8_881cba'

def setup_inputs(seed: int=0):
    np.random.seed(seed)
    _w = jnp.asarray

    def _rec_inputs():
        import jax
        import jax.numpy as jnp
        _gk = jax.random.key(seed)
        x = -0.0009044 + 1 * jax.random.normal(jax.random.fold_in(_gk, 1), (12500, 16), jnp.float32)
        src = jax.random.randint(jax.random.fold_in(_gk, 2), (400000,), 0, 12500, jnp.int32)
        dst = jax.random.randint(jax.random.fold_in(_gk, 3), (400000,), 0, 12500, jnp.int32)
        _o = jnp.argsort(dst, stable=True)
        src = src[_o]
        dst = dst[_o]
        edge_attr_8 = -5.3897e-05 + 0.999841 * jax.random.normal(jax.random.fold_in(_gk, 11), (400000, 8), jnp.float32)
        node_vec1 = -0.00472126 + 0.997171 * jax.random.normal(jax.random.fold_in(_gk, 13), (12500, 1), jnp.float32)
        return (x, src, dst, edge_attr_8, node_vec1)
    x, src, dst, edge_attr_8, node_vec1 = _rec_inputs()

    def _L0_gnn_setup():
        import jax, jax.numpy as jnp
        import numpy as np
        N = 12500
        E = 100000
        F_IN = 16
        H1, C1 = (3, 32)
        H2, C2 = (1, 32)
        NC = 16
        SLOPE = 0.2

        def _gat_layer(x, src, dst, W, a_s, a_d, b, heads, outc):
            h = (x @ W).reshape(N, heads, outc)
            alpha_s = (h * a_s).sum(-1)
            alpha_d = (h * a_d).sum(-1)
            e = jax.nn.leaky_relu(alpha_s[src] + alpha_d[dst], SLOPE)
            m = jax.ops.segment_max(e, dst, num_segments=N)
            p = jnp.exp(e - m[dst])
            z = jax.ops.segment_sum(p, dst, num_segments=N)
            alpha = p / (z[dst] + 1e-16)
            out = jax.ops.segment_sum(h[src] * alpha[:, :, None], dst, num_segments=N)
            return out.reshape(N, heads * outc) + b
        key = jax.random.key(seed)
        ks = jax.random.split(key, 12)
        s = 0.1
        return {'x': jax.random.normal(ks[0], (N, F_IN), jnp.float32), 'edge_index': jax.random.randint(ks[1], (2, E), 0, N, dtype=jnp.int32), 'W1': jax.random.normal(ks[2], (F_IN, H1 * C1), jnp.float32) * s, 'a_src1': jax.random.normal(ks[3], (H1, C1), jnp.float32) * s, 'a_dst1': jax.random.normal(ks[4], (H1, C1), jnp.float32) * s, 'b1': jnp.zeros((H1 * C1,), jnp.float32), 'W2': jax.random.normal(ks[5], (H1 * C1, H2 * C2), jnp.float32) * s, 'a_src2': jax.random.normal(ks[6], (H2, C2), jnp.float32) * s, 'a_dst2': jax.random.normal(ks[7], (H2, C2), jnp.float32) * s, 'b2': jnp.zeros((H2 * C2,), jnp.float32), 'Wf': jax.random.normal(ks[8], (C2, NC), jnp.float32) * s, 'bf': jnp.zeros((NC,), jnp.float32)}
    _L0_gnn_all = _L0_gnn_setup()
    _L0_gnn_in = {k: v for k, v in _L0_gnn_all.items() if k in ('W1', 'a_src1', 'a_dst1', 'b1', 'W2', 'a_src2', 'a_dst2', 'b2', 'Wf', 'bf')}
    del _L0_gnn_all

    def _L1_gnn_setup():
        import jax, jax.numpy as jnp
        import numpy as np
        BN_EPS = 1e-05

        def gcn_conv(x, edge_index, W, b, num_nodes):
            src, dst = (edge_index[0], edge_index[1])
            loop = jnp.arange(num_nodes, dtype=edge_index.dtype)
            src_f = jnp.concatenate([src, loop])
            dst_f = jnp.concatenate([dst, loop])
            deg = jax.ops.segment_sum(jnp.ones_like(dst_f, dtype=x.dtype), dst_f, num_segments=num_nodes)
            dinv = jnp.where(deg > 0, jax.lax.rsqrt(deg), 0.0)
            norm = dinv[src_f] * dinv[dst_f]
            h = x @ W
            msg = h[src_f] * norm[:, None]
            out = jax.ops.segment_sum(msg, dst_f, num_segments=num_nodes)
            return out + b
        key = jax.random.key(seed)
        k = jax.random.split(key, 6)
        N, E, D, H = (12500, 250000, 16, 32)
        x = jax.random.normal(k[0], (N, D), dtype=jnp.float32)
        edge_index = jax.random.randint(k[1], (2, E), 0, N, dtype=jnp.int64)
        W1 = jax.random.normal(k[2], (D, H), dtype=jnp.float32) / np.sqrt(D)
        b1 = jnp.zeros((H,), dtype=jnp.float32)
        gamma = jnp.ones((H,), dtype=jnp.float32)
        beta = jnp.zeros((H,), dtype=jnp.float32)
        W2 = jax.random.normal(k[3], (H, D), dtype=jnp.float32) / np.sqrt(H)
        b2 = jnp.zeros((D,), dtype=jnp.float32)
        return {'x': x, 'edge_index': edge_index, 'W1': W1, 'b1': b1, 'gamma': gamma, 'beta': beta, 'W2': W2, 'b2': b2, 'num_nodes': N}
    _L1_gnn_all = _L1_gnn_setup()
    _L1_gnn_in = {k: v for k, v in _L1_gnn_all.items() if k in ('W1', 'b1', 'gamma', 'beta', 'W2', 'b2')}
    del _L1_gnn_all

    def _L2_gnn_setup():
        import jax, jax.numpy as jnp
        import numpy as np
        STALK_DIM = 16
        N_NODES = 6250
        N_EDGES = 50000
        HIDDEN = 64
        key = jax.random.key(seed)
        k1, k2, k3, k4 = jax.random.split(key, 4)
        d = STALK_DIM
        x = jax.random.normal(k1, (N_NODES, d), dtype=jnp.float32)
        edge_index = jax.random.randint(k2, (2, N_EDGES), 0, N_NODES, dtype=jnp.int64)
        W1 = jax.random.normal(k3, (HIDDEN, 2 * d), dtype=jnp.float32) * (1.0 / np.sqrt(2 * d))
        b1 = jnp.zeros((HIDDEN,), dtype=jnp.float32)
        W2 = jax.random.normal(k4, (d, HIDDEN), dtype=jnp.float32) * (1.0 / np.sqrt(HIDDEN))
        b2 = jnp.zeros((d,), dtype=jnp.float32)
        return {'x': x, 'edge_index': edge_index, 'W1': W1, 'b1': b1, 'W2': W2, 'b2': b2}
    _L2_gnn_all = _L2_gnn_setup()
    _L2_gnn_in = {k: v for k, v in _L2_gnn_all.items() if k in ('W1', 'b1', 'W2', 'b2')}
    del _L2_gnn_all

    def _L3_gnn_setup():
        import jax, jax.numpy as jnp
        import numpy as np
        N_NODES = 12500
        N_EDGES = 400000
        D_NODE = 16
        D_EDGE = 8
        D_HIDDEN = 16
        key = jax.random.key(seed)
        ks = jax.random.split(key, 8)
        node_features = jax.random.normal(ks[0], (N_NODES, D_NODE), dtype=jnp.float32)
        edge_attr_e3nn = jax.random.normal(ks[1], (N_EDGES, D_EDGE), dtype=jnp.float32)
        node_attr_scalar_raw = jax.random.normal(ks[2], (N_NODES, 1), dtype=jnp.float32)
        W_msg_tp = jax.random.normal(ks[3], (D_NODE, D_EDGE, D_HIDDEN), dtype=jnp.float32)
        W_msg_lin = jax.random.normal(ks[4], (D_HIDDEN, D_HIDDEN), dtype=jnp.float32)
        W_upd_tp = jax.random.normal(ks[5], (D_NODE, D_HIDDEN, D_HIDDEN), dtype=jnp.float32)
        W_upd_lin = jax.random.normal(ks[6], (D_HIDDEN, D_NODE), dtype=jnp.float32)
        edge_index = jax.random.randint(ks[7], (2, N_EDGES), 0, N_NODES, dtype=jnp.int64)
        return {'node_features': node_features, 'edge_attr_e3nn': edge_attr_e3nn, 'node_attr_scalar_raw': node_attr_scalar_raw, 'W_msg_tp': W_msg_tp, 'W_msg_lin': W_msg_lin, 'W_upd_tp': W_upd_tp, 'W_upd_lin': W_upd_lin, 'edge_index': edge_index}
    _L3_gnn_all = _L3_gnn_setup()
    _L3_gnn_in = {k: v for k, v in _L3_gnn_all.items() if k in ('W_msg_tp', 'W_msg_lin', 'W_upd_tp', 'W_upd_lin')}
    del _L3_gnn_all
    return {'x': x, 'src': src, 'dst': dst, 'edge_attr_8': edge_attr_8, 'node_vec1': node_vec1, 'L0_gnn_W1': _L0_gnn_in['W1'], 'L0_gnn_a_src1': _L0_gnn_in['a_src1'], 'L0_gnn_a_dst1': _L0_gnn_in['a_dst1'], 'L0_gnn_b1': _L0_gnn_in['b1'], 'L0_gnn_W2': _L0_gnn_in['W2'], 'L0_gnn_a_src2': _L0_gnn_in['a_src2'], 'L0_gnn_a_dst2': _L0_gnn_in['a_dst2'], 'L0_gnn_b2': _L0_gnn_in['b2'], 'L0_gnn_Wf': _L0_gnn_in['Wf'], 'L0_gnn_bf': _L0_gnn_in['bf'], 'L1_gnn_W1': _L1_gnn_in['W1'], 'L1_gnn_b1': _L1_gnn_in['b1'], 'L1_gnn_gamma': _L1_gnn_in['gamma'], 'L1_gnn_beta': _L1_gnn_in['beta'], 'L1_gnn_W2': _L1_gnn_in['W2'], 'L1_gnn_b2': _L1_gnn_in['b2'], 'L2_gnn_W1': _L2_gnn_in['W1'], 'L2_gnn_b1': _L2_gnn_in['b1'], 'L2_gnn_W2': _L2_gnn_in['W2'], 'L2_gnn_b2': _L2_gnn_in['b2'], 'L3_gnn_W_msg_tp': _L3_gnn_in['W_msg_tp'], 'L3_gnn_W_msg_lin': _L3_gnn_in['W_msg_lin'], 'L3_gnn_W_upd_tp': _L3_gnn_in['W_upd_tp'], 'L3_gnn_W_upd_lin': _L3_gnn_in['W_upd_lin']}

def reference(x, src, dst, edge_attr_8, node_vec1, L0_gnn_W1, L0_gnn_a_src1, L0_gnn_a_dst1, L0_gnn_b1, L0_gnn_W2, L0_gnn_a_src2, L0_gnn_a_dst2, L0_gnn_b2, L0_gnn_Wf, L0_gnn_bf, L1_gnn_W1, L1_gnn_b1, L1_gnn_gamma, L1_gnn_beta, L1_gnn_W2, L1_gnn_b2, L2_gnn_W1, L2_gnn_b1, L2_gnn_W2, L2_gnn_b2, L3_gnn_W_msg_tp, L3_gnn_W_msg_lin, L3_gnn_W_upd_tp, L3_gnn_W_upd_lin):
    import jax
    import jax.numpy as jnp

    def _L0_gnn_ref(x, edge_index, W1, a_src1, a_dst1, b1, W2, a_src2, a_dst2, b2, Wf, bf):
        import jax, jax.numpy as jnp
        import numpy as np
        N = 12500
        E = 100000
        F_IN = 16
        H1, C1 = (3, 32)
        H2, C2 = (1, 32)
        NC = 16
        SLOPE = 0.2

        def _gat_layer(x, src, dst, W, a_s, a_d, b, heads, outc):
            h = (x @ W).reshape(N, heads, outc)
            alpha_s = (h * a_s).sum(-1)
            alpha_d = (h * a_d).sum(-1)
            e = jax.nn.leaky_relu(alpha_s[src] + alpha_d[dst], SLOPE)
            m = jax.ops.segment_max(e, dst, num_segments=N)
            p = jnp.exp(e - m[dst])
            z = jax.ops.segment_sum(p, dst, num_segments=N)
            alpha = p / (z[dst] + 1e-16)
            out = jax.ops.segment_sum(h[src] * alpha[:, :, None], dst, num_segments=N)
            return out.reshape(N, heads * outc) + b
        loops = jnp.arange(N, dtype=edge_index.dtype)
        src = jnp.concatenate([edge_index[0], loops])
        dst = jnp.concatenate([edge_index[1], loops])
        h = jax.nn.selu(_gat_layer(x, src, dst, W1, a_src1, a_dst1, b1, H1, C1))
        h = jax.nn.selu(_gat_layer(h, src, dst, W2, a_src2, a_dst2, b2, H2, C2))
        return h @ Wf + bf

    def _L1_gnn_ref(x, edge_index, W1, b1, gamma, beta, W2, b2, num_nodes):
        import jax, jax.numpy as jnp
        import numpy as np
        BN_EPS = 1e-05

        def gcn_conv(x, edge_index, W, b, num_nodes):
            src, dst = (edge_index[0], edge_index[1])
            loop = jnp.arange(num_nodes, dtype=edge_index.dtype)
            src_f = jnp.concatenate([src, loop])
            dst_f = jnp.concatenate([dst, loop])
            deg = jax.ops.segment_sum(jnp.ones_like(dst_f, dtype=x.dtype), dst_f, num_segments=num_nodes)
            dinv = jnp.where(deg > 0, jax.lax.rsqrt(deg), 0.0)
            norm = dinv[src_f] * dinv[dst_f]
            h = x @ W
            msg = h[src_f] * norm[:, None]
            out = jax.ops.segment_sum(msg, dst_f, num_segments=num_nodes)
            return out + b
        h = gcn_conv(x, edge_index, W1, b1, num_nodes)
        mean = jnp.mean(h, axis=0)
        var = jnp.var(h, axis=0)
        h = (h - mean) * jax.lax.rsqrt(var + BN_EPS) * gamma + beta
        h = jax.nn.relu(h)
        out = gcn_conv(h, edge_index, W2, b2, num_nodes)
        return out

    def _L2_gnn_ref(x, edge_index, W1, b1, W2, b2):
        import jax, jax.numpy as jnp
        import numpy as np
        STALK_DIM = 16
        N_NODES = 6250
        N_EDGES = 50000
        HIDDEN = 64
        d = x.shape[1]
        n = x.shape[0]
        src, dst = (edge_index[0], edge_index[1])
        xs, xd = (x[src], x[dst])

        def reflection(a, b):
            h = jax.nn.relu(jnp.concatenate([a, b], axis=1) @ W1.T + b1)
            return h @ W2.T + b2

        def householder(v):
            vn = v / jnp.maximum(jnp.linalg.norm(v, axis=1, keepdims=True), 1e-12)
            return jnp.eye(d, dtype=v.dtype)[None] - 2.0 * vn[:, :, None] * vn[:, None, :]
        F_s = householder(reflection(xs, xd))
        F_d = householder(reflection(xd, xs))
        L_sd = -jnp.einsum('eki,ekj->eij', F_s, F_d)
        ones_e = jnp.ones(src.shape[0], dtype=x.dtype)
        deg = jnp.zeros(n, dtype=x.dtype).at[src].add(ones_e).at[dst].add(ones_e)
        deg_inv_sqrt = 1.0 / jnp.sqrt(jnp.maximum(deg, 1e-05))
        coef = deg_inv_sqrt[src] * deg_inv_sqrt[dst]
        msg_s = coef[:, None] * jnp.einsum('eij,ej->ei', L_sd, xd)
        msg_d = coef[:, None] * jnp.einsum('eji,ej->ei', L_sd, xs)
        out = x - jnp.zeros_like(x).at[src].add(msg_s) - jnp.zeros_like(x).at[dst].add(msg_d)
        return jax.nn.relu(out)

    def _L3_gnn_ref(node_features, edge_attr_e3nn, node_attr_scalar_raw, W_msg_tp, W_msg_lin, W_upd_tp, W_upd_lin, edge_index):
        import jax, jax.numpy as jnp
        import numpy as np
        N_NODES = 12500
        N_EDGES = 400000
        D_NODE = 16
        D_EDGE = 8
        D_HIDDEN = 16
        n_nodes = node_features.shape[0]
        row = edge_index[0]
        col = edge_index[1]
        norm_msg_tp = 1.0 / np.float32(np.sqrt(D_NODE * D_EDGE))
        norm_upd_tp = 1.0 / np.float32(np.sqrt(D_NODE * D_HIDDEN))
        norm_lin = 1.0 / np.float32(np.sqrt(D_HIDDEN))
        x_j = node_features[col]
        m = jnp.einsum('ei,ej,ijh->eh', x_j, edge_attr_e3nn, W_msg_tp) * norm_msg_tp
        m = jax.nn.silu(m)
        m = m @ W_msg_lin * norm_lin
        agg = jax.ops.segment_sum(m, row, num_segments=n_nodes)
        u = jnp.einsum('ni,nh,ihk->nk', node_features, agg, W_upd_tp) * norm_upd_tp
        u = jax.nn.silu(u)
        u = u @ W_upd_lin * norm_lin
        return node_features + u
    edge_index = jnp.stack([src, dst])
    x = _layernorm(x + _L0_gnn_ref(x, edge_index, L0_gnn_W1, L0_gnn_a_src1, L0_gnn_a_dst1, L0_gnn_b1, L0_gnn_W2, L0_gnn_a_src2, L0_gnn_a_dst2, L0_gnn_b2, L0_gnn_Wf, L0_gnn_bf), axis=-1)
    x = _layernorm(x + _L1_gnn_ref(x, edge_index, L1_gnn_W1, L1_gnn_b1, L1_gnn_gamma, L1_gnn_beta, L1_gnn_W2, L1_gnn_b2, 12500), axis=-1)
    x = _layernorm(x + _L2_gnn_ref(x, edge_index, L2_gnn_W1, L2_gnn_b1, L2_gnn_W2, L2_gnn_b2), axis=-1)
    x = _layernorm(x + _L3_gnn_ref(x, edge_attr_8, node_vec1, L3_gnn_W_msg_tp, L3_gnn_W_msg_lin, L3_gnn_W_upd_tp, L3_gnn_W_upd_lin, edge_index), axis=-1)
    return x

_drawn_inputs = setup_inputs


def setup_inputs(seed=0):
    import zlib

    import numpy as np

    out = dict(_drawn_inputs(seed))
    spreads = {'L0_gnn_b1': (0.0, 0.1),
     'L0_gnn_b2': (0.0, 0.1),
     'L0_gnn_bf': (0.0, 0.1),
     'L1_gnn_b1': (0.0, 2.0),
     'L1_gnn_gamma': (1.0, 0.2),
     'L1_gnn_beta': (0.0, 0.1),
     'L1_gnn_b2': (0.0, 0.1),
     'L2_gnn_b1': (0.0, 0.8),
     'L2_gnn_b2': (0.0, 0.458)}
    factors = {'L0_gnn_a_dst1': 64.0,
     'L0_gnn_a_src2': 28.711,
     'L0_gnn_a_dst2': 64.0,
     'L0_gnn_a_src1': 2.728}
    for name, (base, spread) in spreads.items():
        noise = np.random.default_rng([zlib.crc32(name.encode()), seed]).standard_normal(out[name].shape)
        drawn = base * np.exp(spread * noise) if base else spread * noise
        out[name] = jnp.asarray(drawn.astype(out[name].dtype))
    for name, factor in factors.items():
        out[name] = (out[name] * factor).astype(out[name].dtype)
    return out
```

```python
import numpy as np
import concourse.bass as bass
from concourse import mybir
from contextlib import ExitStack

F32 = mybir.dt.float32
BF16 = mybir.dt.bfloat16
I32 = mybir.dt.int32
ALU = mybir.AluOpType
ACT = mybir.ActivationFunctionType
AX = mybir.AxisListType

P = 128
N, E = 12500, 400000
LANE = E // P
CH = 125
NCH = LANE // CH
PAIRS = NCH // 2
GRP = 5
NG = CH // GRP
NT = 100
NP = NT * P
XT = 25
FULL, REST = N // P, N % P
D = 16
H1, C1 = 3, 32
C2 = 32
HID = 64
DE = 8
BIG = 1e30
SELU_ALPHA, SELU_SCALE = 1.6732632423543772, 1.0507009873554805


class Chain:

    def __init__(self, eng, sem):
        self.eng, self.sem, self.n, self.base, self.starts = eng, sem, 0, [], []

    def __call__(self, ins):
        self.n += 1
        ins.then_inc(self.sem, 1)
        self.eng.wait_ge(self.sem, sum(self.base[1:], self.base[0]) + self.n if self.base else self.n)

    def enter(self, i, per):
        self.base.append(i * per)
        self.starts.append(self.n)

    def leave(self, count, per):
        assert self.n - self.starts[-1] == per, (self.n - self.starts[-1], per)
        self.n = self.starts.pop() + count * per
        self.base.pop()


def over_chunks(eng, body, chain=None, per=0):
    with eng.Fori(0, PAIRS) as j:
        if chain:
            chain.enter(j, 2 * per)
        body(2 * j, 0, j)
        body(2 * j + 1, 1, j)
        if chain:
            chain.leave(PAIRS, 2 * per)
    body(NCH - 1, 0, PAIRS)


def cols(i, n=CH):
    return bass.ds(i * n, n)


def rows(ap):
    return ap[0:E, :].rearrange("(p c) f -> p c f", p=P)


def bc(ap, shape, axis):
    return ap.unsqueeze(axis).to_broadcast(shape)


class Ctx:

    def __init__(self, nc, stack):
        self.nc, self.stack, self.count = nc, stack, 0

    def sb(self, name, shape, dt=F32):
        return self.stack.enter_context(self.nc.sbuf_tensor(name, shape, dt))[tuple(slice(None) for _ in shape)]

    def ps(self, name, shape, dt=F32):
        return self.stack.enter_context(self.nc.psum_tensor(name, shape, dt))[tuple(slice(None) for _ in shape)]

    def sem(self, name):
        sem = self.stack.enter_context(self.nc.semaphore(name))
        self.stack.callback(self.nc.sync.sem_clear, sem)
        return sem

    def pool_dma_sem(self, name):
        sem = self.stack.enter_context(self.nc.semaphore(name))
        self.stack.callback(self.nc.gpsimd.sem_clear, sem)
        self.stack.callback(self.nc.gpsimd.dma_reset, range(sem.num, sem.num + 1))
        return sem

    def dram(self, name, shape, dt=F32):
        return self.nc.dram_tensor(name, shape, dt).ap()


def scope(k):
    return Ctx(k.nc, k.stack.enter_context(ExitStack()))



def node_linear(k, name, src, w, out, K, M):
    with ExitStack() as st:
        c = Ctx(k.nc, st)
        stage = c.sb(name + "_stage", [P, GRP, K])
        tT = c.sb(name + "_tT", [K, GRP * P])
        pT = c.ps(name + "_pT", [K, 1024])
        pO = c.ps(name + "_pO", [P, 512])
        staged, transposed, copied, product, evacuated = (
            c.sem(name + s) for s in ("_staged", "_transposed", "_copied", "_product", "_evacuated"))
        with k.nc.Block() as block:
            @block.vector
            def _(v):
                with v.Fori(0, NT // GRP) as i:
                    v.tensor_copy(stage[:, :, :], src[:, cols(i, GRP), :]).then_inc(staged, 1)
                    v.wait_ge(product, i + 1)
                    v.tensor_copy(out[:, cols(i, GRP), :],
                                  pO[:, 0:GRP * M].rearrange("p (g m) -> p g m", g=GRP)).then_inc(evacuated, 1)
                    v.wait_ge(evacuated, i + 1)

            @block.scalar
            def _(a):
                with a.Fori(0, NT // GRP) as i:
                    a.wait_ge(transposed, i + 1)
                    a.activation(tT[:, :], pT[:, 0:GRP * P], ACT.Copy).then_inc(copied, 1)

            @block.tensor
            def _(pe):
                with pe.Fori(0, NT // GRP) as i:
                    pe.wait_ge(staged, i + 1)
                    pe.nop(nofuse=True)
                    for g in range(GRP):
                        mm = pe.transpose(pT[:, g * P:(g + 1) * P], stage[:, g, :], k.ident[:, :])
                    mm.then_inc(transposed, 1)
                    pe.wait_ge(copied, i + 1)
                    for g in range(GRP):
                        mm = pe.matmul(pO[:, g * M:(g + 1) * M], tT[:, g * P:(g + 1) * P], w,
                                       start=True, stop=True)
                    mm.then_inc(product, 1)


def layer_norm(k, name, x, out):
    with ExitStack() as st:
        c = Ctx(k.nc, st)
        sq = c.sb(name + "_sq", [P, NT, D])
        mean = c.sb(name + "_mean", [P, NT])
        var = c.sb(name + "_var", [P, NT])
        sd = c.sb(name + "_sd", [P, NT])
        step, var_ready, sd_ready = c.sem(name + "_step"), c.sem(name + "_var_ready"), c.sem(name + "_sd_ready")
        with k.nc.Block() as block:
            @block.vector
            def _(v):
                ch = Chain(v, step)
                ch(v.tensor_reduce(mean[:, :], x[:, :, :], axis=AX.X, op=ALU.add))
                ch(v.tensor_scalar(mean[:, :], mean[:, :], 1.0 / D, None, ALU.mult))
                ch(v.tensor_tensor(x[:, :, :], x[:, :, :], bc(mean[:, :], [P, NT, D], 2), ALU.subtract))
                ch(v.tensor_tensor(sq[:, :, :], x[:, :, :], x[:, :, :], ALU.mult))
                ch(v.tensor_reduce(var[:, :], sq[:, :, :], axis=AX.X, op=ALU.add))
                v.tensor_scalar(var[:, :], var[:, :], 1.0 / D, 1e-5, ALU.mult, ALU.add).then_inc(var_ready, 1)
                v.wait_ge(sd_ready, 1)
                ch(v.reciprocal(var[:, :], sd[:, :]))
                ch(v.tensor_tensor(out[:, :, :], x[:, :, :], bc(var[:, :], [P, NT, D], 2), ALU.mult))

            @block.scalar
            def _(a):
                a.wait_ge(var_ready, 1)
                a.activation(sd[:, :], var[:, :], ACT.Sqrt).then_inc(sd_ready, 1)


def selu(k, name, x, tmp, bias):
    with ExitStack() as st:
        c = Ctx(k.nc, st)
        step, neg, exps = c.sem(name + "_step"), c.sem(name + "_neg"), c.sem(name + "_exps")
        shape = [P, NT, x.shape[2]]
        with k.nc.Block() as block:
            @block.vector
            def _(v):
                ch = Chain(v, step)
                ch(v.tensor_tensor(x[:, :, :], x[:, :, :], bc(bias, shape, 1), ALU.add))
                v.tensor_scalar(tmp[:, :, :], x[:, :, :], 0.0, None, ALU.min).then_inc(neg, 1)
                ch(v.tensor_scalar(x[:, :, :], x[:, :, :], 0.0, SELU_SCALE, ALU.max, ALU.mult))
                v.wait_ge(exps, 1)
                ch(v.tensor_scalar(tmp[:, :, :], tmp[:, :, :], 1.0, SELU_ALPHA * SELU_SCALE,
                                   ALU.subtract, ALU.mult))
                ch(v.tensor_tensor(x[:, :, :], x[:, :, :], tmp[:, :, :], ALU.add))

            @block.scalar
            def _(a):
                a.wait_ge(neg, 1)
                a.activation(tmp[:, :, :], tmp[:, :, :], ACT.Exp).then_inc(exps, 1)


def store_nodes(k, name, parts, table):
    with ExitStack() as st:
        c = Ctx(k.nc, st)
        stored = c.sem(name + "_stored")
        with k.nc.Block() as block:
            @block.sync
            def _(s):
                at = 0
                view = table[0:NP, :].rearrange("(t p) f -> p t f", p=P)
                for part in parts:
                    w = part.shape[2]
                    s.dma_start(view[:, :, at:at + w], part).then_inc(stored, 16)
                    at += w
                s.wait_ge(stored, 16 * len(parts))


def vector_block(k, name, body):
    with ExitStack() as st:
        step = Ctx(k.nc, st).sem(name + "_step")
        with k.nc.Block() as block:
            @block.vector
            def _(v):
                body(v, Chain(v, step))



def lane_carries(k, name, last, F, order, op, table):
    with ExitStack() as st:
        c = Ctx(k.nc, st)
        T = c.sb(name + "_T", [F, P])
        whole = c.sb(name + "_whole", [F, P])
        zero = c.sb(name + "_zero", [1, F])
        out_sem, in_sem, step, done = (c.sem(name + s) for s in ("_out", "_in", "_step", "_done"))
        buf = k.lanes[0:P, 0:F]
        with k.nc.Block() as block:
            @block.vector
            def _(v):
                ch = Chain(v, step)
                ch(v.memset(zero[:, :], 0.0))
                v.wait_ge(in_sem, 32)
                if op == ALU.add:
                    ch(v.tensor_tensor_scan(T[:, :], whole[:, :], T[:, :], 0.0, ALU.mult, ALU.add))
                else:
                    ch(v.tensor_scalar(whole[:, :], whole[:, :], 1.0, BIG, ALU.subtract, ALU.mult))
                    ch(v.tensor_tensor_scan(T[:, :], whole[:, :], T[:, :], -BIG, ALU.add, ALU.max))

            @block.sync
            def _(s):
                with k.nc.allow_non_contiguous_dma("transpose of a small tile"):
                    s.dma_start(buf, last).then_inc(out_sem, 16)
                    s.wait_ge(out_sem, 16)
                    s.dma_start(T[:, :], buf.rearrange("p f -> f p")).then_inc(in_sem, 16)
                    s.dma_start(whole[:, :], order["whole_row"].to_broadcast([F, P])).then_inc(in_sem, 16)
                    s.wait_ge(step, 2 if op == ALU.add else 3)
                    s.dma_start(table[1:P + 1, :].rearrange("p f -> f p"), T[:, :]).then_inc(done, 16)
                    s.dma_start(table[0:1, :], zero[:, :]).then_inc(done, 16)
                s.wait_ge(done, 32)


def extract(k, name, scans, carries, order, out, F, op):
    with ExitStack() as st:
        c = Ctx(k.nc, st)
        si = c.sb(name + "_si", [P, XT], I32)
        sl = c.sb(name + "_sl", [P, XT], I32)
        gs = c.sb(name + "_gs", [P, XT, F])
        gc = c.sb(name + "_gc", [P, XT, F])
        staged, step, joined = (c.sem(name + s) for s in ("_staged", "_step", "_joined"))
        got = c.pool_dma_sem(name + "_got")
        shape = [P, XT, F]
        with k.nc.Block() as block:
            @block.gpsimd
            def _(g):
                with g.Fori(0, NT // XT) as i:
                    g.wait_ge(joined, i + 1)
                    g.tensor_copy(si[:, :], order["end"][:, cols(i, XT)]).then_inc(staged, 1)
                    g.tensor_copy(sl[:, :], order["end_lane"][:, cols(i, XT)]).then_inc(staged, 1)
                    g.wait_ge(staged, 2 * i + 2)
                    g.nop(nofuse=True)
                    for t in range(XT):
                        g.indirect_dma_start(out=gs[:, t, :], out_offset=None, in_=scans,
                                             in_offset=bass.IndirectOffsetOnAxis(ap=si[:, t:t + 1], axis=0)
                                             ).then_inc(got, 16)
                        g.indirect_dma_start(out=gc[:, t, :], out_offset=None, in_=carries,
                                             in_offset=bass.IndirectOffsetOnAxis(ap=sl[:, t:t + 1], axis=0)
                                             ).then_inc(got, 16)

            @block.vector
            def _(v):
                ch = Chain(v, step)
                v.sem_inc(joined, 1)
                with v.Fori(0, NT // XT) as i:
                    ch.enter(i, 2)
                    v.wait_ge(got, (i + 1) * (32 * XT))
                    if op == ALU.add:
                        ch(v.tensor_tensor(gs[:, :, :], gs[:, :, :],
                                           bc(order["some"][:, cols(i, XT)], shape, 2), ALU.mult))
                        ch(v.tensor_tensor(gc[:, :, :], gc[:, :, :],
                                           bc(order["cross"][:, cols(i, XT)], shape, 2), ALU.mult))
                    else:
                        ch(v.tensor_tensor(gs[:, :, :], gs[:, :, :],
                                           bc(order["none_neg"][:, cols(i, XT)], shape, 2), ALU.add))
                        ch(v.tensor_tensor(gc[:, :, :], gc[:, :, :],
                                           bc(order["cross_neg"][:, cols(i, XT)], shape, 2), ALU.add))
                    ch.leave(NT // XT, 2)
                    v.tensor_tensor(out[:, cols(i, XT), :], gs[:, :, :], gc[:, :, :], op).then_inc(joined, 1)


def spread(k, name, values, F, table, first):
    view = table_view(k, F, E + NP)
    with ExitStack() as st:
        c = Ctx(k.nc, st)
        si = c.sb(name + "_si", [P, XT], I32)
        sv = c.sb(name + "_sv", [P, XT, F])
        staged = c.sem(name + "_staged")
        sent, got = c.pool_dma_sem(name + "_sent"), c.pool_dma_sem(name + "_got")
        with k.nc.Block() as block:
            @block.gpsimd
            def _(g):
                with g.Fori(0, NT // XT) as i:
                    g.tensor_copy(si[:, :], k.by_dst["begin"][:, cols(i, XT)]).then_inc(staged, 1)
                    g.tensor_copy(sv[:, :, :], values[:, cols(i, XT), :]).then_inc(staged, 1)
                    g.wait_ge(staged, 2 * i + 2)
                    g.nop(nofuse=True)
                    for t in range(XT):
                        g.indirect_dma_start(out=view, in_=sv[:, t, :], in_offset=None,
                                             out_offset=bass.IndirectOffsetOnAxis(ap=si[:, t:t + 1], axis=0)
                                             ).then_inc(sent, 16)
                    g.wait_ge(sent, (i + 1) * (16 * XT))
                    g.nop(nofuse=True)
                g.indirect_dma_start(out=first, out_offset=None, in_=table,
                                     in_offset=bass.IndirectOffsetOnAxis(ap=k.first_dst[:, 0:1], axis=0)
                                     ).then_inc(got, 16)
                g.wait_ge(got, 16)


def table_view(k, F, n):
    return k.spread_buf[0:n * F].rearrange("(r f) -> r f", f=F)


def gather_column_loop(g, k, i, j, b, table, G, stage, staged, freed, credit, got, index):
    g.wait_ge(freed[b], (j + 1) * credit)
    g.tensor_copy(stage[b][:, :], index[:, cols(i)]).then_inc(staged[b], 1)
    g.wait_ge(staged[b], j + 1)
    g.nop(nofuse=True)
    for t in range(CH):
        g.indirect_dma_start(out=G[b][:, t, :], out_offset=None, in_=table,
                             in_offset=bass.IndirectOffsetOnAxis(ap=stage[b][:, t:t + 1], axis=0)
                             ).then_inc(got[b], 16)



def setup(k, x, src, dst):
    c = k
    with ExitStack() as st:
        t = Ctx(k.nc, st)
        iota_i = t.sb("iota_i", [P, P], I32)
        part_i = t.sb("part_i", [P, 1], I32)
        part_one = t.sb("part_one", [P, P])
        lane_first = t.sb("lane_first", [P, 1], I32)
        zeros = t.sb("zeros", [P, 4250])
        zsrc = zeros[:, :]
        loaded, made, step, zeroed, whole_out = (t.sem(s) for s in
                                                 ("su_loaded", "su_made", "su_step", "su_zeroed", "su_whole"))
        xclear, zero_made = t.sem("su_xclear"), t.sem("su_zero_made")
        with k.nc.Block() as block:
            @block.sync
            def _(s):
                s.dma_start(c.dst_i[:, :], dst.rearrange("(p c) -> p c", p=P)).then_inc(loaded, 16)
                s.dma_start(c.src_i[:, :], src.rearrange("(p c) -> p c", p=P)).then_inc(loaded, 16)
                s.wait_ge(xclear, 2)
                with k.nc.allow_non_contiguous_dma("one value of each lane"):
                    s.dma_start(lane_first[1:P, :],
                                dst.rearrange("(p c) -> p c", p=P)[0:P - 1, LANE - 1:LANE]).then_inc(loaded, 16)
                    s.dma_start(c.first_dst[:, :],
                                dst.rearrange("(p c) -> p c", p=P)[:, 0:1]).then_inc(loaded, 16)
                s.dma_start(c.x[:, 0:FULL, :],
                            x[0:FULL * P, :].rearrange("(t p) f -> p t f", p=P)).then_inc(loaded, 16)
                s.dma_start(c.x[0:REST, FULL, :], x[FULL * P:N, :]).then_inc(loaded, 16)
                s.wait_ge(made, 1)
                s.wait_ge(zero_made, 1)
                s.dma_start(c.by_dst["whole_row"].rearrange("a p -> p a"), c.whole[:, :]).then_inc(whole_out, 16)
                flat = c.spread_buf[:].rearrange("(r p f) -> r p f", p=P, f=SPREAD_PIECE)
                for r in range(SPREAD_PIECES):
                    s.dma_start(flat[r], zsrc[:, 0:SPREAD_PIECE]).then_inc(zeroed, 16)
                s.wait_ge(zeroed, 16 * SPREAD_PIECES)
                s.wait_ge(whole_out, 16)

            @block.gpsimd
            def _(g):
                g.iota(iota_i[:, :], pattern=[[1, P]], base=0, channel_multiplier=0).then_inc(step, 1)
                g.iota(part_i[:, :], pattern=[[0, 1]], base=0, channel_multiplier=1).then_inc(step, 1)
                g.memset(zsrc, 0.0).then_inc(zero_made, 1)

            @block.vector
            def _(v):
                v.memset(lane_first[:, :], -1).then_inc(xclear, 1)
                v.memset(c.x[:, FULL:NT, :], 0.0).then_inc(xclear, 1)
                v.wait_ge(step, 2)
                ch = Chain(v, step)
                ch.n = 2
                ch(v.tensor_copy(c.iota[:, :], iota_i[:, :]))
                ch(v.tensor_copy(c.part[:, :], part_i[:, :]))
                ch(v.tensor_scalar(c.ident[:, :], c.iota[:, :], c.part[:, 0:1], None, ALU.is_equal))
                ch(v.tensor_scalar(c.before[:, :], c.iota[:, :], c.part[:, 0:1], None, ALU.is_gt))
                ch(v.memset(c.ones[:, :], 1.0))
                ch(v.tensor_copy(c.ident_b[:, :], c.ident[:, :]))
                ch(v.tensor_scalar(c.ident128_b[:, :], c.ident[:, :], float(P), None, ALU.mult))
                ch(v.memset(c.earlier[:, 0:(GRP - 1) * P], 1.0))
                ch(v.tensor_scalar(c.earlier[:, (GRP - 1) * P:], c.iota[:, :], c.part[:, 0:1], None, ALU.is_lt))
                ch(v.memset(c.node_mask[:, :], 1.0))
                ch(v.memset(c.node_mask[:, FULL + 1:NT], 0.0))
                ch(v.tensor_scalar(c.node_mask[:, FULL:FULL + 1], c.part[:, 0:1], float(REST), None, ALU.is_lt))
                v.wait_ge(loaded, 96)
                ch(v.tensor_tensor(c.keep_d[:, 0:1], c.dst_i[:, 0:1], lane_first[:, :], ALU.is_equal))
                ch(v.tensor_tensor(c.keep_d[:, 1:LANE], c.dst_i[:, 1:LANE], c.dst_i[:, 0:LANE - 1], ALU.is_equal))
                v.tensor_reduce(c.whole[:, :], c.keep_d[:, :], axis=AX.X, op=ALU.min).then_inc(made, 1)
                v.wait_ge(made, 1)


SPREAD_F = 17
SPREAD_PIECE = 4250
SPREAD_PIECES = (E + NP) * SPREAD_F // (P * SPREAD_PIECE) + 1
SPREAD_SIZE = SPREAD_PIECES * P * SPREAD_PIECE


def digits(k, name, src_i, lo, hi):
    with ExitStack() as st:
        t = Ctx(k.nc, st).sb(name + "_t", [P, LANE], I32)

        def body(v, ch):
            ch(v.tensor_scalar(t[:, :], src_i[:, :], P - 1, None, ALU.bitwise_and))
            ch(v.tensor_copy(lo[:, :], t[:, :]))
            ch(v.tensor_scalar(t[:, :], src_i[:, :], 7, None, ALU.logical_shift_right))
            ch(v.tensor_copy(hi[:, :], t[:, :]))
        vector_block(k, name, body)


def order_tables(k, name, counts, order):
    with ExitStack() as st:
        c = Ctx(k.nc, st)
        pt = c.ps(name + "_pt", [P, 512])
        tot = c.sb(name + "_tot", [P, NT])
        run = c.sb(name + "_run", [P, NT])
        start = order["start"]
        endf = c.sb(name + "_endf", [P, NT])
        le = c.sb(name + "_le", [P, NT])
        ls = c.sb(name + "_ls", [P, NT])
        lane0 = c.sb(name + "_lane0", [P, P])
        ge = c.sb(name + "_ge", [P, NT, P])
        idx = c.sb(name + "_idx", [P, NT], I32)
        idf = c.sb(name + "_idf", [P, NT])
        summed, iotad, step = (c.sem(name + s) for s in ("_summed", "_iotad", "_step"))
        with k.nc.Block() as block:
            @block.tensor
            def _(pe):
                pe.matmul(pt[:, 0:NT], k.before[:, :], counts[:, :], start=True, stop=True)
                pe.matmul(pt[:, NT:2 * NT], k.ones[:, :], counts[:, :], start=True, stop=True).then_inc(summed, 1)

            @block.gpsimd
            def _(g):
                g.iota(idx[:, :], pattern=[[P, NT]], base=E, channel_multiplier=1).then_inc(iotad, 1)

            @block.vector
            def _(v):
                ch = Chain(v, step)
                ch(v.memset(ge[:, 0, 0:NT], 1.0))
                v.wait_ge(summed, 1)
                ch(v.tensor_copy(tot[:, :], pt[:, NT:2 * NT]))
                ch(v.tensor_tensor_scan(run[:, :], ge[:, 0, 0:NT], tot[:, :], 0.0, ALU.mult, ALU.add))
                ch(v.tensor_tensor(run[:, :], run[:, :], tot[:, :], ALU.subtract))
                ch(v.tensor_tensor(start[:, :], run[:, :], pt[:, 0:NT], ALU.add))
                ch(v.tensor_scalar(order["some"][:, :], counts[:, :], 0.5, None, ALU.is_gt))
                ch(v.tensor_scalar(order["none_neg"][:, :], order["some"][:, :], 1.0, BIG, ALU.subtract, ALU.mult))
                ch(v.tensor_tensor(endf[:, :], start[:, :], counts[:, :], ALU.add))
                ch(v.tensor_scalar(endf[:, :], endf[:, :], 1.0, 0.0, ALU.subtract, ALU.max))
                ch(v.tensor_copy(order["end"][:, :], endf[:, :]))
                ch(v.tensor_scalar(lane0[:, :], k.iota[:, :], float(LANE), float(LANE), ALU.mult, ALU.add))
                for pos, lane in ((endf, le), (start, ls)):
                    ch(v.tensor_tensor(ge[:, :, :], bc(pos[:, :], [P, NT, P], 2), bc(lane0[:, :], [P, NT, P], 1),
                                       ALU.is_ge))
                    ch(v.tensor_reduce(lane[:, :], ge[:, :, :], axis=AX.X, op=ALU.add))
                ch(v.tensor_copy(order["end_lane"][:, :], le[:, :]))
                ch(v.tensor_tensor(order["cross"][:, :], le[:, :], ls[:, :], ALU.is_gt))
                ch(v.tensor_tensor(order["cross"][:, :], order["cross"][:, :], order["some"][:, :], ALU.mult))
                ch(v.tensor_scalar(order["cross_neg"][:, :], order["cross"][:, :], 1.0, BIG,
                                   ALU.subtract, ALU.mult))
                v.wait_ge(iotad, 1)
                ch(v.tensor_copy(idf[:, :], idx[:, :]))
                ch(v.tensor_tensor(endf[:, :], start[:, :], idf[:, :], ALU.subtract))
                ch(v.tensor_tensor(endf[:, :], endf[:, :], order["some"][:, :], ALU.mult))
                ch(v.tensor_tensor(endf[:, :], endf[:, :], idf[:, :], ALU.add))
                ch(v.tensor_copy(order["begin"][:, :], endf[:, :]))


def new_order(k, name):
    o = {}
    for f in ("start", "some", "none_neg", "cross", "cross_neg", "count"):
        o[f] = k.sb(f"{name}_{f}", [P, NT])
    for f in ("end", "end_lane", "begin"):
        o[f] = k.sb(f"{name}_{f}", [P, NT], I32)
    o["whole_row"] = k.dram(f"{name}_whole_row", [1, P])
    return o



def scan_chunk(v, ch, data, keep, carry, F, op=ALU.mult, op1=ALU.add, at=0):
    for f in range(F):
        ch(v.tensor_tensor_scan(data[:, :, at + f], keep, data[:, :, at + f], carry[:, f:f + 1], op, op1))
    ch(v.tensor_copy(carry[:, 0:F], data[:, CH - 1, at:at + F]))


def histogram_vector(v, lo, hi, oh_lo, oh_hi, k, i, ready, used):
    v.nop(nofuse=True)
    with v.Fori(0, NG) as q:
        v.wait_ge(used, i * NG + q + 1)
        v.tensor_tensor(oh_lo[:, :, :], bc(lo[:, bass.ds(i * CH + q * GRP, GRP)], [P, GRP, P], 2),
                        bc(k.iota[:, :], [P, GRP, P], 1), ALU.is_equal).then_inc(ready, 1)
        v.tensor_tensor(oh_hi[:, :, :], bc(hi[:, bass.ds(i * CH + q * GRP, GRP)], [P, GRP, NT], 2),
                        bc(k.iota[:, 0:NT], [P, GRP, NT], 1), ALU.is_equal).then_inc(ready, 1)


def histogram_tensor(pe, oh_lo, oh_hi, acc, i, ready, used):
    with pe.Fori(0, NG) as q:
        pe.wait_ge(ready, (i * NG + q) * 2 + 2)
        for g in range(GRP):
            mm = pe.matmul(acc[:, 0:NT], oh_lo[:, g, :], oh_hi[:, g, :], start=False, stop=True,
                           skip_group_check=True)
        mm.then_inc(used, 1)


def gat_gather(k, name, table, F, heads, lo, hi, counts, edges, maxes, carry):
    FX = F - heads
    with ExitStack() as st:
        c = Ctx(k.nc, st)
        G = [c.sb(f"{name}_G{b}", [P, CH, F]) for b in range(2)]
        S = [c.sb(f"{name}_S{b}", [P, CH, heads]) for b in range(2)]
        stage = [c.sb(f"{name}_stage{b}", [P, CH], I32) for b in range(2)]
        neg = c.sb(name + "_neg", [P, CH])
        oh_lo = c.sb(name + "_oh_lo", [P, GRP, P], BF16)
        oh_hi = c.sb(name + "_oh_hi", [P, GRP, NT], BF16)
        acc = c.ps(name + "_acc", [P, 512])
        staged = [c.sem(f"{name}_staged{b}") for b in range(2)]
        got = [c.pool_dma_sem(f"{name}_got{b}") for b in range(2)]
        stored = [c.sem(f"{name}_stored{b}") for b in range(2)]
        scanned, step, ready, used, counted = (
            c.sem(name + s) for s in ("_scanned", "_step", "_ready", "_used", "_counted"))
        with k.nc.Block() as block:
            @block.gpsimd
            def _(g):
                over_chunks(g, lambda i, b, j: gather_column_loop(
                    g, k, i, j, b, table, G, stage, staged, stored, 32, got, k.src_i))

            @block.vector
            def _(v):
                ch = Chain(v, step)
                ch(v.memset(carry[:, 0:heads], -BIG))
                ch(v.memset(oh_lo[:, :, :], 0.0))

                def chunk(i, b, j):
                    v.wait_ge(stored[b], (j + 1) * 32)
                    ch(v.tensor_scalar(neg[:, :], k.keep_d[:, cols(i)], 1.0, BIG, ALU.subtract, ALU.mult))
                    v.wait_ge(got[b], (j + 1) * (16 * CH))
                    for h in range(heads):
                        ch(v.tensor_tensor_scan(S[b][:, :, h], neg[:, :], G[b][:, :, FX + h],
                                                carry[:, h:h + 1], ALU.add, ALU.max))
                    v.tensor_copy(carry[:, 0:heads], S[b][:, CH - 1, :]).then_inc(scanned, 1)
                    v.wait_ge(scanned, i + 1)
                    histogram_vector(v, lo, hi, oh_lo, oh_hi, k, i, ready, used)
                over_chunks(v, chunk, ch, 1 + heads)
                v.wait_ge(used, NCH * NG + 1)
                v.tensor_copy(counts[:, :], acc[:, 0:NT]).then_inc(counted, 1)

            @block.tensor
            def _(pe):
                pe.wait_ge(step, 2)
                pe.matmul(acc[:, 0:NT], oh_lo[:, 0, :], oh_lo[:, 1, 0:NT], start=True, stop=True,
                          skip_group_check=True).then_inc(used, 1)
                over_chunks(pe, lambda i, b, j: histogram_tensor(pe, oh_lo, oh_hi, acc, i, ready, used))

            @block.sync
            def _(s):
                for b in range(2):
                    s.sem_inc(stored[b], 32)

                def chunk(i, b, j):
                    s.wait_ge(scanned, i + 1)
                    s.dma_start(edges.rearrange("p (c f) -> p c f", f=F)[:, cols(i), :],
                                G[b][:, :, :]).then_inc(stored[b], 16)
                    s.dma_start(rows(maxes)[:, cols(i), :], S[b][:, :, :]).then_inc(stored[b], 16)
                over_chunks(s, chunk)
                s.wait_ge(stored[0], 32 * (PAIRS + 2))
                s.wait_ge(stored[1], 32 * (PAIRS + 1))


def gat_weigh(k, name, F, heads, edges, scans, first, carry):
    FX = F - heads
    FO = heads * FX + heads
    with ExitStack() as st:
        c = Ctx(k.nc, st)
        G = [c.sb(f"{name}_G{b}", [P, CH, F]) for b in range(2)]
        X = [c.sb(f"{name}_X{b}", [P, CH, 2 * heads]) for b in range(2)]
        W = [c.sb(f"{name}_W{b}", [P, CH, FO]) for b in range(2)]
        begin = c.sb(name + "_begin", [P, CH])
        e1 = c.sb(name + "_e1", [P, CH, heads])
        loaded = [c.sem(f"{name}_loaded{b}") for b in range(2)]
        stored = [c.sem(f"{name}_stored{b}") for b in range(2)]
        scanned, step, logits, probs = (c.sem(name + s) for s in ("_scanned", "_step", "_logits", "_probs"))
        with k.nc.Block() as block:
            @block.sync
            def _(s):
                for b in range(2):
                    s.sem_inc(stored[b], 16)

                def load(i, b):
                    s.dma_start(G[b][:, :, :],
                                edges.rearrange("p (c f) -> p c f", f=F)[:, cols(i), :]).then_inc(loaded[b], 16)
                    s.dma_start(X[b][:, :, :],
                                rows(table_view(k, 2 * heads, E))[:, cols(i), :]).then_inc(loaded[b], 16)

                def chunk(i, b, j, more):
                    s.wait_ge(scanned, i + 1)
                    s.dma_start(rows(scans)[:, cols(i), :], W[b][:, :, :]).then_inc(stored[b], 16)
                    if more:
                        load(i + 2, b)
                load(0, 0)
                load(1, 1)
                with s.Fori(0, PAIRS - 1) as j:
                    chunk(2 * j, 0, j, True)
                    chunk(2 * j + 1, 1, j, True)
                chunk(NCH - 3, 0, PAIRS - 1, True)
                chunk(NCH - 2, 1, PAIRS - 1, False)
                chunk(NCH - 1, 0, PAIRS, False)
                s.wait_ge(stored[0], 16 * (PAIRS + 2))
                s.wait_ge(stored[1], 16 * (PAIRS + 1))

            @block.vector
            def _(v):
                ch = Chain(v, step)
                ch(v.memset(carry[:, 0:FO], 0.0))

                def chunk(i, b, j):
                    keep = k.keep_d[:, cols(i)]
                    v.wait_ge(loaded[b], (j + 1) * 32)
                    ch(v.tensor_scalar(begin[:, :], keep, -1.0, 1.0, ALU.mult, ALU.add))
                    ch(v.tensor_tensor(X[b][:, :, :], X[b][:, :, :], bc(begin[:, :], [P, CH, 2 * heads], 2),
                                       ALU.mult))
                    scan_chunk(v, ch, X[b], keep, first, 2 * heads)
                    ch(v.tensor_tensor(e1[:, :, :], G[b][:, :, FX:F], X[b][:, :, 0:heads], ALU.add))
                    ch(v.scalar_tensor_tensor(out=e1[:, :, :], in0=e1[:, :, :], scalar=0.2, in1=e1[:, :, :],
                                              op0=ALU.mult, op1=ALU.max))
                    v.wait_ge(stored[b], (j + 1) * 16)
                    v.tensor_tensor(W[b][:, :, heads * FX:FO], e1[:, :, :], X[b][:, :, heads:2 * heads],
                                    ALU.subtract).then_inc(logits, 1)
                    v.wait_ge(probs, i + 1)
                    for h in range(heads):
                        ch(v.tensor_tensor(W[b][:, :, h * FX:(h + 1) * FX], G[b][:, :, 0:FX],
                                           bc(W[b][:, :, heads * FX + h], [P, CH, FX], 2), ALU.mult))
                    for f in range(FO):
                        ch(v.tensor_tensor_scan(W[b][:, :, f], keep, W[b][:, :, f], carry[:, f:f + 1],
                                                ALU.mult, ALU.add))
                    v.tensor_copy(carry[:, 0:FO], W[b][:, CH - 1, :]).then_inc(scanned, 1)
                    v.wait_ge(scanned, i + 1)
                over_chunks(v, chunk, ch, 5 + 3 * heads + FO)

            @block.scalar
            def _(a):
                def chunk(i, b, j):
                    a.wait_ge(logits, i + 1)
                    a.activation(W[b][:, :, heads * FX:FO], W[b][:, :, heads * FX:FO], ACT.Exp).then_inc(probs, 1)
                over_chunks(a, chunk)


def gcn_gather(k, name, table, scans, carry, side):
    with ExitStack() as st:
        c = Ctx(k.nc, st)
        G = [c.sb(f"{name}_G{b}", [P, CH, D]) for b in range(2)]
        stage = [c.sb(f"{name}_stage{b}", [P, CH], I32) for b in range(2)]
        staged = [c.sem(f"{name}_staged{b}") for b in range(2)]
        got = [c.pool_dma_sem(f"{name}_got{b}") for b in range(2)]
        stored = [c.sem(f"{name}_stored{b}") for b in range(2)]
        scanned, step = c.sem(name + "_scanned"), c.sem(name + "_step")
        side_vector, side_tensor, side_scalar, side_steps = side(k, c, name)
        with k.nc.Block() as block:
            @block.gpsimd
            def _(g):
                over_chunks(g, lambda i, b, j: gather_column_loop(
                    g, k, i, j, b, table, G, stage, staged, stored, 16, got, k.src_i))

            @block.vector
            def _(v):
                ch = Chain(v, step)
                ch(v.memset(carry[:, 0:D], 0.0))

                def chunk(i, b, j):
                    v.wait_ge(got[b], (j + 1) * (16 * CH))
                    for f in range(D):
                        ch(v.tensor_tensor_scan(G[b][:, :, f], k.keep_d[:, cols(i)], G[b][:, :, f],
                                                carry[:, f:f + 1], ALU.mult, ALU.add))
                    v.tensor_copy(carry[:, 0:D], G[b][:, CH - 1, :]).then_inc(scanned, 1)
                    v.wait_ge(scanned, i + 1)
                    v.nop(nofuse=True)
                    with v.Fori(0, NG) as q:
                        ch.enter(q, side_steps)
                        side_vector(v, ch, i, q)
                        ch.leave(NG, side_steps)
                over_chunks(v, chunk, ch, D + NG * side_steps)

            @block.tensor
            def _(pe):
                side_tensor(pe, None, None)

                def chunk(i, b, j):
                    with pe.Fori(0, NG) as q:
                        side_tensor(pe, i, q)
                over_chunks(pe, chunk)

            @block.scalar
            def _(a):
                side_scalar(a)

            @block.sync
            def _(s):
                for b in range(2):
                    s.sem_inc(stored[b], 16)

                def chunk(i, b, j):
                    s.wait_ge(scanned, i + 1)
                    s.dma_start(rows(scans)[:, cols(i), :], G[b][:, :, :]).then_inc(stored[b], 16)
                over_chunks(s, chunk)
                s.wait_ge(stored[0], 16 * (PAIRS + 2))
                s.wait_ge(stored[1], 16 * (PAIRS + 1))


def count_in_group(k, c, name):
    pB = c.ps(name + "_pB", [P, 1024])
    junk = c.sb(name + "_junk", [P, GRP * P])
    src_f = c.sb(name + "_src_f", [P, GRP])
    rowed, used = c.sem(name + "_rowed"), c.sem(name + "_used")

    def vector(v, ch, i, q):
        at = bass.ds(i * CH + q * GRP, GRP)
        ch(v.tensor_copy(src_f[:, :], k.src_i[:, at]))
        v.wait_ge(rowed, i * NG + q + 1)
        for g in range(GRP):
            ins = v.scalar_tensor_tensor(out=junk[:, 0:(g + 1) * P], in0=pB[:, 0:(g + 1) * P],
                                         scalar=src_f[:, g:g + 1], in1=k.earlier[:, (GRP - 1 - g) * P:],
                                         op0=ALU.is_equal, op1=ALU.mult, accum_out=k.cnt5[:, g:g + 1])
            ch(ins)
        v.tensor_copy(k.cnt[:, at], k.cnt5[:, :]).then_inc(used, 1)
        v.wait_ge(used, i * NG + q + 2)

    def tensor(pe, i, q):
        if i is None:
            pe.sem_inc(used, 1)
            return
        pe.wait_ge(used, i * NG + q + 1)
        for g in range(GRP):
            at = bass.ds(i * CH + q * GRP + g, 1)
            pe.matmul(pB[:, g * P:(g + 1) * P], k.src_lo[:, at].to_broadcast([P, P]), k.ident_b[:, :],
                      start=True, stop=False)
            mm = pe.matmul(pB[:, g * P:(g + 1) * P], k.src_hi[:, at].to_broadcast([P, P]), k.ident128_b[:, :],
                           start=False, stop=True)
        mm.then_inc(rowed, 1)

    return vector, tensor, lambda a: None, 1 + GRP


def count_before_group(k, c, name):
    pB = c.ps(name + "_pB", [P, 1024])
    pT = c.ps(name + "_pT", [P, 512])
    pR = c.ps(name + "_pR", [P, 512])
    table = c.sb(name + "_table", [P, NT])
    oh_lo = c.sb(name + "_oh_lo", [P, GRP, P], BF16)
    oh_hi = c.sb(name + "_oh_hi", [P, GRP, NT], BF16)
    loT = c.sb(name + "_loT", [P, GRP, P])
    prod = c.sb(name + "_prod", [P, GRP, NT])
    r5 = c.sb(name + "_r5", [P, GRP])
    rowed, hot, hotT, looked, added, copied, ranked = (
        c.sem(name + s) for s in ("_rowed", "_hot", "_hotT", "_looked", "_added", "_copied", "_ranked"))

    def vector(v, ch, i, q):
        n = i * NG + q
        at = bass.ds(i * CH + q * GRP, GRP)
        v.wait_ge(added, n + 1)
        v.tensor_tensor(oh_lo[:, :, :], bc(k.src_lo[:, at], [P, GRP, P], 2), bc(k.iota[:, :], [P, GRP, P], 1),
                        ALU.is_equal).then_inc(hot, 1)
        ch(v.tensor_tensor(oh_hi[:, :, :], bc(k.src_hi[:, at], [P, GRP, NT], 2),
                           bc(k.iota[:, 0:NT], [P, GRP, NT], 1), ALU.is_equal))
        v.wait_ge(rowed, n + 1)
        v.tensor_scalar(loT[:, :, :], pB[:, 0:GRP * P].rearrange("p (g q) -> p g q", g=GRP), k.part[:, 0:1], None,
                        ALU.is_equal).then_inc(hotT, 1)
        v.wait_ge(looked, n + 1)
        ch(v.tensor_tensor(prod[:, :, :], pR[:, 0:GRP * NT].rearrange("p (g t) -> p g t", g=GRP), oh_hi[:, :, :],
                           ALU.mult))
        ch(v.tensor_reduce(r5[:, :], prod[:, :, :], axis=AX.X, op=ALU.add))
        v.tensor_tensor(k.rank[:, at], r5[:, :], k.cnt[:, at], ALU.add).then_inc(ranked, 1)
        v.wait_ge(ranked, n + 1)

    def tensor(pe, i, q):
        if i is None:
            pe.matmul(pT[:, 0:NT], k.ident[:, :], k.by_src["start"][:, :], start=True, stop=True,
                      skip_group_check=True).then_inc(added, 1)
            return
        n = i * NG + q
        for g in range(GRP):
            at = bass.ds(i * CH + q * GRP + g, 1)
            mm = pe.matmul(pB[:, g * P:(g + 1) * P], k.src_lo[:, at].to_broadcast([P, P]), k.ident_b[:, :],
                           start=True, stop=True)
        mm.then_inc(rowed, 1)
        pe.wait_ge(hotT, n + 1)
        pe.wait_ge(copied, n + 1)
        for g in range(GRP):
            mm = pe.matmul(pR[:, g * NT:(g + 1) * NT], loT[:, g, :], table[:, :], start=True, stop=True)
        mm.then_inc(looked, 1)
        for g in range(GRP):
            mm = pe.matmul(pT[:, 0:NT], oh_lo[:, g, :], oh_hi[:, g, :], start=False, stop=True,
                           skip_group_check=True)
        mm.then_inc(added, 1)

    def scalar(a):
        with a.Fori(0, NCH * NG) as n:
            a.wait_ge(added, n + 1)
            a.activation(table[:, :], pT[:, 0:NT], ACT.Copy).then_inc(copied, 1)

    return vector, tensor, scalar, 3


def scatter_column_loop(g, k, i, j, b, view, M, stage, staged, ready, sent):
    g.tensor_copy(stage[b][:, :], k.rank[:, cols(i)]).then_inc(staged[b], 1)
    g.wait_ge(staged[b], j + 1)
    g.wait_ge(ready, i + 1)
    g.nop(nofuse=True)
    for t in range(CH):
        g.indirect_dma_start(out=view, in_=M[b][:, t, :], in_offset=None,
                             out_offset=bass.IndirectOffsetOnAxis(ap=stage[b][:, t:t + 1], axis=0)
                             ).then_inc(sent[b], 16)


def release_messages(g, b, j, sent, mfree):
    g.wait_ge(sent[b], (j + 1) * (16 * CH))
    g.nop(nofuse=True).then_inc(mfree[b], 1)


def sheaf_edges(k, name, table, scans, messages, first, carry, w1, b1, w2, b2):
    F = D + 1
    with ExitStack() as st:
        c = Ctx(k.nc, st)
        G = [c.sb(f"{name}_G{b}", [P, CH, F]) for b in range(2)]
        X = [c.sb(f"{name}_X{b}", [P, CH, F]) for b in range(2)]
        M = [c.sb(f"{name}_M{b}", [P, CH, F]) for b in range(2)]
        O = [c.sb(f"{name}_O{b}", [P, CH, D]) for b in range(2)]
        stage = [c.sb(f"{name}_stage{b}", [P, CH], I32) for b in range(2)]
        rstage = [c.sb(f"{name}_rstage{b}", [P, CH], I32) for b in range(2)]
        V = c.sb(name + "_V", [P, CH, 2, D])
        T = c.sb(name + "_T", [P, CH, 2, D])
        nrm = c.sb(name + "_nrm", [P, CH, 2])
        dot = c.sb(name + "_dot", [P, CH])
        begin = c.sb(name + "_begin", [P, CH])
        pair = c.sb(name + "_pair", [P, GRP, 2, D])
        pairT = c.sb(name + "_pairT", [2 * D, 2, GRP * P // 2])
        hid = c.sb(name + "_hid", [P, 2, GRP * P // 2])
        pT = c.ps(name + "_pT", [2 * D, 1024])
        pH = c.ps(name + "_pH", [P, 2, 512])
        pV = c.ps(name + "_pV", [P, 512])
        staged = [c.sem(f"{name}_staged{b}") for b in range(2)]
        rstaged = [c.sem(f"{name}_rstaged{b}") for b in range(2)]
        got = [c.pool_dma_sem(f"{name}_got{b}") for b in range(2)]
        free = [c.sem(f"{name}_free{b}") for b in range(2)]
        sent = [c.pool_dma_sem(f"{name}_sent{b}") for b in range(2)]
        mfree = [c.sem(f"{name}_mfree{b}") for b in range(2)]
        loaded = [c.sem(f"{name}_loaded{b}") for b in range(2)]
        stored = [c.sem(f"{name}_stored{b}") for b in range(2)]
        messaged, scanned, step, paired, transposed, copied, hidden, relued, vectored, evacuated = (
            c.sem(name + s) for s in ("_messaged", "_scanned", "_step", "_paired", "_transposed", "_copied",
                                      "_hidden", "_relued", "_vectored", "_evacuated"))
        HALF = GRP * P // 2
        with k.nc.Block() as block:
            @block.gpsimd
            def _(g):
                def gather(i, b, j):
                    gather_column_loop(g, k, i, j, b, table, G, stage, staged, free, 1, got, k.src_i)

                def scatter(i, b, j):
                    scatter_column_loop(g, k, i, j, b, messages, M, rstage, rstaged, messaged, sent)
                for b in range(2):
                    g.sem_inc(mfree[b], 1)
                gather(0, 0, 0)
                with g.Fori(0, PAIRS) as j:
                    gather(2 * j + 1, 1, j)
                    scatter(2 * j, 0, j)
                    gather(2 * j + 2, 0, j + 1)
                    release_messages(g, 0, j, sent, mfree)
                    scatter(2 * j + 1, 1, j)
                    release_messages(g, 1, j, sent, mfree)
                scatter(NCH - 1, 0, PAIRS)
                g.wait_ge(sent[0], 16 * CH * (PAIRS + 1))

            @block.vector
            def _(v):
                for b in range(2):
                    v.sem_inc(free[b], 1)
                ch = Chain(v, step)
                ch(v.memset(carry[:, 0:D], 0.0))

                def reflect(out, y, n):
                    vec, tmp = V[:, :, n, :], T[:, :, 1, :]
                    ch(v.tensor_tensor(tmp, y, vec, ALU.mult))
                    ch(v.tensor_reduce(dot[:, :], tmp, axis=AX.X, op=ALU.add))
                    ch(v.tensor_tensor(dot[:, :], dot[:, :], nrm[:, :, n], ALU.mult))
                    ch(v.tensor_tensor(tmp, vec, bc(dot[:, :], [P, CH, D], 2), ALU.mult))
                    ch(v.tensor_tensor(out, y, tmp, ALU.subtract))

                def chunk(i, b, j):
                    keep = k.keep_d[:, cols(i)]
                    v.wait_ge(loaded[b], (j + 1) * 16)
                    ch(v.tensor_scalar(begin[:, :], keep, -1.0, 1.0, ALU.mult, ALU.add))
                    ch(v.tensor_tensor(X[b][:, :, :], X[b][:, :, :], bc(begin[:, :], [P, CH, F], 2), ALU.mult))
                    scan_chunk(v, ch, X[b], keep, first, F)
                    v.wait_ge(got[b], (j + 1) * (16 * CH))
                    v.nop(nofuse=True)
                    with v.Fori(0, NG) as q:
                        ch.enter(q, 1)
                        at = bass.ds(q * GRP, GRP)
                        ch(v.tensor_copy(pair[:, :, 0, :], G[b][:, at, 0:D]))
                        v.tensor_copy(pair[:, :, 1, :], X[b][:, at, 0:D]).then_inc(paired, 1)
                        v.wait_ge(vectored, i * NG + q + 1)
                        v.tensor_tensor(V[:, at, :, :].rearrange("p c n d -> p c (n d)"),
                                        pV[:, 0:GRP * 2 * D].rearrange("p (c n) -> p c n", c=GRP),
                                        bc(b2[:, :], [P, GRP, 2 * D], 1), ALU.add).then_inc(evacuated, 1)
                        v.wait_ge(evacuated, i * NG + q + 1)
                        ch.leave(NG, 1)
                    ch(v.tensor_tensor(T[:, :, :, :], V[:, :, :, :], V[:, :, :, :], ALU.mult))
                    ch(v.tensor_reduce(nrm[:, :, :], T[:, :, :, :], axis=AX.X, op=ALU.add))
                    ch(v.tensor_scalar(nrm[:, :, :], nrm[:, :, :], 1e-24, None, ALU.max))
                    ch(v.reciprocal(nrm[:, :, :], nrm[:, :, :]))
                    ch(v.tensor_scalar(nrm[:, :, :], nrm[:, :, :], 2.0, None, ALU.mult))
                    A = T[:, :, 0, :]
                    v.wait_ge(mfree[b], j + 1)
                    reflect(A, X[b][:, :, 0:D], 1)
                    reflect(A, A, 0)
                    ch(v.tensor_tensor(M[b][:, :, 0:D], A, bc(X[b][:, :, D], [P, CH, D], 2), ALU.mult))
                    v.tensor_copy(M[b][:, :, D], k.src_i[:, cols(i)]).then_inc(messaged, 1)
                    v.wait_ge(stored[b], (j + 1) * 16)
                    reflect(A, G[b][:, :, 0:D], 0)
                    reflect(A, A, 1)
                    v.tensor_tensor(O[b][:, :, :], A, bc(G[b][:, :, D], [P, CH, D], 2),
                                    ALU.mult).then_inc(free[b], 1)
                    v.wait_ge(free[b], j + 2)
                    for f in range(D):
                        ch(v.tensor_tensor_scan(O[b][:, :, f], keep, O[b][:, :, f], carry[:, f:f + 1],
                                                ALU.mult, ALU.add))
                    v.tensor_copy(carry[:, 0:D], O[b][:, CH - 1, :]).then_inc(scanned, 1)
                    v.wait_ge(scanned, i + 1)
                over_chunks(v, chunk, ch, 2 + F + 1 + NG + 5 + 20 + 1 + D)

            @block.tensor
            def _(pe):
                def chunk(i, b, j):
                    with pe.Fori(0, NG) as q:
                        n = i * NG + q
                        pe.wait_ge(paired, n + 1)
                        for g in range(GRP):
                            mm = pe.transpose(pT[:, g * P:(g + 1) * P],
                                              pair[:, g, :, :].rearrange("p n d -> p (n d)"), k.ident[:, :])
                        mm.then_inc(transposed, 1)
                        pe.wait_ge(copied, n + 1)
                        for h in range(2):
                            mm = pe.matmul(pH[:, h, 0:HALF], w1[:, :], pairT[:, h, :], start=True, stop=True)
                        mm.then_inc(hidden, 1)
                        pe.wait_ge(relued, n + 1)
                        flat = hid[:, :, :].rearrange("p a q -> p (a q)")
                        for g in range(GRP):
                            mm = pe.matmul(pV[:, g * 2 * D:(g + 1) * 2 * D], flat[:, g * P:(g + 1) * P], w2[:, :],
                                           start=True, stop=True)
                        mm.then_inc(vectored, 1)
                over_chunks(pe, chunk)

            @block.scalar
            def _(a):
                with a.Fori(0, NCH * NG) as n:
                    a.wait_ge(transposed, n + 1)
                    a.activation(pairT[:, :, :].rearrange("p a q -> p (a q)"), pT[:, 0:GRP * P],
                                 ACT.Copy).then_inc(copied, 1)
                    a.wait_ge(hidden, n + 1)
                    a.activation(hid[:, :, :], pH[:, :, 0:HALF], ACT.Relu, bias=b1[:, 0:1]).then_inc(relued, 1)

            @block.sync
            def _(s):
                for b in range(2):
                    s.sem_inc(stored[b], 16)

                def load(i, b):
                    s.dma_start(X[b][:, :, :], rows(table_view(k, F, E))[:, cols(i), :]).then_inc(loaded[b], 16)

                def chunk(i, b, j, more):
                    s.wait_ge(scanned, i + 1)
                    s.dma_start(rows(scans)[:, cols(i), :], O[b][:, :, :]).then_inc(stored[b], 16)
                    if more:
                        load(i + 2, b)
                load(0, 0)
                load(1, 1)
                with s.Fori(0, PAIRS - 1) as j:
                    chunk(2 * j, 0, j, True)
                    chunk(2 * j + 1, 1, j, True)
                chunk(NCH - 3, 0, PAIRS - 1, True)
                chunk(NCH - 2, 1, PAIRS - 1, False)
                chunk(NCH - 1, 0, PAIRS, False)
                s.wait_ge(stored[0], 16 * (PAIRS + 2))
                s.wait_ge(stored[1], 16 * (PAIRS + 1))


def src_order_scan(k, name, messages, scans, carry, F, find_keep):
    with ExitStack() as st:
        c = Ctx(k.nc, st)
        G = [c.sb(f"{name}_G{b}", [P, CH, F]) for b in range(2)]
        O = [c.sb(f"{name}_O{b}", [P, CH, D]) for b in range(2)]
        prev = c.sb(name + "_prev", [P, 1])
        loaded = [c.sem(f"{name}_loaded{b}") for b in range(2)]
        stored = [c.sem(f"{name}_stored{b}") for b in range(2)]
        cleared, scanned, step, prevd, whole = (
            c.sem(name + s) for s in ("_cleared", "_scanned", "_step", "_prevd", "_whole"))
        extra = 3 if find_keep else 0
        with k.nc.Block() as block:
            @block.sync
            def _(s):
                for b in range(2):
                    s.sem_inc(stored[b], 16)
                if find_keep:
                    s.wait_ge(cleared, 1)
                    with k.nc.allow_non_contiguous_dma("one value of each lane"):
                        s.dma_start(prev[1:P, :], rows(messages)[0:P - 1, LANE - 1, D:D + 1]).then_inc(prevd, 16)

                def load(i, b):
                    s.dma_start(G[b][:, :, :], rows(messages)[:, cols(i), :]).then_inc(loaded[b], 16)

                def chunk(i, b, j, more):
                    s.wait_ge(scanned, i + 1)
                    s.dma_start(rows(scans)[:, cols(i), :], O[b][:, :, :]).then_inc(stored[b], 16)
                    if more:
                        load(i + 2, b)
                load(0, 0)
                load(1, 1)
                with s.Fori(0, PAIRS - 1) as j:
                    chunk(2 * j, 0, j, True)
                    chunk(2 * j + 1, 1, j, True)
                chunk(NCH - 3, 0, PAIRS - 1, True)
                chunk(NCH - 2, 1, PAIRS - 1, False)
                chunk(NCH - 1, 0, PAIRS, False)
                if find_keep:
                    s.wait_ge(whole, 1)
                    s.dma_start(k.by_src["whole_row"].rearrange("a p -> p a"), k.whole[:, :]).then_inc(whole, 16)
                    s.wait_ge(whole, 17)
                s.wait_ge(stored[0], 16 * (PAIRS + 2))
                s.wait_ge(stored[1], 16 * (PAIRS + 1))

            @block.vector
            def _(v):
                ch = Chain(v, step)
                ch(v.memset(carry[:, 0:D], 0.0))
                if find_keep:
                    v.memset(prev[:, :], -1.0).then_inc(cleared, 1)
                    v.wait_ge(prevd, 16)

                def chunk(i, b, j):
                    v.wait_ge(loaded[b], (j + 1) * 16)
                    if find_keep:
                        ids = G[b][:, :, D]
                        ch(v.tensor_tensor(k.keep_s[:, bass.ds(i * CH, 1)], ids[:, 0:1], prev[:, :], ALU.is_equal))
                        ch(v.tensor_tensor(k.keep_s[:, bass.ds(i * CH + 1, CH - 1)], ids[:, 1:CH], ids[:, 0:CH - 1],
                                           ALU.is_equal))
                        ch(v.tensor_copy(prev[:, :], ids[:, CH - 1:CH]))
                    v.wait_ge(stored[b], (j + 1) * 16)
                    for f in range(D):
                        ch(v.tensor_tensor_scan(O[b][:, :, f], k.keep_s[:, cols(i)], G[b][:, :, f],
                                                carry[:, f:f + 1], ALU.mult, ALU.add))
                    v.tensor_copy(carry[:, 0:D], O[b][:, CH - 1, :]).then_inc(scanned, 1)
                    v.wait_ge(scanned, i + 1)
                over_chunks(v, chunk, ch, D + extra)
                if find_keep:
                    v.tensor_reduce(k.whole[:, :], k.keep_s[:, :], axis=AX.X, op=ALU.min).then_inc(whole, 1)


def product_edges(k, name, attr, messages, first, w):
    with ExitStack() as st:
        c = Ctx(k.nc, st)
        X = [c.sb(f"{name}_X{b}", [P, CH, D]) for b in range(2)]
        A = [c.sb(f"{name}_A{b}", [P, CH, DE]) for b in range(2)]
        M = [c.sb(f"{name}_M{b}", [P, CH, D]) for b in range(2)]
        rstage = [c.sb(f"{name}_rstage{b}", [P, CH], I32) for b in range(2)]
        begin = c.sb(name + "_begin", [P, CH])
        outer = c.sb(name + "_outer", [P, GRP, D, DE])
        outT = c.sb(name + "_outT", [P, GRP * P])
        pT = c.ps(name + "_pT", [P, 1024])
        pM = c.ps(name + "_pM", [P, 512])
        rstaged = [c.sem(f"{name}_rstaged{b}") for b in range(2)]
        sent = [c.pool_dma_sem(f"{name}_sent{b}") for b in range(2)]
        mfree = [c.sem(f"{name}_mfree{b}") for b in range(2)]
        loaded = [c.sem(f"{name}_loaded{b}") for b in range(2)]
        messaged, used, step, outered, transposed, copied, product, silued = (
            c.sem(name + s) for s in ("_messaged", "_used", "_step", "_outered", "_transposed", "_copied",
                                      "_product", "_silued"))
        norm = 1.0 / float(np.float32(np.sqrt(D * DE)))
        with k.nc.Block() as block:
            @block.gpsimd
            def _(g):
                for b in range(2):
                    g.sem_inc(mfree[b], 1)

                def scatter(i, b, j):
                    scatter_column_loop(g, k, i, j, b, messages, M, rstage, rstaged, messaged, sent)
                with g.Fori(0, PAIRS) as j:
                    scatter(2 * j, 0, j)
                    release_messages(g, 0, j, sent, mfree)
                    scatter(2 * j + 1, 1, j)
                    release_messages(g, 1, j, sent, mfree)
                scatter(NCH - 1, 0, PAIRS)
                g.wait_ge(sent[0], 16 * CH * (PAIRS + 1))

            @block.vector
            def _(v):
                ch = Chain(v, step)
                ch(v.memset(begin[:, :], 0.0))

                def chunk(i, b, j):
                    keep = k.keep_d[:, cols(i)]
                    v.wait_ge(loaded[b], (j + 1) * 32)
                    ch(v.tensor_scalar(begin[:, :], keep, -1.0, 1.0, ALU.mult, ALU.add))
                    ch(v.tensor_tensor(X[b][:, :, :], X[b][:, :, :], bc(begin[:, :], [P, CH, D], 2), ALU.mult))
                    scan_chunk(v, ch, X[b], keep, first, D)
                    v.nop(nofuse=True)
                    with v.Fori(0, NG) as q:
                        at = bass.ds(q * GRP, GRP)
                        v.wait_ge(transposed, i * NG + q + 1)
                        v.tensor_tensor(outer[:, :, :, :], bc(X[b][:, at, :], [P, GRP, D, DE], 3),
                                        bc(A[b][:, at, :], [P, GRP, D, DE], 2), ALU.mult).then_inc(outered, 1)
                    v.engine_nop().then_inc(used, 1)
                over_chunks(v, chunk, ch, 2 + D + 1)

            @block.tensor
            def _(pe):
                pe.sem_inc(transposed, 1)

                def chunk(i, b, j):
                    with pe.Fori(0, NG) as q:
                        n = i * NG + q
                        pe.wait_ge(outered, n + 1)
                        for g in range(GRP):
                            mm = pe.transpose(pT[:, g * P:(g + 1) * P],
                                              outer[:, g, :, :].rearrange("p i j -> p (i j)"), k.ident[:, :])
                        mm.then_inc(transposed, 1)
                        pe.wait_ge(copied, n + 1)
                        for g in range(GRP):
                            mm = pe.matmul(pM[:, g * D:(g + 1) * D], outT[:, g * P:(g + 1) * P], w[:, :],
                                           start=True, stop=True)
                        mm.then_inc(product, 1)
                over_chunks(pe, chunk)

            @block.scalar
            def _(a):
                def chunk(i, b, j):
                    a.wait_ge(mfree[b], j + 1)
                    a.nop(nofuse=True)
                    with a.Fori(0, NG) as q:
                        n = i * NG + q
                        a.wait_ge(transposed, n + 2)
                        a.activation(outT[:, :], pT[:, 0:GRP * P], ACT.Copy).then_inc(copied, 1)
                        a.wait_ge(product, n + 1)
                        a.activation(M[b][:, bass.ds(q * GRP, GRP), :],
                                     pM[:, 0:GRP * D].rearrange("p (g d) -> p g d", g=GRP), ACT.Silu,
                                     scale=norm).then_inc(silued, 1)
                    a.wait_ge(silued, (i + 1) * NG)
                    a.nop(nofuse=True).then_inc(messaged, 1)
                over_chunks(a, chunk)

            @block.sync
            def _(s):
                def load(i, b):
                    s.dma_start(X[b][:, :, :], rows(table_view(k, D, E))[:, cols(i), :]).then_inc(loaded[b], 16)
                    s.dma_start(A[b][:, :, :], rows(attr)[:, cols(i), :]).then_inc(loaded[b], 16)

                def next_load(i, b):
                    s.wait_ge(used, i + 1)
                    load(i + 2, b)
                load(0, 0)
                load(1, 1)
                with s.Fori(0, PAIRS - 1) as j:
                    next_load(2 * j, 0)
                    next_load(2 * j + 1, 1)
                next_load(NCH - 3, 0)



def program(nc, x, src, dst, attr, w, out):
    with ExitStack() as st:
        k = Ctx(nc, st)
        k.src_i = k.sb("src_i", [P, LANE], I32)
        k.keep_d = k.sb("keep_d", [P, LANE])
        k.ident = k.sb("ident", [P, P])
        k.iota = k.sb("iota", [P, P])
        k.part = k.sb("part", [P, 1])
        k.before = k.sb("before", [P, P])
        k.ones = k.sb("ones", [P, P])
        k.ident_b = k.sb("ident_b", [P, P], BF16)
        k.ident128_b = k.sb("ident128_b", [P, P], BF16)
        k.earlier = k.sb("earlier", [P, GRP * P])
        k.node_mask = k.sb("node_mask", [P, NT])
        k.whole = k.sb("whole", [P, 1])
        k.first_dst = k.sb("first_dst", [P, 1], I32)
        k.cnt5 = k.sb("cnt5", [P, GRP])
        k.x = k.sb("x", [P, NT, D])
        y = k.sb("y", [P, NT, D])
        carry = k.sb("carry", [P, 51])
        first = k.sb("first", [P, SPREAD_F])
        k.by_dst = new_order(k, "by_dst")
        k.by_src = new_order(k, "by_src")
        k.lanes = k.dram("lanes", [P, 51])
        k.spread_buf = k.dram("spread_buf", [SPREAD_SIZE])
        scan16 = k.dram("scan16", [E, D])
        carry16 = k.dram("carry16", [P + 1, D])
        tab16 = k.dram("tab16", [NP, D])
        tab16b = k.dram("tab16b", [NP, D])
        messages = k.dram("messages", [E, D + 1])
        messages2 = k.dram("messages2", [E, D])

        k.rank = k.sb("rank", [P, LANE], I32)
        k.keep_s = k.sb("keep_s", [P, LANE])
        with ExitStack() as s12:
            k.h2 = Ctx(nc, s12).sb("h2", [P, NT, C2 + 2])
            with ExitStack() as s1:
                c = Ctx(nc, s1)
                digs = [c.sb(n, [P, LANE], BF16) for n in ("dst_lo", "dst_hi")]
                with ExitStack() as s0:
                    k.dst_i = Ctx(nc, s0).sb("dst_i", [P, LANE], I32)
                    setup(k, x, src, dst)
                    digits(k, "dd", k.dst_i, *digs)
                gat1(k, w, digs, carry, first, y)
            with ExitStack() as s2:
                c = Ctx(nc, s2)
                k.cnt = c.sb("cnt", [P, LANE])
                k.src_lo, k.src_hi = (c.sb(n, [P, LANE], BF16) for n in ("src_lo", "src_hi"))
                digits(k, "ds", k.src_i, k.src_lo, k.src_hi)
                gat2(k, w, carry, first, y)
                gcn(k, w, carry, y, scan16, carry16, tab16, tab16b)
        sheaf(k, w, carry, first, y, scan16, carry16, messages)
        product(k, w, carry, first, y, scan16, carry16, messages2, attr)

        stored = k.sem("out_stored")
        with nc.Block() as block:
            @block.sync
            def _(s):
                s.dma_start(out[0:FULL * P, :].rearrange("(t p) f -> p t f", p=P),
                            k.x[:, 0:FULL, :]).then_inc(stored, 16)
                s.dma_start(out[FULL * P:N, :], k.x[0:REST, FULL, :]).then_inc(stored, 16)
                s.wait_ge(stored, 32)


def load_small(k, name, copies):
    with ExitStack() as st:
        loaded = Ctx(k.nc, st).sem(name + "_loaded")
        with k.nc.Block() as block:
            @block.sync
            def _(s):
                with k.nc.allow_non_contiguous_dma("small weights"):
                    for dst, src in copies:
                        s.dma_start(dst, src).then_inc(loaded, 16)
                s.wait_ge(loaded, 16 * len(copies))


def row_bc(ap, n=P):
    return ap.rearrange("(a f) -> a f", a=1).to_broadcast([n, ap.shape[0]])


def gat1(k, w, digs, carry, first, y):
    nc = k.nc
    F = D + H1
    edges = k.dram("edges1", [P, LANE * F])
    maxes, scans = k.dram("maxes1", [E, H1]), k.dram("scans1", [E, H1 * D + H1])
    mcar, scar = k.dram("mcar1", [P + 1, H1]), k.dram("scar1", [P + 1, H1 * D + H1])
    tab, stab = k.dram("tab1", [NP, F]), k.dram("stab1", [NP, 2 * H1])
    h2 = k.h2
    with ExitStack() as st:
        c = Ctx(nc, st)
        w1 = c.sb("g1_w1", [D, H1 * C1])
        a1 = c.sb("g1_a1", [D, 2, H1 * C1])
        wa = c.sb("g1_wa", [D, 2, H1])
        w1d = c.sb("g1_w1d", [H1 * D, H1 * C1])
        b1 = c.sb("g1_b1", [P, H1 * C1])
        w2 = c.sb("g1_w2", [H1 * C1, C2 + 2])
        a2 = c.sb("g1_a2", [H1 * C1, 2, C2])
        t2 = c.sb("g1_t2", [H1 * C1, 2, C2])
        al = c.sb("g1_al", [P, NT, 2 * H1])
        sv = c.sb("g1_sv", [P, NT, 2 * H1])
        pself = c.sb("g1_pself", [P, NT, H1])
        vector_block(k, "g1z", lambda v, ch: ch(v.memset(w1d[:, :], 0.0)))
        load_small(k, "g1l", [
            (w1[:, :], w["L0_gnn_W1"]),
            (a1[:, 0, :], row_bc(w["L0_gnn_a_src1"].rearrange("h c -> (h c)"), D)),
            (a1[:, 1, :], row_bc(w["L0_gnn_a_dst1"].rearrange("h c -> (h c)"), D)),
            (b1[:, :], row_bc(w["L0_gnn_b1"])),
            (w2[:, 0:C2], w["L0_gnn_W2"]),
            (a2[:, 0, :], row_bc(w["L0_gnn_a_src2"].rearrange("h c -> (h c)"), H1 * C1)),
            (a2[:, 1, :], row_bc(w["L0_gnn_a_dst2"].rearrange("h c -> (h c)"), H1 * C1)),
        ] + [(w1d[D * h:D * h + D, C1 * h:C1 * h + C1], w["L0_gnn_W1"][:, C1 * h:C1 * h + C1]) for h in range(H1)])

        def fold(v, ch):
            for s in range(2):
                ch(v.tensor_tensor(a1[:, s, :], a1[:, s, :], w1[:, :], ALU.mult))
                ch(v.tensor_reduce(wa[:, s, :], a1[:, s, :].rearrange("p (h c) -> p h c", h=H1), axis=AX.X,
                                   op=ALU.add))
                ch(v.tensor_tensor(t2[:, s, :], a2[:, s, :], w2[:, 0:C2], ALU.mult))
                ch(v.tensor_reduce(w2[:, C2 + s:C2 + s + 1], t2[:, s, :], axis=AX.X, op=ALU.add))
        vector_block(k, "g1f", fold)
        node_linear(k, "g1a", k.x, wa[:, :, :].rearrange("p s h -> p (s h)"), al, D, 2 * H1)
        store_nodes(k, "g1t", [k.x[:, :, :], al[:, :, 0:H1]], tab)
        gat_gather(k, "g1g", tab, F, H1, *digs, k.by_dst["count"], edges, maxes, carry)
        order_tables(k, "g1o", k.by_dst["count"], k.by_dst)
        gat_between(k, "g1", H1, al, sv, pself, maxes, mcar, stab, carry, first)
        gat_weigh(k, "g1w", F, H1, edges, scans, first, carry)
        FO = H1 * D + H1
        lane_carries(k, "g1c", carry[:, 0:FO], FO, k.by_dst, ALU.add, scar)
        with ExitStack() as s3:
            c3 = Ctx(nc, s3)
            agg = c3.sb("g1_agg", [P, NT, FO])
            h1 = c3.sb("g1_h1", [P, NT, H1 * C1])
            extract(k, "g1x", scans, scar, k.by_dst, agg, FO, ALU.add)
            with ExitStack() as s4:
                gat_normalise(k, "g1n", agg, k.x, pself, H1, D, Ctx(nc, s4))
            node_linear(k, "g1b", agg[:, :, 0:H1 * D], w1d[:, :], h1, H1 * D, H1 * C1)
            with ExitStack() as s4:
                tmp = Ctx(nc, s4).sb("g1_tmp", [P, NT, H1 * C1])
                selu(k, "g1s", h1, tmp, b1[:, :])
            node_linear(k, "g1c2", h1, w2[:, :], h2, H1 * C1, C2 + 2)


def gat_between(k, name, heads, al, sv, pself, maxes, mcar, stab, carry, first):
    lane_carries(k, name + "m", carry[:, 0:heads], heads, k.by_dst, ALU.max, mcar)
    extract(k, name + "e", maxes, mcar, k.by_dst, pself, heads, ALU.max)
    with ExitStack() as st:
        c = Ctx(k.nc, st)
        step, logits, probs = c.sem(name + "b_step"), c.sem(name + "b_logits"), c.sem(name + "b_probs")
        with k.nc.Block() as block:
            @block.vector
            def _(v):
                ch = Chain(v, step)
                a_src, a_dst, m = al[:, :, 0:heads], al[:, :, heads:2 * heads], sv[:, :, heads:2 * heads]
                ch(v.tensor_copy(sv[:, :, 0:heads], a_dst))
                ch(v.tensor_tensor(m, pself[:, :, :], a_src, ALU.max))
                ch(v.tensor_tensor(m, m, a_dst, ALU.add))
                ch(v.scalar_tensor_tensor(out=m, in0=m, scalar=0.2, in1=m, op0=ALU.mult, op1=ALU.max))
                ch(v.tensor_tensor(pself[:, :, :], a_src, a_dst, ALU.add))
                ch(v.scalar_tensor_tensor(out=pself[:, :, :], in0=pself[:, :, :], scalar=0.2, in1=pself[:, :, :],
                                          op0=ALU.mult, op1=ALU.max))
                v.tensor_tensor(pself[:, :, :], pself[:, :, :], m, ALU.subtract).then_inc(logits, 1)

            @block.scalar
            def _(a):
                a.wait_ge(logits, 1)
                a.activation(pself[:, :, :], pself[:, :, :], ACT.Exp).then_inc(probs, 1)
    store_nodes(k, name + "u", [sv[:, :, :]], stab)
    spread(k, name + "p", sv, 2 * heads, stab, first[:, 0:2 * heads])


def gat_normalise(k, name, agg, x, pself, heads, FX, c):
    tmp = c.sb(name + "_tmp", [P, NT, FX])
    inv = c.sb(name + "_inv", [P, NT, heads])

    def body(v, ch):
        z = agg[:, :, heads * FX:heads * FX + heads]
        ch(v.tensor_tensor(inv[:, :, :], z, pself[:, :, :], ALU.add))
        ch(v.tensor_scalar(inv[:, :, :], inv[:, :, :], 1e-16, None, ALU.add))
        ch(v.reciprocal(inv[:, :, :], inv[:, :, :]))
        for h in range(heads):
            part = agg[:, :, h * FX:(h + 1) * FX]
            ch(v.tensor_tensor(tmp[:, :, :], x, bc(pself[:, :, h], [P, NT, FX], 2), ALU.mult))
            ch(v.tensor_tensor(part, part, tmp[:, :, :], ALU.add))
            ch(v.tensor_tensor(part, part, bc(inv[:, :, h], [P, NT, FX], 2), ALU.mult))
    vector_block(k, name, body)


def gat2(k, w, carry, first, y):
    nc = k.nc
    F = C2 + 1
    edges = k.dram("edges2", [P, LANE * F])
    maxes, scans = k.dram("maxes2", [E, 1]), k.dram("scans2", [E, F])
    mcar, scar = k.dram("mcar2", [P + 1, 1]), k.dram("scar2", [P + 1, F])
    tab, stab = k.dram("tab2", [NP, F]), k.dram("stab2", [NP, 2])
    with ExitStack() as st:
        c = Ctx(nc, st)
        b2 = c.sb("g2_b2", [P, C2])
        wf = c.sb("g2_wf", [C2, D])
        bf = c.sb("g2_bf", [P, D])
        sv = c.sb("g2_sv", [P, NT, 2])
        pself = c.sb("g2_pself", [P, NT, 1])
        load_small(k, "g2l", [(b2[:, :], row_bc(w["L0_gnn_b2"])), (wf[:, :], w["L0_gnn_Wf"]),
                              (bf[:, :], row_bc(w["L0_gnn_bf"]))])
        store_nodes(k, "g2t", [k.h2[:, :, 0:F]], tab)
        gat_gather(k, "g2g", tab, F, 1, k.src_lo, k.src_hi, k.by_src["count"], edges, maxes, carry)
        order_tables(k, "g2o", k.by_src["count"], k.by_src)
        gat_between(k, "g2", 1, k.h2[:, :, C2:C2 + 2], sv, pself, maxes, mcar, stab, carry, first)
        gat_weigh(k, "g2w", F, 1, edges, scans, first, carry)
        lane_carries(k, "g2c", carry[:, 0:F], F, k.by_dst, ALU.add, scar)
        with ExitStack() as s3:
            c3 = Ctx(nc, s3)
            agg = c3.sb("g2_agg", [P, NT, F])
            extract(k, "g2x", scans, scar, k.by_dst, agg, F, ALU.add)
            with ExitStack() as s4:
                gat_normalise(k, "g2n", agg, k.h2[:, :, 0:C2], pself, 1, C2, Ctx(nc, s4))
            with ExitStack() as s4:
                tmp = Ctx(nc, s4).sb("g2_tmp", [P, NT, C2])
                selu(k, "g2s", agg[:, :, 0:C2], tmp, b2[:, :])
            node_linear(k, "g2f", agg[:, :, 0:C2], wf[:, :], y, C2, D)

        def residual(v, ch):
            ch(v.tensor_tensor(y[:, :, :], y[:, :, :], bc(bf[:, :], [P, NT, D], 1), ALU.add))
            ch(v.tensor_tensor(y[:, :, :], y[:, :, :], k.x[:, :, :], ALU.add))
        vector_block(k, "g2r", residual)
        layer_norm(k, "g2y", y, k.x)


def root_inverse(k, name, src, out, floor):
    with ExitStack() as st:
        c = Ctx(k.nc, st)
        t = c.sb(name + "_t", [P, NT])
        ready, rooted, done = c.sem(name + "_ready"), c.sem(name + "_rooted"), c.sem(name + "_done")
        with k.nc.Block() as block:
            @block.vector
            def _(v):
                v.tensor_scalar(t[:, :], src, floor, None, ALU.max).then_inc(ready, 1)
                v.wait_ge(rooted, 1)
                v.reciprocal(out, t[:, :]).then_inc(done, 1)

            @block.scalar
            def _(a):
                a.wait_ge(ready, 1)
                a.activation(t[:, :], t[:, :], ACT.Sqrt).then_inc(rooted, 1)


def gcn(k, w, carry, y, scan16, carry16, tab16, tab16b):
    nc = k.nc
    HG = 32
    with ExitStack() as st:
        c = Ctx(nc, st)
        w1, w2 = c.sb("c_w1", [D, HG]), c.sb("c_w2", [HG, D])
        b1, gamma, beta = (c.sb(n, [P, HG]) for n in ("c_b1", "c_gamma", "c_beta"))
        b2 = c.sb("c_b2", [P, D])
        dinv = c.sb("c_dinv", [P, NT])
        xs = c.sb("c_xs", [P, NT, D])
        agg = c.sb("c_agg", [P, NT, D])
        h = c.sb("c_h", [P, NT, HG])
        load_small(k, "cl", [(w1[:, :], w["L1_gnn_W1"]), (w2[:, :], w["L1_gnn_W2"]),
                             (b1[:, :], row_bc(w["L1_gnn_b1"])), (gamma[:, :], row_bc(w["L1_gnn_gamma"])),
                             (beta[:, :], row_bc(w["L1_gnn_beta"])), (b2[:, :], row_bc(w["L1_gnn_b2"]))])
        vector_block(k, "cd", lambda v, ch: ch(v.tensor_scalar(
            dinv[:, :], k.by_dst["count"][:, :], 1.0, None, ALU.add)))
        root_inverse(k, "cr", dinv[:, :], dinv[:, :], 1.0)

        def aggregate(name, values, table, side):
            vector_block(k, name + "a", lambda v, ch: ch(v.tensor_tensor(
                xs[:, :, :], values, bc(dinv[:, :], [P, NT, D], 2), ALU.mult)))
            store_nodes(k, name + "b", [xs[:, :, :]], table)
            gcn_gather(k, name + "c", table, scan16, carry, side)
            lane_carries(k, name + "d", carry[:, 0:D], D, k.by_dst, ALU.add, carry16)
            extract(k, name + "e", scan16, carry16, k.by_dst, agg, D, ALU.add)

            def finish(v, ch):
                ch(v.tensor_tensor(agg[:, :, :], agg[:, :, :], xs[:, :, :], ALU.add))
                ch(v.tensor_tensor(agg[:, :, :], agg[:, :, :], bc(dinv[:, :], [P, NT, D], 2), ALU.mult))
            vector_block(k, name + "f", finish)

        aggregate("c1", k.x[:, :, :], tab16, count_in_group)
        node_linear(k, "ch", agg, w1[:, :], h, D, HG)
        batch_norm_relu(k, "cn", h, b1, gamma, beta, HG)
        node_linear(k, "co", h, w2[:, :], y, HG, D)
        aggregate("c2", y[:, :, :], tab16b, count_before_group)

        def residual(v, ch):
            ch(v.tensor_tensor(y[:, :, :], agg[:, :, :], bc(b2[:, :], [P, NT, D], 1), ALU.add))
            ch(v.tensor_tensor(y[:, :, :], y[:, :, :], k.x[:, :, :], ALU.add))
        vector_block(k, "cs", residual)
        layer_norm(k, "cy", y, k.x)


def batch_norm_relu(k, name, h, b1, gamma, beta, HG):
    with ExitStack() as st:
        c = Ctx(k.nc, st)
        t = c.sb(name + "_t", [P, NT, HG])
        part = c.sb(name + "_part", [P, HG])
        mean = c.sb(name + "_mean", [P, HG])
        var = c.sb(name + "_var", [P, HG])
        pS = c.ps(name + "_pS", [P, 512])
        step, ready, summed, rooted = (c.sem(name + s) for s in ("_step", "_ready", "_summed", "_rooted"))
        shape = [P, NT, HG]
        with k.nc.Block() as block:
            @block.tensor
            def _(pe):
                for n in range(2):
                    pe.wait_ge(ready, n + 1)
                    pe.matmul(pS[:, n * HG:(n + 1) * HG], k.ones[:, :], part[:, :],
                              start=True, stop=True).then_inc(summed, 1)

            @block.scalar
            def _(a):
                a.wait_ge(ready, 3)
                a.activation(var[:, :], var[:, :], ACT.Sqrt).then_inc(rooted, 1)

            @block.vector
            def _(v):
                ch = Chain(v, step)
                ch(v.tensor_tensor(h[:, :, :], h[:, :, :], bc(b1[:, :], shape, 1), ALU.add))
                ch(v.tensor_tensor(t[:, :, :], h[:, :, :], bc(k.node_mask[:, :], shape, 2), ALU.mult))
                v.tensor_reduce(part[:, :], t[:, :, :].rearrange("p t f -> p f t"), axis=AX.X,
                                op=ALU.add).then_inc(ready, 1)
                v.wait_ge(summed, 1)
                ch(v.tensor_scalar(mean[:, :], pS[:, 0:HG], 1.0 / N, None, ALU.mult))
                ch(v.tensor_tensor(h[:, :, :], h[:, :, :], bc(mean[:, :], shape, 1), ALU.subtract))
                ch(v.tensor_tensor(t[:, :, :], h[:, :, :], h[:, :, :], ALU.mult))
                ch(v.tensor_tensor(t[:, :, :], t[:, :, :], bc(k.node_mask[:, :], shape, 2), ALU.mult))
                v.tensor_reduce(part[:, :], t[:, :, :].rearrange("p t f -> p f t"), axis=AX.X,
                                op=ALU.add).then_inc(ready, 1)
                v.wait_ge(summed, 2)
                v.tensor_scalar(var[:, :], pS[:, HG:2 * HG], 1.0 / N, 1e-5, ALU.mult, ALU.add).then_inc(ready, 1)
                v.wait_ge(rooted, 1)
                ch(v.reciprocal(var[:, :], var[:, :]))
                ch(v.tensor_tensor(var[:, :], var[:, :], gamma[:, :], ALU.mult))
                ch(v.tensor_tensor(h[:, :, :], h[:, :, :], bc(var[:, :], shape, 1), ALU.mult))
                ch(v.tensor_tensor(h[:, :, :], h[:, :, :], bc(beta[:, :], shape, 1), ALU.add))
                ch(v.tensor_scalar(h[:, :, :], h[:, :, :], 0.0, None, ALU.max))


def sheaf(k, w, carry, first, y, scan16, carry16, messages):
    nc = k.nc
    tab = k.dram("tab5", [NP, D + 1])
    with ExitStack() as st:
        c = Ctx(nc, st)
        w1 = c.sb("s_w1", [2 * D, 2, HID])
        b1 = c.sb("s_b1", [2 * HID, 1])
        w2 = c.sb("s_w2", [2 * HID, 2, D])
        b2 = c.sb("s_b2", [P, 2 * D])
        xd = c.sb("s_xd", [P, NT, D + 1])
        agg = c.sb("s_agg", [P, NT, D])
        vector_block(k, "sz", lambda v, ch: ch(v.memset(w2[:, :, :], 0.0)))
        W1, W2 = w["L2_gnn_W1"], w["L2_gnn_W2"]
        load_small(k, "sl", [
            (w1[0:2 * D, 0, :], W1.rearrange("h i -> i h")),
            (w1[0:D, 1, :], W1[:, D:2 * D].rearrange("h i -> i h")),
            (w1[D:2 * D, 1, :], W1[:, 0:D].rearrange("h i -> i h")),
            (b1[0:HID, :], w["L2_gnn_b1"].rearrange("(h a) -> h a", a=1)),
            (b1[HID:2 * HID, :], w["L2_gnn_b1"].rearrange("(h a) -> h a", a=1)),
            (w2[0:HID, 0, :], W2.rearrange("o h -> h o")),
            (w2[HID:2 * HID, 1, :], W2.rearrange("o h -> h o")),
            (b2[:, 0:D], row_bc(w["L2_gnn_b2"])), (b2[:, D:2 * D], row_bc(w["L2_gnn_b2"]))])

        def degrees(v, ch):
            ch(v.tensor_copy(xd[:, :, 0:D], k.x[:, :, :]))
            ch(v.tensor_tensor(xd[:, :, D], k.by_dst["count"][:, :], k.by_src["count"][:, :], ALU.add))
        vector_block(k, "sd", degrees)
        root_inverse(k, "sr", xd[:, :, D], xd[:, :, D], 1e-5)
        store_nodes(k, "st", [xd[:, :, :]], tab)
        spread(k, "sp", xd, D + 1, tab, first[:, 0:D + 1])
        sheaf_edges(k, "se", tab, scan16, messages, first, carry,
                    w1[:, :, :].rearrange("p a h -> p (a h)"), b1, w2[:, :, :].rearrange("p a h -> p (a h)"), b2)
        lane_carries(k, "sc", carry[:, 0:D], D, k.by_dst, ALU.add, carry16)
        extract(k, "sx", scan16, carry16, k.by_dst, agg, D, ALU.add)
        src_order_scan(k, "ss", messages, scan16, carry, D + 1, True)
        lane_carries(k, "sq", carry[:, 0:D], D, k.by_src, ALU.add, carry16)
        extract(k, "sw", scan16, carry16, k.by_src, y, D, ALU.add)

        def residual(v, ch):
            ch(v.tensor_tensor(y[:, :, :], y[:, :, :], agg[:, :, :], ALU.add))
            ch(v.tensor_tensor(y[:, :, :], y[:, :, :], bc(xd[:, :, D], [P, NT, D], 2), ALU.mult))
            ch(v.tensor_tensor(y[:, :, :], y[:, :, :], k.x[:, :, :], ALU.add))
            ch(v.tensor_scalar(y[:, :, :], y[:, :, :], 0.0, None, ALU.max))
            ch(v.tensor_tensor(y[:, :, :], y[:, :, :], k.x[:, :, :], ALU.add))
        vector_block(k, "sv", residual)
        layer_norm(k, "sy", y, k.x)


def product(k, w, carry, first, y, scan16, carry16, messages, attr):
    nc = k.nc
    tab = k.dram("tab6", [NP, D])
    norm_lin = 1.0 / float(np.float32(np.sqrt(D)))
    norm_upd = 1.0 / float(np.float32(np.sqrt(D * D)))
    with ExitStack() as st:
        c = Ctx(nc, st)
        wm = c.sb("p_wm", [P, D])
        wl = c.sb("p_wl", [D, D])
        wu = c.sb("p_wu", [P, 2, D])
        wo = c.sb("p_wo", [D, D])
        agg = c.sb("p_agg", [P, NT, D])
        load_small(k, "pl", [
            (wm[:, :], w["L3_gnn_W_msg_tp"].rearrange("i j h -> (i j) h")), (wl[:, :], w["L3_gnn_W_msg_lin"]),
            (wu[:, 0, :], w["L3_gnn_W_upd_tp"][0:D // 2].rearrange("i j h -> (i j) h")),
            (wu[:, 1, :], w["L3_gnn_W_upd_tp"][D // 2:D].rearrange("i j h -> (i j) h")),
            (wo[:, :], w["L3_gnn_W_upd_lin"])])
        store_nodes(k, "pt", [k.x[:, :, :]], tab)
        spread(k, "pp", k.x, D, tab, first[:, 0:D])
        product_edges(k, "pe", attr, messages, first, wm)
        src_order_scan(k, "ps", messages, scan16, carry, D, False)
        lane_carries(k, "pc", carry[:, 0:D], D, k.by_src, ALU.add, carry16)
        extract(k, "px", scan16, carry16, k.by_src, y, D, ALU.add)
        node_linear(k, "pn", y, wl[:, :], agg, D, D)
        vector_block(k, "pq", lambda v, ch: ch(v.tensor_scalar(
            agg[:, :, :], agg[:, :, :], norm_lin, None, ALU.mult)))
        u = c.sb("p_u", [P, NT, D])
        for half in range(2):
            with ExitStack() as s3:
                o = Ctx(nc, s3).sb(f"p_o{half}", [P, NT, D // 2, D])

                def outer(v, ch):
                    for i in range(D // 2):
                        n = half * (D // 2) + i
                        ch(v.tensor_tensor(o[:, :, i, :], agg[:, :, :], bc(k.x[:, :, n], [P, NT, D], 2), ALU.mult))
                vector_block(k, f"po{half}", outer)
                node_linear(k, f"pm{half}", o[:, :, :, :].rearrange("p t i d -> p t (i d)"), wu[:, half, :],
                            u if half else y, P, D)
        with ExitStack() as s3:
            c3 = Ctx(nc, s3)
            summed, silued = c3.sem("pa_summed"), c3.sem("pa_silued")
            with nc.Block() as block:
                @block.vector
                def _(v):
                    v.tensor_tensor(u[:, :, :], u[:, :, :], y[:, :, :], ALU.add).then_inc(summed, 1)

                @block.scalar
                def _(a):
                    a.wait_ge(summed, 1)
                    a.activation(u[:, :, :], u[:, :, :], ACT.Silu, scale=norm_upd).then_inc(silued, 1)
        node_linear(k, "pw", u, wo[:, :], y, D, D)

        def residual(v, ch):
            ch(v.scalar_tensor_tensor(out=y[:, :, :], in0=y[:, :, :], scalar=norm_lin, in1=k.x[:, :, :],
                                      op0=ALU.mult, op1=ALU.add))
            ch(v.tensor_tensor(y[:, :, :], y[:, :, :], k.x[:, :, :], ALU.add))
        vector_block(k, "pr", residual)
        layer_norm(k, "py", y, k.x)


_EDGE = ["x", "src", "dst", "edge_attr_8"]
_WEIGHTS = ["L0_gnn_W1", "L0_gnn_a_src1", "L0_gnn_a_dst1", "L0_gnn_b1", "L0_gnn_W2", "L0_gnn_a_src2",
            "L0_gnn_a_dst2", "L0_gnn_b2", "L0_gnn_Wf", "L0_gnn_bf", "L1_gnn_W1", "L1_gnn_b1", "L1_gnn_gamma",
            "L1_gnn_beta", "L1_gnn_W2", "L1_gnn_b2", "L2_gnn_W1", "L2_gnn_b1", "L2_gnn_W2", "L2_gnn_b2",
            "L3_gnn_W_msg_tp", "L3_gnn_W_msg_lin", "L3_gnn_W_upd_tp", "L3_gnn_W_upd_lin"]


def kernel(**inputs):
    import numpy as _np
    import concourse.bacc as _bacc
    from concourse import mybir as _mybir
    from concourse.bass_utils import run_bass_kernel_spmd as _run

    nc = _bacc.Bacc("TRN2", target_bir_lowering=False, num_devices=1)
    arrays, args = {}, {}
    for name in _EDGE + _WEIGHTS:
        a = _np.ascontiguousarray(inputs[name])
        arrays[f"in_{name}_dram"] = a
        args[name] = nc.dram_tensor(f"in_{name}_dram", a.shape, _mybir.dt.from_np(a.dtype), kind="ExternalInput").ap()
    out = nc.dram_tensor("out_0_dram", (N, D), F32, kind="ExternalOutput").ap()
    program(nc, args["x"], args["src"], args["dst"], args["edge_attr_8"], args, out)
    r = _run(nc, [arrays], core_ids=[0])
    return r.results[0]["out_0_dram"]
```

```python
import numpy as np
import concourse.bass as bass
from concourse import mybir
from contextlib import ExitStack

F32 = mybir.dt.float32
BF16 = mybir.dt.bfloat16
I32 = mybir.dt.int32
ALU = mybir.AluOpType
ACT = mybir.ActivationFunctionType
AX = mybir.AxisListType

P = 128
N, E = 12500, 400000
LANE = E // P
CH = 125
NCH = LANE // CH
PAIRS = NCH // 2
GRP = 5
NG = CH // GRP
NT = 100
NP = NT * P
XT = 25
FULL, REST = N // P, N % P
D = 16
H1, C1 = 3, 32
C2 = 32
HID = 64
DE = 8
BIG = 1e30
SELU_ALPHA, SELU_SCALE = 1.6732632423543772, 1.0507009873554805


class Chain:

    def __init__(self, eng, sem):
        self.eng, self.sem, self.n, self.base, self.starts = eng, sem, 0, [], []

    def loose(self, ins):
        self.n += 1
        ins.then_inc(self.sem, 1)

    def wait(self):
        self.eng.wait_ge(self.sem, sum(self.base[1:], self.base[0]) + self.n if self.base else self.n)

    def __call__(self, ins):
        self.loose(ins)
        self.wait()

    def enter(self, i, per):
        self.base.append(i * per)
        self.starts.append(self.n)

    def leave(self, count, per):
        assert self.n - self.starts[-1] == per, (self.n - self.starts[-1], per)
        self.n = self.starts.pop() + count * per
        self.base.pop()


def over_chunks(eng, body, chain=None, per=0):
    with eng.Fori(0, PAIRS) as j:
        if chain:
            chain.enter(j, 2 * per)
        body(2 * j, 0, j)
        body(2 * j + 1, 1, j)
        if chain:
            chain.leave(PAIRS, 2 * per)
    body(NCH - 1, 0, PAIRS)


def cols(i, n=CH):
    return bass.ds(i * n, n)


def rows(ap):
    return ap[0:E, :].rearrange("(p c) f -> p c f", p=P)


def bc(ap, shape, axis):
    return ap.unsqueeze(axis).to_broadcast(shape)


class Ctx:

    def __init__(self, nc, stack):
        self.nc, self.stack, self.count = nc, stack, 0

    def sb(self, name, shape, dt=F32):
        return self.stack.enter_context(self.nc.sbuf_tensor(name, shape, dt))[tuple(slice(None) for _ in shape)]

    def ps(self, name, shape, dt=F32):
        return self.stack.enter_context(self.nc.psum_tensor(name, shape, dt))[tuple(slice(None) for _ in shape)]

    def sem(self, name):
        sem = self.stack.enter_context(self.nc.semaphore(name))
        self.stack.callback(self.nc.sync.sem_clear, sem)
        return sem

    def pool_dma_sem(self, name):
        sem = self.stack.enter_context(self.nc.semaphore(name))
        self.stack.callback(self.nc.gpsimd.sem_clear, sem)
        self.stack.callback(self.nc.gpsimd.dma_reset, range(sem.num, sem.num + 1))
        return sem

    def dram(self, name, shape, dt=F32):
        return self.nc.dram_tensor(name, shape, dt).ap()


def scope(k):
    return Ctx(k.nc, k.stack.enter_context(ExitStack()))



def node_linear(k, name, src, w, out, K, M):
    groups = NT // GRP
    with ExitStack() as st:
        c = Ctx(k.nc, st)
        stage = [c.sb(f"{name}_stage{b}", [P, GRP, K]) for b in range(2)]
        tT = [c.sb(f"{name}_tT{b}", [K, GRP * P]) for b in range(2)]
        pT = [c.ps(f"{name}_pT{b}", [K, 1024]) for b in range(2)]
        pO = [c.ps(f"{name}_pO{b}", [P, 512]) for b in range(2)]
        staged, transposed, copied, product, evacuated = (
            c.sem(name + s) for s in ("_staged", "_transposed", "_copied", "_product", "_evacuated"))
        with k.nc.Block() as block:
            @block.vector
            def _(v):
                def stage_group(n, b, first=False):
                    if not first:
                        v.wait_ge(transposed, n - 1)
                    v.tensor_copy(stage[b][:, :, :], src[:, cols(n, GRP), :]).then_inc(staged, 1)

                def evacuate(n, b):
                    v.wait_ge(product, n + 1)
                    v.tensor_copy(out[:, cols(n, GRP), :],
                                  pO[b][:, 0:GRP * M].rearrange("p (g m) -> p g m", g=GRP)).then_inc(evacuated, 1)
                stage_group(0, 0, True)
                stage_group(1, 1, True)
                with v.Fori(0, groups // 2 - 1) as j:
                    stage_group(2 * j + 2, 0)
                    evacuate(2 * j, 0)
                    stage_group(2 * j + 3, 1)
                    evacuate(2 * j + 1, 1)
                evacuate(groups - 2, 0)
                evacuate(groups - 1, 1)

            @block.scalar
            def _(a):
                def copy(n, b):
                    a.wait_ge(transposed, n + 1)
                    a.activation(tT[b][:, :], pT[b][:, 0:GRP * P], ACT.Copy).then_inc(copied, 1)
                with a.Fori(0, groups // 2) as j:
                    copy(2 * j, 0)
                    copy(2 * j + 1, 1)

            @block.tensor
            def _(pe):
                def transpose(n, b):
                    pe.wait_ge(staged, n + 1)
                    pe.nop(nofuse=True)
                    for g in range(GRP):
                        mm = pe.transpose(pT[b][:, g * P:(g + 1) * P], stage[b][:, g, :], k.ident[:, :])
                    mm.then_inc(transposed, 1)

                def multiply(n, b, first=False):
                    pe.wait_ge(copied, n + 1)
                    if not first:
                        pe.wait_ge(evacuated, n - 1)
                    for g in range(GRP):
                        mm = pe.matmul(pO[b][:, g * M:(g + 1) * M], tT[b][:, g * P:(g + 1) * P], w,
                                       start=True, stop=True)
                    mm.then_inc(product, 1)
                transpose(0, 0)
                transpose(1, 1)
                multiply(0, 0, True)
                transpose(2, 0)
                multiply(1, 1, True)
                with pe.Fori(1, groups // 2 - 1) as j:
                    transpose(2 * j + 1, 1)
                    multiply(2 * j, 0)
                    transpose(2 * j + 2, 0)
                    multiply(2 * j + 1, 1)
                transpose(groups - 1, 1)
                multiply(groups - 2, 0)
                multiply(groups - 1, 1)


def layer_norm(k, name, x, out):
    with ExitStack() as st:
        c = Ctx(k.nc, st)
        sq = c.sb(name + "_sq", [P, NT, D])
        mean = c.sb(name + "_mean", [P, NT])
        var = c.sb(name + "_var", [P, NT])
        sd = c.sb(name + "_sd", [P, NT])
        step, var_ready, sd_ready = c.sem(name + "_step"), c.sem(name + "_var_ready"), c.sem(name + "_sd_ready")
        with k.nc.Block() as block:
            @block.vector
            def _(v):
                ch = Chain(v, step)
                ch(v.tensor_reduce(mean[:, :], x[:, :, :], axis=AX.X, op=ALU.add))
                ch(v.tensor_scalar(mean[:, :], mean[:, :], 1.0 / D, None, ALU.mult))
                ch(v.tensor_tensor(x[:, :, :], x[:, :, :], bc(mean[:, :], [P, NT, D], 2), ALU.subtract))
                ch(v.tensor_tensor(sq[:, :, :], x[:, :, :], x[:, :, :], ALU.mult))
                ch(v.tensor_reduce(var[:, :], sq[:, :, :], axis=AX.X, op=ALU.add))
                v.tensor_scalar(var[:, :], var[:, :], 1.0 / D, 1e-5, ALU.mult, ALU.add).then_inc(var_ready, 1)
                v.wait_ge(sd_ready, 1)
                ch(v.reciprocal(var[:, :], sd[:, :]))
                ch(v.tensor_tensor(out[:, :, :], x[:, :, :], bc(var[:, :], [P, NT, D], 2), ALU.mult))

            @block.scalar
            def _(a):
                a.wait_ge(var_ready, 1)
                a.activation(sd[:, :], var[:, :], ACT.Sqrt).then_inc(sd_ready, 1)


def selu(k, name, x, tmp, bias):
    with ExitStack() as st:
        c = Ctx(k.nc, st)
        step, neg, exps = c.sem(name + "_step"), c.sem(name + "_neg"), c.sem(name + "_exps")
        shape = [P, NT, x.shape[2]]
        with k.nc.Block() as block:
            @block.vector
            def _(v):
                ch = Chain(v, step)
                ch(v.tensor_tensor(x[:, :, :], x[:, :, :], bc(bias, shape, 1), ALU.add))
                v.tensor_scalar(tmp[:, :, :], x[:, :, :], 0.0, None, ALU.min).then_inc(neg, 1)
                ch(v.tensor_scalar(x[:, :, :], x[:, :, :], 0.0, SELU_SCALE, ALU.max, ALU.mult))
                v.wait_ge(exps, 1)
                ch(v.tensor_scalar(tmp[:, :, :], tmp[:, :, :], 1.0, SELU_ALPHA * SELU_SCALE,
                                   ALU.subtract, ALU.mult))
                ch(v.tensor_tensor(x[:, :, :], x[:, :, :], tmp[:, :, :], ALU.add))

            @block.scalar
            def _(a):
                a.wait_ge(neg, 1)
                a.activation(tmp[:, :, :], tmp[:, :, :], ACT.Exp).then_inc(exps, 1)


def store_nodes(k, name, parts, table):
    with ExitStack() as st:
        c = Ctx(k.nc, st)
        stored = c.sem(name + "_stored")
        with k.nc.Block() as block:
            @block.sync
            def _(s):
                at = 0
                view = table[0:NP, :].rearrange("(t p) f -> p t f", p=P)
                for part in parts:
                    w = part.shape[2]
                    s.dma_start(view[:, :, at:at + w], part).then_inc(stored, 16)
                    at += w
                s.wait_ge(stored, 16 * len(parts))


def vector_block(k, name, body):
    with ExitStack() as st:
        step = Ctx(k.nc, st).sem(name + "_step")
        with k.nc.Block() as block:
            @block.vector
            def _(v):
                body(v, Chain(v, step))



def lane_carries(k, name, last, F, order, op, scans):
    with ExitStack() as st:
        c = Ctx(k.nc, st)
        T = c.sb(name + "_T", [F, P])
        whole = c.sb(name + "_whole", [F, P])
        carried = c.sb(name + "_carried", [P, F])
        ends = c.sb(name + "_ends", [P, F])
        out_sem, in_sem, step, shifted, back = (
            c.sem(name + s) for s in ("_out", "_in", "_step", "_shifted", "_back"))
        got, sent = c.pool_dma_sem(name + "_got"), c.pool_dma_sem(name + "_sent")
        buf, table = k.lanes[0:P, 0:F], k.carried[0:P + 1, 0:F]
        scanned = 2 if op == ALU.add else 3
        with k.nc.Block() as block:
            @block.vector
            def _(v):
                ch = Chain(v, step)
                ch(v.memset(carried[:, :], 0.0))
                v.wait_ge(in_sem, 32)
                if op == ALU.add:
                    ch(v.tensor_tensor_scan(T[:, :], whole[:, :], T[:, :], 0.0, ALU.mult, ALU.add))
                else:
                    ch(v.tensor_scalar(whole[:, :], whole[:, :], 1.0, BIG, ALU.subtract, ALU.mult))
                    ch(v.tensor_tensor_scan(T[:, :], whole[:, :], T[:, :], -BIG, ALU.add, ALU.max))
                v.wait_ge(back, 16)
                v.wait_ge(got, 16)
                ch(v.tensor_tensor(ends[:, :], ends[:, :], carried[:, :], op))

            @block.gpsimd
            def _(g):
                g.indirect_dma_start(out=ends[:, :], out_offset=None, in_=scans[0:E, :],
                                     in_offset=bass.IndirectOffsetOnAxis(ap=order["mend_from"][:, 0:1], axis=0)
                                     ).then_inc(got, 16)
                g.wait_ge(step, scanned + 1)
                g.indirect_dma_start(out=scans, in_=ends[:, :], in_offset=None,
                                     out_offset=bass.IndirectOffsetOnAxis(ap=order["mend_to"][:, 0:1], axis=0)
                                     ).then_inc(sent, 16)
                g.wait_ge(sent, 16)

            @block.sync
            def _(s):
                with k.nc.allow_non_contiguous_dma("transpose of a small tile"):
                    s.dma_start(buf, last).then_inc(out_sem, 16)
                    s.wait_ge(out_sem, 16)
                    s.dma_start(T[:, :], buf.rearrange("p f -> f p")).then_inc(in_sem, 16)
                    s.dma_start(whole[:, :], order["whole_row"].to_broadcast([F, P])).then_inc(in_sem, 16)
                    s.wait_ge(step, scanned)
                    s.dma_start(table[0:P, :].rearrange("p f -> f p"), T[:, :]).then_inc(shifted, 16)
                    s.wait_ge(shifted, 16)
                    s.dma_start(carried[1:P, :], table[0:P - 1, :]).then_inc(back, 16)


def mend_tables(k, name, order, first_id):
    tab = k.dram(name + "_tab", [NP, 3])
    with ExitStack() as st:
        c = Ctx(k.nc, st)
        node = c.sb(name + "_node", [P, NT, 3])
        row = c.sb(name + "_row", [P, 3])
        to = c.sb(name + "_to", [P, 1])
        spare = c.sb(name + "_spare", [P, 1])

        def fields(v, ch):
            ch(v.tensor_copy(node[:, :, 0], order["end"][:, :]))
            ch(v.tensor_copy(node[:, :, 1], order["end_lane"][:, :]))
            ch(v.tensor_copy(node[:, :, 2], order["cross"][:, :]))
        vector_block(k, name + "f", fields)
        store_nodes(k, name + "s", [node[:, :, :]], tab)
        got, step = c.pool_dma_sem(name + "_got"), c.sem(name + "_step")
        with k.nc.Block() as block:
            @block.gpsimd
            def _(g):
                g.indirect_dma_start(out=row[:, :], out_offset=None, in_=tab,
                                     in_offset=bass.IndirectOffsetOnAxis(ap=first_id[:, 0:1], axis=0)
                                     ).then_inc(got, 16)

            @block.vector
            def _(v):
                ch = Chain(v, step)
                v.wait_ge(got, 16)
                ch(v.tensor_copy(order["mend_from"][:, :], row[:, 0:1]))
                ch(v.tensor_tensor(row[:, 1:2], row[:, 1:2], k.part[:, :], ALU.is_equal))
                ch(v.tensor_tensor(row[:, 1:2], row[:, 1:2], row[:, 2:3], ALU.mult))
                ch(v.tensor_scalar(spare[:, :], k.part[:, :], float(E), None, ALU.add))
                ch(v.tensor_tensor(to[:, :], row[:, 0:1], spare[:, :], ALU.subtract))
                ch(v.tensor_tensor(to[:, :], to[:, :], row[:, 1:2], ALU.mult))
                ch(v.tensor_tensor(to[:, :], to[:, :], spare[:, :], ALU.add))
                ch(v.tensor_copy(order["mend_to"][:, :], to[:, :]))


def extract(k, name, scans, order, out, F, op):
    with ExitStack() as st:
        c = Ctx(k.nc, st)
        si = [c.sb(f"{name}_si{b}", [P, XT], I32) for b in range(2)]
        gs = [c.sb(f"{name}_gs{b}", [P, XT, F]) for b in range(2)]
        staged, joined = ([c.sem(f"{name}_{s}{b}") for b in range(2)] for s in ("staged", "joined"))
        got = [c.pool_dma_sem(f"{name}_got{b}") for b in range(2)]
        shape = [P, XT, F]
        with k.nc.Block() as block:
            @block.gpsimd
            def _(g):
                def step(i, b, j):
                    g.wait_ge(joined[b], j + 1)
                    g.tensor_copy(si[b][:, :], order["end"][:, cols(i, XT)]).then_inc(staged[b], 1)
                    g.wait_ge(staged[b], j + 1)
                    g.nop(nofuse=True)
                    for t in range(XT):
                        g.indirect_dma_start(out=gs[b][:, t, :], out_offset=None, in_=scans[0:E, :],
                                             in_offset=bass.IndirectOffsetOnAxis(ap=si[b][:, t:t + 1], axis=0)
                                             ).then_inc(got[b], 16)
                with g.Fori(0, NT // XT // 2) as j:
                    step(2 * j, 0, j)
                    step(2 * j + 1, 1, j)

            @block.vector
            def _(v):
                for b in range(2):
                    v.sem_inc(joined[b], 1)

                def step(i, b, j):
                    v.wait_ge(got[b], (j + 1) * (16 * XT))
                    if op == ALU.add:
                        v.tensor_tensor(out[:, cols(i, XT), :], gs[b][:, :, :],
                                        bc(order["some"][:, cols(i, XT)], shape, 2), ALU.mult).then_inc(joined[b], 1)
                    else:
                        v.tensor_tensor(out[:, cols(i, XT), :], gs[b][:, :, :],
                                        bc(order["none_neg"][:, cols(i, XT)], shape, 2), ALU.add).then_inc(joined[b], 1)
                with v.Fori(0, NT // XT // 2) as j:
                    step(2 * j, 0, j)
                    step(2 * j + 1, 1, j)


def spread(k, name, values, F, table, first):
    view = table_view(k, F, E + NP)
    with ExitStack() as st:
        c = Ctx(k.nc, st)
        si = c.sb(name + "_si", [P, XT], I32)
        sv = c.sb(name + "_sv", [P, XT, F])
        staged = c.sem(name + "_staged")
        sent, got = c.pool_dma_sem(name + "_sent"), c.pool_dma_sem(name + "_got")
        with k.nc.Block() as block:
            @block.gpsimd
            def _(g):
                with g.Fori(0, NT // XT) as i:
                    g.tensor_copy(si[:, :], k.by_dst["begin"][:, cols(i, XT)]).then_inc(staged, 1)
                    g.tensor_copy(sv[:, :, :], values[:, cols(i, XT), :]).then_inc(staged, 1)
                    g.wait_ge(staged, 2 * i + 2)
                    g.nop(nofuse=True)
                    for t in range(XT):
                        g.indirect_dma_start(out=view, in_=sv[:, t, :], in_offset=None,
                                             out_offset=bass.IndirectOffsetOnAxis(ap=si[:, t:t + 1], axis=0)
                                             ).then_inc(sent, 16)
                    g.wait_ge(sent, (i + 1) * (16 * XT))
                    g.nop(nofuse=True)
                g.indirect_dma_start(out=first, out_offset=None, in_=table,
                                     in_offset=bass.IndirectOffsetOnAxis(ap=k.first_dst[:, 0:1], axis=0)
                                     ).then_inc(got, 16)
                g.wait_ge(got, 16)


def table_view(k, F, n):
    return k.spread_buf[0:n * F].rearrange("(r f) -> r f", f=F)


def gather_column_loop(g, k, i, j, b, table, G, stage, staged, freed, credit, got, index):
    g.wait_ge(freed[b], (j + 1) * credit)
    g.tensor_copy(stage[b][:, :], index[:, cols(i)]).then_inc(staged[b], 1)
    g.wait_ge(staged[b], j + 1)
    g.nop(nofuse=True)
    for t in range(CH):
        g.indirect_dma_start(out=G[b][:, t, :], out_offset=None, in_=table,
                             in_offset=bass.IndirectOffsetOnAxis(ap=stage[b][:, t:t + 1], axis=0)
                             ).then_inc(got[b], 16)



def setup(k, x, src, dst):
    c = k
    with ExitStack() as st:
        t = Ctx(k.nc, st)
        iota_i = t.sb("iota_i", [P, P], I32)
        part_i = t.sb("part_i", [P, 1], I32)
        part_one = t.sb("part_one", [P, P])
        lane_first = t.sb("lane_first", [P, 1], I32)
        loaded, made, step, whole_out = (t.sem(s) for s in ("su_loaded", "su_made", "su_step", "su_whole"))
        xclear = t.sem("su_xclear")
        with k.nc.Block() as block:
            @block.sync
            def _(s):
                s.dma_start(c.dst_i[:, :], dst.rearrange("(p c) -> p c", p=P)).then_inc(loaded, 16)
                s.dma_start(c.src_i[:, :], src.rearrange("(p c) -> p c", p=P)).then_inc(loaded, 16)
                s.wait_ge(xclear, 2)
                with k.nc.allow_non_contiguous_dma("one value of each lane"):
                    s.dma_start(lane_first[1:P, :],
                                dst.rearrange("(p c) -> p c", p=P)[0:P - 1, LANE - 1:LANE]).then_inc(loaded, 16)
                    s.dma_start(c.first_dst[:, :],
                                dst.rearrange("(p c) -> p c", p=P)[:, 0:1]).then_inc(loaded, 16)
                s.dma_start(c.x[:, 0:FULL, :],
                            x[0:FULL * P, :].rearrange("(t p) f -> p t f", p=P)).then_inc(loaded, 16)
                s.dma_start(c.x[0:REST, FULL, :], x[FULL * P:N, :]).then_inc(loaded, 16)
                s.wait_ge(made, 1)
                s.dma_start(c.by_dst["whole_row"].rearrange("a p -> p a"), c.whole[:, :]).then_inc(whole_out, 16)
                s.wait_ge(whole_out, 16)

            @block.gpsimd
            def _(g):
                g.iota(iota_i[:, :], pattern=[[1, P]], base=0, channel_multiplier=0).then_inc(step, 1)
                g.iota(part_i[:, :], pattern=[[0, 1]], base=0, channel_multiplier=1).then_inc(step, 1)

            @block.vector
            def _(v):
                v.memset(lane_first[:, :], -1).then_inc(xclear, 1)
                v.memset(c.x[:, FULL:NT, :], 0.0).then_inc(xclear, 1)
                v.wait_ge(step, 2)
                ch = Chain(v, step)
                ch.n = 2
                ch(v.tensor_copy(c.iota[:, :], iota_i[:, :]))
                ch(v.tensor_copy(c.part[:, :], part_i[:, :]))
                ch(v.tensor_scalar(c.ident[:, :], c.iota[:, :], c.part[:, 0:1], None, ALU.is_equal))
                ch(v.tensor_scalar(c.before[:, :], c.iota[:, :], c.part[:, 0:1], None, ALU.is_gt))
                ch(v.memset(c.ones[:, :], 1.0))
                ch(v.tensor_copy(c.ident_b[:, :], c.ident[:, :]))
                ch(v.tensor_scalar(c.ident128_b[:, :], c.ident[:, :], float(P), None, ALU.mult))
                ch(v.memset(c.earlier[:, 0:(GRP - 1) * P], 1.0))
                ch(v.tensor_scalar(c.earlier[:, (GRP - 1) * P:], c.iota[:, :], c.part[:, 0:1], None, ALU.is_lt))
                ch(v.memset(c.node_mask[:, :], 1.0))
                ch(v.memset(c.node_mask[:, FULL + 1:NT], 0.0))
                ch(v.tensor_scalar(c.node_mask[:, FULL:FULL + 1], c.part[:, 0:1], float(REST), None, ALU.is_lt))
                v.wait_ge(loaded, 96)
                ch(v.tensor_tensor(c.keep_d[:, 0:1], c.dst_i[:, 0:1], lane_first[:, :], ALU.is_equal))
                ch(v.tensor_tensor(c.keep_d[:, 1:LANE], c.dst_i[:, 1:LANE], c.dst_i[:, 0:LANE - 1], ALU.is_equal))
                v.tensor_reduce(c.whole[:, :], c.keep_d[:, :], axis=AX.X, op=ALU.min).then_inc(made, 1)
                v.wait_ge(made, 1)


SPREAD_F = 17
SPREAD_PIECE = 4250
SPREAD_PIECES = (E + NP) * SPREAD_F // (P * SPREAD_PIECE) + 1
SPREAD_SIZE = SPREAD_PIECES * P * SPREAD_PIECE


def digits(k, name, src_i, lo, hi):
    with ExitStack() as st:
        t = Ctx(k.nc, st).sb(name + "_t", [P, LANE], I32)

        def body(v, ch):
            ch(v.tensor_scalar(t[:, :], src_i[:, :], P - 1, None, ALU.bitwise_and))
            ch(v.tensor_copy(lo[:, :], t[:, :]))
            ch(v.tensor_scalar(t[:, :], src_i[:, :], 7, None, ALU.logical_shift_right))
            ch(v.tensor_copy(hi[:, :], t[:, :]))
        vector_block(k, name, body)


def order_tables(k, name, counts, order):
    with ExitStack() as st:
        c = Ctx(k.nc, st)
        pt = c.ps(name + "_pt", [P, 512])
        tot = c.sb(name + "_tot", [P, NT])
        run = c.sb(name + "_run", [P, NT])
        start = order["start"]
        endf = c.sb(name + "_endf", [P, NT])
        le = c.sb(name + "_le", [P, NT])
        ls = c.sb(name + "_ls", [P, NT])
        lane0 = c.sb(name + "_lane0", [P, P])
        ge = c.sb(name + "_ge", [P, NT, P])
        idx = c.sb(name + "_idx", [P, NT], I32)
        idf = c.sb(name + "_idf", [P, NT])
        summed, iotad, step = (c.sem(name + s) for s in ("_summed", "_iotad", "_step"))
        with k.nc.Block() as block:
            @block.tensor
            def _(pe):
                pe.matmul(pt[:, 0:NT], k.before[:, :], counts[:, :], start=True, stop=True)
                pe.matmul(pt[:, NT:2 * NT], k.ones[:, :], counts[:, :], start=True, stop=True).then_inc(summed, 1)

            @block.gpsimd
            def _(g):
                g.iota(idx[:, :], pattern=[[P, NT]], base=E, channel_multiplier=1).then_inc(iotad, 1)

            @block.vector
            def _(v):
                ch = Chain(v, step)
                ch(v.memset(ge[:, 0, 0:NT], 1.0))
                v.wait_ge(summed, 1)
                ch(v.tensor_copy(tot[:, :], pt[:, NT:2 * NT]))
                ch(v.tensor_tensor_scan(run[:, :], ge[:, 0, 0:NT], tot[:, :], 0.0, ALU.mult, ALU.add))
                ch(v.tensor_tensor(run[:, :], run[:, :], tot[:, :], ALU.subtract))
                ch(v.tensor_tensor(start[:, :], run[:, :], pt[:, 0:NT], ALU.add))
                ch(v.tensor_scalar(order["some"][:, :], counts[:, :], 0.5, None, ALU.is_gt))
                ch(v.tensor_scalar(order["none_neg"][:, :], order["some"][:, :], 1.0, BIG, ALU.subtract, ALU.mult))
                ch(v.tensor_tensor(endf[:, :], start[:, :], counts[:, :], ALU.add))
                ch(v.tensor_scalar(endf[:, :], endf[:, :], 1.0, 0.0, ALU.subtract, ALU.max))
                ch(v.tensor_copy(order["end"][:, :], endf[:, :]))
                ch(v.tensor_scalar(lane0[:, :], k.iota[:, :], float(LANE), float(LANE), ALU.mult, ALU.add))
                for pos, lane in ((endf, le), (start, ls)):
                    ch(v.tensor_tensor(ge[:, :, :], bc(pos[:, :], [P, NT, P], 2), bc(lane0[:, :], [P, NT, P], 1),
                                       ALU.is_ge))
                    ch(v.tensor_reduce(lane[:, :], ge[:, :, :], axis=AX.X, op=ALU.add))
                ch(v.tensor_copy(order["end_lane"][:, :], le[:, :]))
                ch(v.tensor_tensor(order["cross"][:, :], le[:, :], ls[:, :], ALU.is_gt))
                ch(v.tensor_tensor(order["cross"][:, :], order["cross"][:, :], order["some"][:, :], ALU.mult))
                v.wait_ge(iotad, 1)
                ch(v.tensor_copy(idf[:, :], idx[:, :]))
                ch(v.tensor_tensor(endf[:, :], start[:, :], idf[:, :], ALU.subtract))
                ch(v.tensor_tensor(endf[:, :], endf[:, :], order["some"][:, :], ALU.mult))
                ch(v.tensor_tensor(endf[:, :], endf[:, :], idf[:, :], ALU.add))
                ch(v.tensor_copy(order["begin"][:, :], endf[:, :]))


def new_order(k, name):
    o = {}
    for f in ("start", "some", "none_neg", "cross", "count"):
        o[f] = k.sb(f"{name}_{f}", [P, NT])
    for f in ("end", "end_lane", "begin"):
        o[f] = k.sb(f"{name}_{f}", [P, NT], I32)
    for f in ("mend_from", "mend_to"):
        o[f] = k.sb(f"{name}_{f}", [P, 1], I32)
    o["whole_row"] = k.dram(f"{name}_whole_row", [1, P])
    return o



def scan_chunk(v, ch, data, keep, carry, F, op=ALU.mult, op1=ALU.add, at=0):
    for f in range(F):
        ch.loose(v.tensor_tensor_scan(data[:, :, at + f], keep, data[:, :, at + f], carry[:, f:f + 1], op, op1))
    ch.wait()
    ch(v.tensor_copy(carry[:, 0:F], data[:, CH - 1, at:at + F]))


def histograms(k, c, name):
    digits_of = ((k.dst_lo, k.dst_hi), (k.src_lo, k.src_hi))
    counts = (k.by_dst["count"], k.by_src["count"])
    oh_lo = [c.sb(f"{name}_oh_lo{o}", [P, GRP, P], BF16) for o in range(2)]
    oh_hi = [c.sb(f"{name}_oh_hi{o}", [P, GRP, NT], BF16) for o in range(2)]
    acc = [c.ps(f"{name}_acc{o}", [P, 512]) for o in range(2)]
    cleared, ready, used, counted, zero_made, zeroed = (
        c.sem(name + s) for s in ("_cleared", "_ready", "_used", "_counted", "_zero_made", "_zeroed"))
    zeros = c.sb(name + "_zeros", [P, SPREAD_PIECE])

    def scalar(a):
        a.wait_ge(zero_made, 1)
        flat = k.spread_buf[:].rearrange("(r p f) -> r p f", p=P, f=SPREAD_PIECE)
        for r in range(SPREAD_PIECES):
            a.dma_start(flat[r], zeros[:, :]).then_inc(zeroed, 16)
        a.wait_ge(zeroed, 16 * SPREAD_PIECES)

    def vector_first(v):
        v.memset(zeros[:, :], 0.0).then_inc(zero_made, 1)
        for o in range(2):
            v.memset(oh_lo[o][:, :, :], 0.0).then_inc(cleared, 1)
        v.wait_ge(cleared, 2)

    def vector(v, ch, i, q):
        at = bass.ds(i * CH + q * GRP, GRP)
        v.wait_ge(used, i * NG + q + 1)
        for o, (lo, hi) in enumerate(digits_of):
            v.tensor_tensor(oh_lo[o][:, :, :], bc(lo[:, at], [P, GRP, P], 2),
                            bc(k.iota[:, :], [P, GRP, P], 1), ALU.is_equal).then_inc(ready, 1)
            v.tensor_tensor(oh_hi[o][:, :, :], bc(hi[:, at], [P, GRP, NT], 2),
                            bc(k.iota[:, 0:NT], [P, GRP, NT], 1), ALU.is_equal).then_inc(ready, 1)

    def vector_last(v):
        v.wait_ge(used, NCH * NG + 1)
        for o in range(2):
            v.tensor_copy(counts[o][:, :], acc[o][:, 0:NT]).then_inc(counted, 1)

    def tensor_first(pe):
        pe.wait_ge(cleared, 2)
        for o in range(2):
            mm = pe.matmul(acc[o][:, 0:NT], oh_lo[o][:, 0, :], oh_lo[o][:, 1, 0:NT], start=True, stop=True,
                           skip_group_check=True)
        mm.then_inc(used, 1)

    def tensor(pe, i, q):
        pe.wait_ge(ready, (i * NG + q) * 4 + 4)
        for o in range(2):
            for g in range(GRP):
                mm = pe.matmul(acc[o][:, 0:NT], oh_lo[o][:, g, :], oh_hi[o][:, g, :], start=False, stop=True,
                               skip_group_check=True)
        mm.then_inc(used, 1)

    return Side(vector, tensor, 0, vector_first=vector_first, vector_last=vector_last, tensor_first=tensor_first,
                scalar=scalar)


class Side:

    def __init__(self, vector, tensor, steps, groups=NG, vector_first=None, vector_last=None, tensor_first=None,
                 scalar=None):
        none = lambda eng: None
        self.vector, self.tensor, self.steps, self.groups = vector, tensor, steps, groups
        self.vector_first, self.vector_last = vector_first or none, vector_last or none
        self.tensor_first, self.scalar = tensor_first or none, scalar or none

    def vector_groups(self, v, ch, i):
        v.nop(nofuse=True)
        with v.Fori(0, self.groups) as q:
            ch.enter(q, self.steps)
            self.vector(v, ch, i, q)
            ch.leave(self.groups, self.steps)

    def tensor_groups(self, pe, i):
        with pe.Fori(0, self.groups) as q:
            self.tensor(pe, i, q)


def gat_gather(k, name, table, F, heads, edges, maxes, carry, side):
    FX = F - heads
    with ExitStack() as st:
        c = Ctx(k.nc, st)
        G = [c.sb(f"{name}_G{b}", [P, CH, F]) for b in range(2)]
        S = [c.sb(f"{name}_S{b}", [P, CH, heads]) for b in range(2)]
        stage = [c.sb(f"{name}_stage{b}", [P, CH], I32) for b in range(2)]
        neg = c.sb(name + "_neg", [P, CH])
        side = side(k, c, name + "h")
        staged = [c.sem(f"{name}_staged{b}") for b in range(2)]
        got = [c.pool_dma_sem(f"{name}_got{b}") for b in range(2)]
        stored = [c.sem(f"{name}_stored{b}") for b in range(2)]
        scanned, step = c.sem(name + "_scanned"), c.sem(name + "_step")
        with k.nc.Block() as block:
            @block.gpsimd
            def _(g):
                over_chunks(g, lambda i, b, j: gather_column_loop(
                    g, k, i, j, b, table, G, stage, staged, stored, 32, got, k.src_i))

            @block.vector
            def _(v):
                ch = Chain(v, step)
                ch(v.memset(carry[:, 0:heads], -BIG))
                side.vector_first(v)

                def chunk(i, b, j):
                    side.vector_groups(v, ch, i)
                    v.wait_ge(stored[b], (j + 1) * 32)
                    ch(v.tensor_scalar(neg[:, :], k.keep_d[:, cols(i)], 1.0, BIG, ALU.subtract, ALU.mult))
                    v.wait_ge(got[b], (j + 1) * (16 * CH))
                    for h in range(heads):
                        ch.loose(v.tensor_tensor_scan(S[b][:, :, h], neg[:, :], G[b][:, :, FX + h],
                                                      carry[:, h:h + 1], ALU.add, ALU.max))
                    ch.wait()
                    v.tensor_copy(carry[:, 0:heads], S[b][:, CH - 1, :]).then_inc(scanned, 1)
                    v.wait_ge(scanned, i + 1)
                over_chunks(v, chunk, ch, 1 + heads + side.groups * side.steps)
                side.vector_last(v)

            @block.tensor
            def _(pe):
                side.tensor_first(pe)
                over_chunks(pe, lambda i, b, j: side.tensor_groups(pe, i))

            @block.scalar
            def _(a):
                side.scalar(a)

            @block.sync
            def _(s):
                for b in range(2):
                    s.sem_inc(stored[b], 32)

                def chunk(i, b, j):
                    s.wait_ge(scanned, i + 1)
                    s.dma_start(edges.rearrange("p (c f) -> p c f", f=F)[:, cols(i), :],
                                G[b][:, :, :]).then_inc(stored[b], 16)
                    s.dma_start(rows(maxes)[:, cols(i), :], S[b][:, :, :]).then_inc(stored[b], 16)
                over_chunks(s, chunk)
                s.wait_ge(stored[0], 32 * (PAIRS + 2))
                s.wait_ge(stored[1], 32 * (PAIRS + 1))


def gat_weigh(k, name, F, heads, edges, scans, first, carry):
    FX = F - heads
    FO = heads * FX + heads
    with ExitStack() as st:
        c = Ctx(k.nc, st)
        G = [c.sb(f"{name}_G{b}", [P, CH, F]) for b in range(2)]
        X = [c.sb(f"{name}_X{b}", [P, CH, 2 * heads]) for b in range(2)]
        W = [c.sb(f"{name}_W{b}", [P, CH, FO]) for b in range(2)]
        begin = c.sb(name + "_begin", [P, CH])
        e1 = c.sb(name + "_e1", [P, CH, heads])
        loaded = [c.sem(f"{name}_loaded{b}") for b in range(2)]
        stored = [c.sem(f"{name}_stored{b}") for b in range(2)]
        scanned, step, logits, probs = (c.sem(name + s) for s in ("_scanned", "_step", "_logits", "_probs"))
        with k.nc.Block() as block:
            @block.sync
            def _(s):
                for b in range(2):
                    s.sem_inc(stored[b], 16)

                def load(i, b):
                    s.dma_start(G[b][:, :, :],
                                edges.rearrange("p (c f) -> p c f", f=F)[:, cols(i), :]).then_inc(loaded[b], 16)
                    s.dma_start(X[b][:, :, :],
                                rows(table_view(k, 2 * heads, E))[:, cols(i), :]).then_inc(loaded[b], 16)

                def chunk(i, b, j, more):
                    s.wait_ge(scanned, i + 1)
                    s.dma_start(rows(scans)[:, cols(i), :], W[b][:, :, :]).then_inc(stored[b], 16)
                    if more:
                        load(i + 2, b)
                load(0, 0)
                load(1, 1)
                with s.Fori(0, PAIRS - 1) as j:
                    chunk(2 * j, 0, j, True)
                    chunk(2 * j + 1, 1, j, True)
                chunk(NCH - 3, 0, PAIRS - 1, True)
                chunk(NCH - 2, 1, PAIRS - 1, False)
                chunk(NCH - 1, 0, PAIRS, False)
                s.wait_ge(stored[0], 16 * (PAIRS + 2))
                s.wait_ge(stored[1], 16 * (PAIRS + 1))

            @block.vector
            def _(v):
                ch = Chain(v, step)
                ch(v.memset(carry[:, 0:FO], 0.0))

                def chunk(i, b, j):
                    keep = k.keep_d[:, cols(i)]
                    v.wait_ge(loaded[b], (j + 1) * 32)
                    ch(v.tensor_scalar(begin[:, :], keep, -1.0, 1.0, ALU.mult, ALU.add))
                    ch(v.tensor_tensor(X[b][:, :, :], X[b][:, :, :], bc(begin[:, :], [P, CH, 2 * heads], 2),
                                       ALU.mult))
                    scan_chunk(v, ch, X[b], keep, first, 2 * heads)
                    ch(v.tensor_tensor(e1[:, :, :], G[b][:, :, FX:F], X[b][:, :, 0:heads], ALU.add))
                    ch(v.scalar_tensor_tensor(out=e1[:, :, :], in0=e1[:, :, :], scalar=0.2, in1=e1[:, :, :],
                                              op0=ALU.mult, op1=ALU.max))
                    v.wait_ge(stored[b], (j + 1) * 16)
                    v.tensor_tensor(W[b][:, :, heads * FX:FO], e1[:, :, :], X[b][:, :, heads:2 * heads],
                                    ALU.subtract).then_inc(logits, 1)
                    v.wait_ge(probs, i + 1)
                    for h in range(heads):
                        ch.loose(v.tensor_tensor(W[b][:, :, h * FX:(h + 1) * FX], G[b][:, :, 0:FX],
                                                 bc(W[b][:, :, heads * FX + h], [P, CH, FX], 2), ALU.mult))
                    ch.wait()
                    for f in range(FO):
                        ch.loose(v.tensor_tensor_scan(W[b][:, :, f], keep, W[b][:, :, f], carry[:, f:f + 1],
                                                      ALU.mult, ALU.add))
                    ch.wait()
                    v.tensor_copy(carry[:, 0:FO], W[b][:, CH - 1, :]).then_inc(scanned, 1)
                    v.wait_ge(scanned, i + 1)
                over_chunks(v, chunk, ch, 5 + 3 * heads + FO)

            @block.scalar
            def _(a):
                def chunk(i, b, j):
                    a.wait_ge(logits, i + 1)
                    a.activation(W[b][:, :, heads * FX:FO], W[b][:, :, heads * FX:FO], ACT.Exp).then_inc(probs, 1)
                over_chunks(a, chunk)


def gcn_gather(k, name, table, scans, carry, side):
    with ExitStack() as st:
        c = Ctx(k.nc, st)
        G = [c.sb(f"{name}_G{b}", [P, CH, D]) for b in range(2)]
        stage = [c.sb(f"{name}_stage{b}", [P, CH], I32) for b in range(2)]
        staged = [c.sem(f"{name}_staged{b}") for b in range(2)]
        got = [c.pool_dma_sem(f"{name}_got{b}") for b in range(2)]
        stored = [c.sem(f"{name}_stored{b}") for b in range(2)]
        scanned, step = c.sem(name + "_scanned"), c.sem(name + "_step")
        side = side(k, c, name + "h")
        with k.nc.Block() as block:
            @block.gpsimd
            def _(g):
                over_chunks(g, lambda i, b, j: gather_column_loop(
                    g, k, i, j, b, table, G, stage, staged, stored, 16, got, k.src_i))

            @block.vector
            def _(v):
                ch = Chain(v, step)
                ch(v.memset(carry[:, 0:D], 0.0))
                side.vector_first(v)

                def chunk(i, b, j):
                    side.vector_groups(v, ch, i)
                    v.wait_ge(got[b], (j + 1) * (16 * CH))
                    for f in range(D):
                        ch.loose(v.tensor_tensor_scan(G[b][:, :, f], k.keep_d[:, cols(i)], G[b][:, :, f],
                                                      carry[:, f:f + 1], ALU.mult, ALU.add))
                    ch.wait()
                    v.tensor_copy(carry[:, 0:D], G[b][:, CH - 1, :]).then_inc(scanned, 1)
                    v.wait_ge(scanned, i + 1)
                over_chunks(v, chunk, ch, D + side.groups * side.steps)
                side.vector_last(v)

            @block.tensor
            def _(pe):
                side.tensor_first(pe)
                over_chunks(pe, lambda i, b, j: side.tensor_groups(pe, i))

            @block.scalar
            def _(a):
                side.scalar(a)

            @block.sync
            def _(s):
                for b in range(2):
                    s.sem_inc(stored[b], 16)

                def chunk(i, b, j):
                    s.wait_ge(scanned, i + 1)
                    s.dma_start(rows(scans)[:, cols(i), :], G[b][:, :, :]).then_inc(stored[b], 16)
                over_chunks(s, chunk)
                s.wait_ge(stored[0], 16 * (PAIRS + 2))
                s.wait_ge(stored[1], 16 * (PAIRS + 1))


def count_in_group(k, c, name):
    pB = c.ps(name + "_pB", [P, 1024])
    junk = [c.sb(f"{name}_junk{g}", [P, (g + 1) * P]) for g in range(GRP)]
    src_f = c.sb(name + "_src_f", [P, GRP])
    rowed, used = c.sem(name + "_rowed"), c.sem(name + "_used")

    def vector(v, ch, i, q):
        at = bass.ds(i * CH + q * GRP, GRP)
        ch(v.tensor_copy(src_f[:, :], k.src_i[:, at]))
        v.wait_ge(rowed, i * NG + q + 1)
        for g in range(GRP):
            ins = v.scalar_tensor_tensor(out=junk[g][:, :], in0=pB[:, 0:(g + 1) * P],
                                         scalar=src_f[:, g:g + 1], in1=k.earlier[:, (GRP - 1 - g) * P:],
                                         op0=ALU.is_equal, op1=ALU.mult, accum_out=k.cnt5[:, g:g + 1])
            ch.loose(ins)
        ch.wait()
        v.tensor_copy(k.cnt[:, at], k.cnt5[:, :]).then_inc(used, 1)
        v.wait_ge(used, i * NG + q + 2)

    def tensor(pe, i, q):
        pe.wait_ge(used, i * NG + q + 1)
        for g in range(GRP):
            at = bass.ds(i * CH + q * GRP + g, 1)
            pe.matmul(pB[:, g * P:(g + 1) * P], k.src_lo[:, at].to_broadcast([P, P]), k.ident_b[:, :],
                      start=True, stop=False)
            mm = pe.matmul(pB[:, g * P:(g + 1) * P], k.src_hi[:, at].to_broadcast([P, P]), k.ident128_b[:, :],
                           start=False, stop=True)
        mm.then_inc(rowed, 1)

    return Side(vector, tensor, 1 + GRP, tensor_first=lambda pe: pe.sem_inc(used, 1))


def count_before_group(k, c, name, q0, groups, table_in):
    pB = c.ps(name + "_pB", [P, 1024])
    pT = c.ps(name + "_pT", [P, 512])
    pR = c.ps(name + "_pR", [P, 512])
    table = k.free_place
    oh_lo = c.sb(name + "_oh_lo", [P, GRP, P], BF16)
    oh_hi = c.sb(name + "_oh_hi", [P, GRP, NT], BF16)
    loT = c.sb(name + "_loT", [P, GRP, P])
    prod = c.sb(name + "_prod", [P, GRP, NT])
    r5 = c.sb(name + "_r5", [P, GRP])
    rowed, hot, hotT, looked, added, copied, ranked = (
        c.sem(name + s) for s in ("_rowed", "_hot", "_hotT", "_looked", "_added", "_copied", "_ranked"))

    def vector(v, ch, i, q):
        n = i * groups + q
        at = bass.ds(i * CH + q * GRP + q0 * GRP, GRP)
        v.wait_ge(added, n + 1)
        v.tensor_tensor(oh_lo[:, :, :], bc(k.src_lo[:, at], [P, GRP, P], 2), bc(k.iota[:, :], [P, GRP, P], 1),
                        ALU.is_equal).then_inc(hot, 1)
        ch(v.tensor_tensor(oh_hi[:, :, :], bc(k.src_hi[:, at], [P, GRP, NT], 2),
                           bc(k.iota[:, 0:NT], [P, GRP, NT], 1), ALU.is_equal))
        v.wait_ge(rowed, n + 1)
        v.tensor_scalar(loT[:, :, :], pB[:, 0:GRP * P].rearrange("p (g q) -> p g q", g=GRP), k.part[:, 0:1], None,
                        ALU.is_equal).then_inc(hotT, 1)
        v.wait_ge(looked, n + 1)
        ch(v.tensor_tensor(prod[:, :, :], pR[:, 0:GRP * NT].rearrange("p (g t) -> p g t", g=GRP), oh_hi[:, :, :],
                           ALU.mult))
        ch(v.tensor_reduce(r5[:, :], prod[:, :, :], axis=AX.X, op=ALU.add))
        v.tensor_tensor(k.rank[:, at], r5[:, :], k.cnt[:, at], ALU.add).then_inc(ranked, 1)
        v.wait_ge(ranked, n + 1)

    def tensor_first(pe):
        pe.matmul(pT[:, 0:NT], k.ident[:, :], table_in[:, :], start=True, stop=True,
                  skip_group_check=True).then_inc(added, 1)

    def tensor(pe, i, q):
        n = i * groups + q
        for g in range(GRP):
            at = bass.ds(i * CH + q * GRP + (q0 * GRP + g), 1)
            mm = pe.matmul(pB[:, g * P:(g + 1) * P], k.src_lo[:, at].to_broadcast([P, P]), k.ident_b[:, :],
                           start=True, stop=True)
        mm.then_inc(rowed, 1)
        pe.wait_ge(hotT, n + 1)
        pe.wait_ge(copied, n + 1)
        for g in range(GRP):
            mm = pe.matmul(pR[:, g * NT:(g + 1) * NT], loT[:, g, :], table[:, :], start=True, stop=True)
        mm.then_inc(looked, 1)
        for g in range(GRP):
            mm = pe.matmul(pT[:, 0:NT], oh_lo[:, g, :], oh_hi[:, g, :], start=False, stop=True,
                           skip_group_check=True)
        mm.then_inc(added, 1)

    def scalar(a):
        with a.Fori(0, NCH * groups + 1) as n:
            a.wait_ge(added, n + 1)
            a.activation(table[:, :], pT[:, 0:NT], ACT.Copy).then_inc(copied, 1)

    return Side(vector, tensor, 3, groups, tensor_first=tensor_first, scalar=scalar)


def scatter_column_loop(g, k, i, j, b, view, M, stage, staged, ready, sent, parts=1):
    g.tensor_copy(stage[b][:, :], k.rank[:, cols(i)]).then_inc(staged[b], 1)
    g.wait_ge(staged[b], j + 1)
    for t in range(CH):
        if t % (CH // parts) == 0:
            g.wait_ge(ready, i * parts + (t // (CH // parts) + 1))
            g.nop(nofuse=True)
        g.indirect_dma_start(out=view, in_=M[b][:, t, :], in_offset=None,
                             out_offset=bass.IndirectOffsetOnAxis(ap=stage[b][:, t:t + 1], axis=0)
                             ).then_inc(sent[b], 16)


def release_messages(g, b, j, sent, mfree):
    g.wait_ge(sent[b], (j + 1) * (16 * CH))
    g.nop(nofuse=True).then_inc(mfree[b], 1)


def sheaf_edges(k, name, table, scans, messages, first, carry, w1, b1, w2, b2):
    F = D + 1
    with ExitStack() as st:
        c = Ctx(k.nc, st)
        G = [c.sb(f"{name}_G{b}", [P, CH, F]) for b in range(2)]
        X = [c.sb(f"{name}_X{b}", [P, CH, F]) for b in range(2)]
        M = [c.sb(f"{name}_M{b}", [P, CH, F]) for b in range(2)]
        O = [c.sb(f"{name}_O{b}", [P, CH, D]) for b in range(2)]
        stage = [c.sb(f"{name}_stage{b}", [P, CH], I32) for b in range(2)]
        rstage = [c.sb(f"{name}_rstage{b}", [P, CH], I32) for b in range(2)]
        V = c.sb(name + "_V", [P, CH, 2, D])
        T = c.sb(name + "_T", [P, CH, 2, D])
        nrm = c.sb(name + "_nrm", [P, CH, 2])
        dot = c.sb(name + "_dot", [P, CH])
        begin = c.sb(name + "_begin", [P, CH])
        pair = c.sb(name + "_pair", [P, GRP, 2, D])
        pairT = c.sb(name + "_pairT", [2 * D, 2, GRP * P // 2])
        hid = c.sb(name + "_hid", [P, 2, GRP * P // 2])
        pT = c.ps(name + "_pT", [2 * D, 1024])
        pH = c.ps(name + "_pH", [P, 2, 512])
        pV = c.ps(name + "_pV", [P, 512])
        staged = [c.sem(f"{name}_staged{b}") for b in range(2)]
        rstaged = [c.sem(f"{name}_rstaged{b}") for b in range(2)]
        got = [c.pool_dma_sem(f"{name}_got{b}") for b in range(2)]
        free = [c.sem(f"{name}_free{b}") for b in range(2)]
        sent = [c.pool_dma_sem(f"{name}_sent{b}") for b in range(2)]
        mfree = [c.sem(f"{name}_mfree{b}") for b in range(2)]
        loaded = [c.sem(f"{name}_loaded{b}") for b in range(2)]
        stored = [c.sem(f"{name}_stored{b}") for b in range(2)]
        messaged, scanned, step, paired, transposed, copied, hidden, relued, vectored, evacuated = (
            c.sem(name + s) for s in ("_messaged", "_scanned", "_step", "_paired", "_transposed", "_copied",
                                      "_hidden", "_relued", "_vectored", "_evacuated"))
        HALF = GRP * P // 2
        with k.nc.Block() as block:
            @block.gpsimd
            def _(g):
                def gather(i, b, j):
                    gather_column_loop(g, k, i, j, b, table, G, stage, staged, free, 1, got, k.src_i)

                def scatter(i, b, j):
                    scatter_column_loop(g, k, i, j, b, messages, M, rstage, rstaged, messaged, sent)
                for b in range(2):
                    g.sem_inc(mfree[b], 1)
                gather(0, 0, 0)
                with g.Fori(0, PAIRS) as j:
                    gather(2 * j + 1, 1, j)
                    scatter(2 * j, 0, j)
                    gather(2 * j + 2, 0, j + 1)
                    release_messages(g, 0, j, sent, mfree)
                    scatter(2 * j + 1, 1, j)
                    release_messages(g, 1, j, sent, mfree)
                scatter(NCH - 1, 0, PAIRS)
                g.wait_ge(sent[0], 16 * CH * (PAIRS + 1))

            @block.vector
            def _(v):
                for b in range(2):
                    v.sem_inc(free[b], 1)
                ch = Chain(v, step)
                ch(v.memset(carry[:, 0:D], 0.0))

                def reflect(out, y, n):
                    vec, tmp = V[:, :, n, :], T[:, :, 1, :]
                    ch(v.tensor_tensor(tmp, y, vec, ALU.mult))
                    ch(v.tensor_reduce(dot[:, :], tmp, axis=AX.X, op=ALU.add))
                    ch(v.tensor_tensor(dot[:, :], dot[:, :], nrm[:, :, n], ALU.mult))
                    ch(v.tensor_tensor(tmp, vec, bc(dot[:, :], [P, CH, D], 2), ALU.mult))
                    ch(v.tensor_tensor(out, y, tmp, ALU.subtract))

                def chunk(i, b, j):
                    keep = k.keep_d[:, cols(i)]
                    v.wait_ge(loaded[b], (j + 1) * 16)
                    ch(v.tensor_scalar(begin[:, :], keep, -1.0, 1.0, ALU.mult, ALU.add))
                    ch(v.tensor_tensor(X[b][:, :, :], X[b][:, :, :], bc(begin[:, :], [P, CH, F], 2), ALU.mult))
                    scan_chunk(v, ch, X[b], keep, first, F)
                    v.wait_ge(got[b], (j + 1) * (16 * CH))

                    def pair_group(q):
                        at = bass.ds(q * GRP, GRP)
                        ch(v.tensor_copy(pair[:, :, 0, :], G[b][:, at, 0:D]))
                        v.tensor_copy(pair[:, :, 1, :], X[b][:, at, 0:D]).then_inc(paired, 1)

                    def evacuate(q):
                        v.wait_ge(vectored, i * NG + q + 1)
                        v.tensor_tensor(V[:, bass.ds(q * GRP, GRP), :, :].rearrange("p c n d -> p c (n d)"),
                                        pV[:, 0:GRP * 2 * D].rearrange("p (c n) -> p c n", c=GRP),
                                        bc(b2[:, :], [P, GRP, 2 * D], 1), ALU.add).then_inc(evacuated, 1)
                    pair_group(0)
                    with v.Fori(0, NG - 1) as q:
                        ch.enter(q, 1)
                        v.wait_ge(transposed, i * NG + q + 1)
                        pair_group(q + 1)
                        evacuate(q)
                        ch.leave(NG - 1, 1)
                    evacuate(NG - 1)
                    v.wait_ge(evacuated, (i + 1) * NG)
                    ch(v.tensor_tensor(T[:, :, :, :], V[:, :, :, :], V[:, :, :, :], ALU.mult))
                    ch(v.tensor_reduce(nrm[:, :, :], T[:, :, :, :], axis=AX.X, op=ALU.add))
                    ch(v.tensor_scalar(nrm[:, :, :], nrm[:, :, :], 1e-24, None, ALU.max))
                    ch(v.reciprocal(nrm[:, :, :], nrm[:, :, :]))
                    ch(v.tensor_scalar(nrm[:, :, :], nrm[:, :, :], 2.0, None, ALU.mult))
                    A = T[:, :, 0, :]
                    v.wait_ge(mfree[b], j + 1)
                    reflect(A, X[b][:, :, 0:D], 1)
                    reflect(A, A, 0)
                    ch(v.tensor_tensor(M[b][:, :, 0:D], A, bc(X[b][:, :, D], [P, CH, D], 2), ALU.mult))
                    v.tensor_copy(M[b][:, :, D], k.src_i[:, cols(i)]).then_inc(messaged, 1)
                    v.wait_ge(stored[b], (j + 1) * 16)
                    reflect(A, G[b][:, :, 0:D], 0)
                    reflect(A, A, 1)
                    v.tensor_tensor(O[b][:, :, :], A, bc(G[b][:, :, D], [P, CH, D], 2),
                                    ALU.mult).then_inc(free[b], 1)
                    v.wait_ge(free[b], j + 2)
                    for f in range(D):
                        ch.loose(v.tensor_tensor_scan(O[b][:, :, f], keep, O[b][:, :, f], carry[:, f:f + 1],
                                                      ALU.mult, ALU.add))
                    ch.wait()
                    v.tensor_copy(carry[:, 0:D], O[b][:, CH - 1, :]).then_inc(scanned, 1)
                    v.wait_ge(scanned, i + 1)
                over_chunks(v, chunk, ch, 2 + F + 1 + NG + 5 + 20 + 1 + D)

            @block.tensor
            def _(pe):
                def chunk(i, b, j):
                    def transpose(n):
                        pe.wait_ge(paired, n + 1)
                        pe.nop(nofuse=True)
                        for g in range(GRP):
                            mm = pe.transpose(pT[:, g * P:(g + 1) * P],
                                              pair[:, g, :, :].rearrange("p n d -> p (n d)"), k.ident[:, :])
                        mm.then_inc(transposed, 1)

                    def hidden_layer(n):
                        pe.wait_ge(copied, n + 1)
                        for h in range(2):
                            mm = pe.matmul(pH[:, h, 0:HALF], w1[:, :], pairT[:, h, :], start=True, stop=True)
                        mm.then_inc(hidden, 1)

                    def vectors(n):
                        pe.wait_ge(relued, n + 1)
                        flat = hid[:, :, :].rearrange("p a q -> p (a q)")
                        for g in range(GRP):
                            mm = pe.matmul(pV[:, g * 2 * D:(g + 1) * 2 * D], flat[:, g * P:(g + 1) * P], w2[:, :],
                                           start=True, stop=True)
                        mm.then_inc(vectored, 1)
                    transpose(i * NG)
                    with pe.Fori(0, NG - 1) as q:
                        hidden_layer(i * NG + q)
                        transpose(i * NG + q + 1)
                        vectors(i * NG + q)
                    hidden_layer(i * NG + (NG - 1))
                    pe.wait_ge(evacuated, i * NG + (NG - 1))
                    vectors(i * NG + (NG - 1))
                over_chunks(pe, chunk)

            @block.scalar
            def _(a):
                def copy(n):
                    a.wait_ge(transposed, n + 1)
                    a.activation(pairT[:, :, :].rearrange("p a q -> p (a q)"), pT[:, 0:GRP * P],
                                 ACT.Copy).then_inc(copied, 1)

                def relu(n):
                    a.wait_ge(hidden, n + 1)
                    a.activation(hid[:, :, :], pH[:, :, 0:HALF], ACT.Relu, bias=b1[:, 0:1]).then_inc(relued, 1)

                def chunk(i, b, j):
                    copy(i * NG)
                    with a.Fori(0, NG - 1) as q:
                        relu(i * NG + q)
                        copy(i * NG + q + 1)
                    relu(i * NG + (NG - 1))
                over_chunks(a, chunk)

            @block.sync
            def _(s):
                for b in range(2):
                    s.sem_inc(stored[b], 16)

                def load(i, b):
                    s.dma_start(X[b][:, :, :], rows(table_view(k, F, E))[:, cols(i), :]).then_inc(loaded[b], 16)

                def chunk(i, b, j, more):
                    s.wait_ge(scanned, i + 1)
                    s.dma_start(rows(scans)[:, cols(i), :], O[b][:, :, :]).then_inc(stored[b], 16)
                    if more:
                        load(i + 2, b)
                load(0, 0)
                load(1, 1)
                with s.Fori(0, PAIRS - 1) as j:
                    chunk(2 * j, 0, j, True)
                    chunk(2 * j + 1, 1, j, True)
                chunk(NCH - 3, 0, PAIRS - 1, True)
                chunk(NCH - 2, 1, PAIRS - 1, False)
                chunk(NCH - 1, 0, PAIRS, False)
                s.wait_ge(stored[0], 16 * (PAIRS + 2))
                s.wait_ge(stored[1], 16 * (PAIRS + 1))


def src_order_scan(k, name, messages, scans, carry, F, find_keep):
    with ExitStack() as st:
        c = Ctx(k.nc, st)
        G = [c.sb(f"{name}_G{b}", [P, CH, F]) for b in range(2)]
        O = [c.sb(f"{name}_O{b}", [P, CH, D]) for b in range(2)]
        prev = c.sb(name + "_prev", [P, 1])
        loaded = [c.sem(f"{name}_loaded{b}") for b in range(2)]
        stored = [c.sem(f"{name}_stored{b}") for b in range(2)]
        cleared, scanned, step, prevd, whole = (
            c.sem(name + s) for s in ("_cleared", "_scanned", "_step", "_prevd", "_whole"))
        extra = 3 if find_keep else 0
        with k.nc.Block() as block:
            @block.sync
            def _(s):
                for b in range(2):
                    s.sem_inc(stored[b], 16)
                if find_keep:
                    s.wait_ge(cleared, 1)
                    with k.nc.allow_non_contiguous_dma("one value of each lane"):
                        s.dma_start(prev[1:P, :], rows(messages)[0:P - 1, LANE - 1, D:D + 1]).then_inc(prevd, 16)

                def load(i, b):
                    s.dma_start(G[b][:, :, :], rows(messages)[:, cols(i), :]).then_inc(loaded[b], 16)

                def chunk(i, b, j, more):
                    s.wait_ge(scanned, i + 1)
                    s.dma_start(rows(scans)[:, cols(i), :], O[b][:, :, :]).then_inc(stored[b], 16)
                    if more:
                        load(i + 2, b)
                load(0, 0)
                load(1, 1)
                with s.Fori(0, PAIRS - 1) as j:
                    chunk(2 * j, 0, j, True)
                    chunk(2 * j + 1, 1, j, True)
                chunk(NCH - 3, 0, PAIRS - 1, True)
                chunk(NCH - 2, 1, PAIRS - 1, False)
                chunk(NCH - 1, 0, PAIRS, False)
                if find_keep:
                    s.wait_ge(whole, 1)
                    s.dma_start(k.by_src["whole_row"].rearrange("a p -> p a"), k.whole[:, :]).then_inc(whole, 16)
                    s.wait_ge(whole, 17)
                s.wait_ge(stored[0], 16 * (PAIRS + 2))
                s.wait_ge(stored[1], 16 * (PAIRS + 1))

            @block.vector
            def _(v):
                ch = Chain(v, step)
                ch(v.memset(carry[:, 0:D], 0.0))
                if find_keep:
                    v.memset(prev[:, :], -1.0).then_inc(cleared, 1)
                    v.wait_ge(prevd, 16)

                def chunk(i, b, j):
                    v.wait_ge(loaded[b], (j + 1) * 16)
                    if find_keep:
                        ids = G[b][:, :, D]
                        ch(v.tensor_tensor(k.keep_s[:, bass.ds(i * CH, 1)], ids[:, 0:1], prev[:, :], ALU.is_equal))
                        ch(v.tensor_tensor(k.keep_s[:, bass.ds(i * CH + 1, CH - 1)], ids[:, 1:CH], ids[:, 0:CH - 1],
                                           ALU.is_equal))
                        ch(v.tensor_copy(prev[:, :], ids[:, CH - 1:CH]))
                    v.wait_ge(stored[b], (j + 1) * 16)
                    for f in range(D):
                        ch.loose(v.tensor_tensor_scan(O[b][:, :, f], k.keep_s[:, cols(i)], G[b][:, :, f],
                                                      carry[:, f:f + 1], ALU.mult, ALU.add))
                    ch.wait()
                    v.tensor_copy(carry[:, 0:D], O[b][:, CH - 1, :]).then_inc(scanned, 1)
                    v.wait_ge(scanned, i + 1)
                over_chunks(v, chunk, ch, D + extra)
                if find_keep:
                    v.tensor_reduce(k.whole[:, :], k.keep_s[:, :], axis=AX.X, op=ALU.min).then_inc(whole, 1)


def product_edges(k, name, attr, messages, first, w):
    with ExitStack() as st:
        c = Ctx(k.nc, st)
        X = [c.sb(f"{name}_X{b}", [P, CH, D]) for b in range(2)]
        A = [c.sb(f"{name}_A{b}", [P, CH, DE]) for b in range(2)]
        M = [c.sb(f"{name}_M{b}", [P, CH, D]) for b in range(2)]
        rstage = [c.sb(f"{name}_rstage{b}", [P, CH], I32) for b in range(2)]
        begin = c.sb(name + "_begin", [P, CH])
        outer = c.sb(name + "_outer", [P, GRP, D, DE])
        outT = c.sb(name + "_outT", [P, GRP * P])
        pT = c.ps(name + "_pT", [P, 1024])
        pM = c.ps(name + "_pM", [P, 512])
        rstaged = [c.sem(f"{name}_rstaged{b}") for b in range(2)]
        sent = [c.pool_dma_sem(f"{name}_sent{b}") for b in range(2)]
        mfree = [c.sem(f"{name}_mfree{b}") for b in range(2)]
        loaded = [c.sem(f"{name}_loaded{b}") for b in range(2)]
        used, step, outered, transposed, copied, product, silued = (
            c.sem(name + s) for s in ("_used", "_step", "_outered", "_transposed", "_copied",
                                      "_product", "_silued"))
        norm = 1.0 / float(np.float32(np.sqrt(D * DE)))
        with k.nc.Block() as block:
            @block.gpsimd
            def _(g):
                for b in range(2):
                    g.sem_inc(mfree[b], 1)

                def scatter(i, b, j):
                    scatter_column_loop(g, k, i, j, b, messages, M, rstage, rstaged, silued, sent, NG)
                with g.Fori(0, PAIRS) as j:
                    scatter(2 * j, 0, j)
                    release_messages(g, 0, j, sent, mfree)
                    scatter(2 * j + 1, 1, j)
                    release_messages(g, 1, j, sent, mfree)
                scatter(NCH - 1, 0, PAIRS)
                g.wait_ge(sent[0], 16 * CH * (PAIRS + 1))

            @block.vector
            def _(v):
                ch = Chain(v, step)
                ch(v.memset(begin[:, :], 0.0))

                def chunk(i, b, j):
                    keep = k.keep_d[:, cols(i)]
                    v.wait_ge(loaded[b], (j + 1) * 32)
                    ch(v.tensor_scalar(begin[:, :], keep, -1.0, 1.0, ALU.mult, ALU.add))
                    ch(v.tensor_tensor(X[b][:, :, :], X[b][:, :, :], bc(begin[:, :], [P, CH, D], 2), ALU.mult))
                    scan_chunk(v, ch, X[b], keep, first, D)
                    v.nop(nofuse=True)
                    with v.Fori(0, NG) as q:
                        at = bass.ds(q * GRP, GRP)
                        v.wait_ge(transposed, i * NG + q + 1)
                        v.tensor_tensor(outer[:, :, :, :], bc(X[b][:, at, :], [P, GRP, D, DE], 3),
                                        bc(A[b][:, at, :], [P, GRP, D, DE], 2), ALU.mult).then_inc(outered, 1)
                    v.engine_nop().then_inc(used, 1)
                over_chunks(v, chunk, ch, 2 + D + 1)

            @block.tensor
            def _(pe):
                pe.sem_inc(transposed, 1)

                def chunk(i, b, j):
                    with pe.Fori(0, NG) as q:
                        n = i * NG + q
                        pe.wait_ge(outered, n + 1)
                        for g in range(GRP):
                            mm = pe.transpose(pT[:, g * P:(g + 1) * P],
                                              outer[:, g, :, :].rearrange("p i j -> p (i j)"), k.ident[:, :])
                        mm.then_inc(transposed, 1)
                        pe.wait_ge(copied, n + 1)
                        for g in range(GRP):
                            mm = pe.matmul(pM[:, g * D:(g + 1) * D], outT[:, g * P:(g + 1) * P], w[:, :],
                                           start=True, stop=True)
                        mm.then_inc(product, 1)
                over_chunks(pe, chunk)

            @block.scalar
            def _(a):
                def chunk(i, b, j):
                    a.wait_ge(mfree[b], j + 1)
                    a.nop(nofuse=True)
                    with a.Fori(0, NG) as q:
                        n = i * NG + q
                        a.wait_ge(transposed, n + 2)
                        a.activation(outT[:, :], pT[:, 0:GRP * P], ACT.Copy).then_inc(copied, 1)
                        a.wait_ge(product, n + 1)
                        a.activation(M[b][:, bass.ds(q * GRP, GRP), :],
                                     pM[:, 0:GRP * D].rearrange("p (g d) -> p g d", g=GRP), ACT.Silu,
                                     scale=norm).then_inc(silued, 1)
                over_chunks(a, chunk)

            @block.sync
            def _(s):
                def load(i, b):
                    s.dma_start(X[b][:, :, :], rows(table_view(k, D, E))[:, cols(i), :]).then_inc(loaded[b], 16)
                    s.dma_start(A[b][:, :, :], rows(attr)[:, cols(i), :]).then_inc(loaded[b], 16)

                def next_load(i, b):
                    s.wait_ge(used, i + 1)
                    load(i + 2, b)
                load(0, 0)
                load(1, 1)
                with s.Fori(0, PAIRS - 1) as j:
                    next_load(2 * j, 0)
                    next_load(2 * j + 1, 1)
                next_load(NCH - 3, 0)



def program(nc, x, src, dst, attr, w, out):
    with ExitStack() as st:
        k = Ctx(nc, st)
        k.src_i = k.sb("src_i", [P, LANE], I32)
        k.keep_d = k.sb("keep_d", [P, LANE])
        k.ident = k.sb("ident", [P, P])
        k.iota = k.sb("iota", [P, P])
        k.part = k.sb("part", [P, 1])
        k.before = k.sb("before", [P, P])
        k.ones = k.sb("ones", [P, P])
        k.ident_b = k.sb("ident_b", [P, P], BF16)
        k.ident128_b = k.sb("ident128_b", [P, P], BF16)
        k.earlier = k.sb("earlier", [P, GRP * P])
        k.node_mask = k.sb("node_mask", [P, NT])
        k.whole = k.sb("whole", [P, 1])
        k.first_dst = k.sb("first_dst", [P, 1], I32)
        k.cnt5 = k.sb("cnt5", [P, GRP])
        k.x = k.sb("x", [P, NT, D])
        y = k.sb("y", [P, NT, D])
        carry = k.sb("carry", [P, 51])
        first = k.sb("first", [P, SPREAD_F])
        k.by_dst = new_order(k, "by_dst")
        k.by_src = new_order(k, "by_src")
        k.lanes = k.dram("lanes", [P, 51])
        k.spread_buf = k.dram("spread_buf", [SPREAD_SIZE])
        scan16 = k.dram("scan16", [E + P, D])
        k.carried = k.dram("carried", [P + 1, 51])
        tab16 = k.dram("tab16", [NP, D])
        tab16b = k.dram("tab16b", [NP, D])
        messages = k.dram("messages", [E, D + 1])
        messages2 = k.dram("messages2", [E, D])

        k.rank = k.sb("rank", [P, LANE], I32)
        k.keep_s = k.sb("keep_s", [P, LANE])
        with ExitStack() as s12:
            c = Ctx(nc, s12)
            k.h2 = c.sb("h2", [P, NT, C2 + 2])
            k.src_lo, k.src_hi = (c.sb(n, [P, LANE], BF16) for n in ("src_lo", "src_hi"))
            with ExitStack() as s0:
                k.dst_i = Ctx(nc, s0).sb("dst_i", [P, LANE], I32)
                setup(k, x, src, dst)
                digits(k, "ds", k.src_i, k.src_lo, k.src_hi)
            gat1(k, w, dst, carry, first, y)
            with ExitStack() as s2:
                k.cnt = Ctx(nc, s2).sb("cnt", [P, LANE])
                gat2(k, w, carry, first, y)
                gcn(k, w, carry, y, scan16, tab16, tab16b)
        sheaf(k, w, carry, first, y, scan16, messages)
        product(k, w, carry, first, y, scan16, messages2, attr)

        stored = k.sem("out_stored")
        with nc.Block() as block:
            @block.sync
            def _(s):
                s.dma_start(out[0:FULL * P, :].rearrange("(t p) f -> p t f", p=P),
                            k.x[:, 0:FULL, :]).then_inc(stored, 16)
                s.dma_start(out[FULL * P:N, :], k.x[0:REST, FULL, :]).then_inc(stored, 16)
                s.wait_ge(stored, 32)


def load_small(k, name, copies):
    with ExitStack() as st:
        loaded = Ctx(k.nc, st).sem(name + "_loaded")
        with k.nc.Block() as block:
            @block.sync
            def _(s):
                with k.nc.allow_non_contiguous_dma("small weights"):
                    for dst, src in copies:
                        s.dma_start(dst, src).then_inc(loaded, 16)
                s.wait_ge(loaded, 16 * len(copies))


def row_bc(ap, n=P):
    return ap.rearrange("(a f) -> a f", a=1).to_broadcast([n, ap.shape[0]])


def gat1(k, w, dst, carry, first, y):
    nc = k.nc
    F = D + H1
    edges = k.dram("edges1", [P, LANE * F])
    maxes, scans = k.dram("maxes1", [E + P, H1]), k.dram("scans1", [E + P, H1 * D + H1])
    tab, stab = k.dram("tab1", [NP, F]), k.dram("stab1", [NP, 2 * H1])
    h2 = k.h2
    with ExitStack() as st:
        c = Ctx(nc, st)
        w1 = c.sb("g1_w1", [D, H1 * C1])
        a1 = c.sb("g1_a1", [D, 2, H1 * C1])
        wa = c.sb("g1_wa", [D, 2, H1])
        w1d = c.sb("g1_w1d", [H1 * D, H1 * C1])
        b1 = c.sb("g1_b1", [P, H1 * C1])
        w2 = c.sb("g1_w2", [H1 * C1, C2 + 2])
        a2 = c.sb("g1_a2", [H1 * C1, 2, C2])
        t2 = c.sb("g1_t2", [H1 * C1, 2, C2])
        al = c.sb("g1_al", [P, NT, 2 * H1])
        sv = c.sb("g1_sv", [P, NT, 2 * H1])
        pself = c.sb("g1_pself", [P, NT, H1])
        vector_block(k, "g1z", lambda v, ch: ch(v.memset(w1d[:, :], 0.0)))
        load_small(k, "g1l", [
            (w1[:, :], w["L0_gnn_W1"]),
            (a1[:, 0, :], row_bc(w["L0_gnn_a_src1"].rearrange("h c -> (h c)"), D)),
            (a1[:, 1, :], row_bc(w["L0_gnn_a_dst1"].rearrange("h c -> (h c)"), D)),
            (b1[:, :], row_bc(w["L0_gnn_b1"])),
            (w2[:, 0:C2], w["L0_gnn_W2"]),
            (a2[:, 0, :], row_bc(w["L0_gnn_a_src2"].rearrange("h c -> (h c)"), H1 * C1)),
            (a2[:, 1, :], row_bc(w["L0_gnn_a_dst2"].rearrange("h c -> (h c)"), H1 * C1)),
        ] + [(w1d[D * h:D * h + D, C1 * h:C1 * h + C1], w["L0_gnn_W1"][:, C1 * h:C1 * h + C1]) for h in range(H1)])

        def fold(v, ch):
            for s in range(2):
                ch(v.tensor_tensor(a1[:, s, :], a1[:, s, :], w1[:, :], ALU.mult))
                ch(v.tensor_reduce(wa[:, s, :], a1[:, s, :].rearrange("p (h c) -> p h c", h=H1), axis=AX.X,
                                   op=ALU.add))
                ch(v.tensor_tensor(t2[:, s, :], a2[:, s, :], w2[:, 0:C2], ALU.mult))
                ch(v.tensor_reduce(w2[:, C2 + s:C2 + s + 1], t2[:, s, :], axis=AX.X, op=ALU.add))
        vector_block(k, "g1f", fold)
        node_linear(k, "g1a", k.x, wa[:, :, :].rearrange("p s h -> p (s h)"), al, D, 2 * H1)
        store_nodes(k, "g1t", [k.x[:, :, :], al[:, :, 0:H1]], tab)
        with ExitStack() as s1:
            c1 = Ctx(nc, s1)
            k.dst_lo, k.dst_hi = (c1.sb(n, [P, LANE], BF16) for n in ("dst_lo", "dst_hi"))
            with ExitStack() as s0:
                dst_i = Ctx(nc, s0).sb("dst_again", [P, LANE], I32)
                load_small(k, "dl", [(dst_i[:, :], dst.rearrange("(p c) -> p c", p=P))])
                digits(k, "dd", dst_i, k.dst_lo, k.dst_hi)
            gat_gather(k, "g1g", tab, F, H1, edges, maxes, carry, histograms)
        for name, order in (("g1o", k.by_dst), ("g1q", k.by_src)):
            order_tables(k, name, order["count"], order)
        mend_tables(k, "g1m", k.by_dst, k.first_dst)
        gat_between(k, "g1", H1, al, sv, pself, maxes, stab, carry, first)
        gat_weigh(k, "g1w", F, H1, edges, scans, first, carry)
        FO = H1 * D + H1
        lane_carries(k, "g1c", carry[:, 0:FO], FO, k.by_dst, ALU.add, scans)
        with ExitStack() as s3:
            c3 = Ctx(nc, s3)
            agg = c3.sb("g1_agg", [P, NT, FO])
            h1 = c3.sb("g1_h1", [P, NT, H1 * C1])
            extract(k, "g1x", scans, k.by_dst, agg, FO, ALU.add)
            with ExitStack() as s4:
                gat_normalise(k, "g1n", agg, k.x, pself, H1, D, Ctx(nc, s4))
            node_linear(k, "g1b", agg[:, :, 0:H1 * D], w1d[:, :], h1, H1 * D, H1 * C1)
            with ExitStack() as s4:
                tmp = Ctx(nc, s4).sb("g1_tmp", [P, NT, H1 * C1])
                selu(k, "g1s", h1, tmp, b1[:, :])
            node_linear(k, "g1c2", h1, w2[:, :], h2, H1 * C1, C2 + 2)


def gat_between(k, name, heads, al, sv, pself, maxes, stab, carry, first):
    lane_carries(k, name + "m", carry[:, 0:heads], heads, k.by_dst, ALU.max, maxes)
    extract(k, name + "e", maxes, k.by_dst, pself, heads, ALU.max)
    with ExitStack() as st:
        c = Ctx(k.nc, st)
        step, logits, probs = c.sem(name + "b_step"), c.sem(name + "b_logits"), c.sem(name + "b_probs")
        with k.nc.Block() as block:
            @block.vector
            def _(v):
                ch = Chain(v, step)
                a_src, a_dst, m = al[:, :, 0:heads], al[:, :, heads:2 * heads], sv[:, :, heads:2 * heads]
                ch(v.tensor_copy(sv[:, :, 0:heads], a_dst))
                ch(v.tensor_tensor(m, pself[:, :, :], a_src, ALU.max))
                ch(v.tensor_tensor(m, m, a_dst, ALU.add))
                ch(v.scalar_tensor_tensor(out=m, in0=m, scalar=0.2, in1=m, op0=ALU.mult, op1=ALU.max))
                ch(v.tensor_tensor(pself[:, :, :], a_src, a_dst, ALU.add))
                ch(v.scalar_tensor_tensor(out=pself[:, :, :], in0=pself[:, :, :], scalar=0.2, in1=pself[:, :, :],
                                          op0=ALU.mult, op1=ALU.max))
                v.tensor_tensor(pself[:, :, :], pself[:, :, :], m, ALU.subtract).then_inc(logits, 1)

            @block.scalar
            def _(a):
                a.wait_ge(logits, 1)
                a.activation(pself[:, :, :], pself[:, :, :], ACT.Exp).then_inc(probs, 1)
    store_nodes(k, name + "u", [sv[:, :, :]], stab)
    spread(k, name + "p", sv, 2 * heads, stab, first[:, 0:2 * heads])


def gat_normalise(k, name, agg, x, pself, heads, FX, c):
    tmp = c.sb(name + "_tmp", [P, NT, FX])
    inv = c.sb(name + "_inv", [P, NT, heads])

    def body(v, ch):
        z = agg[:, :, heads * FX:heads * FX + heads]
        ch(v.tensor_tensor(inv[:, :, :], z, pself[:, :, :], ALU.add))
        ch(v.tensor_scalar(inv[:, :, :], inv[:, :, :], 1e-16, None, ALU.add))
        ch(v.reciprocal(inv[:, :, :], inv[:, :, :]))
        for h in range(heads):
            part = agg[:, :, h * FX:(h + 1) * FX]
            ch(v.tensor_tensor(tmp[:, :, :], x, bc(pself[:, :, h], [P, NT, FX], 2), ALU.mult))
            ch(v.tensor_tensor(part, part, tmp[:, :, :], ALU.add))
            ch(v.tensor_tensor(part, part, bc(inv[:, :, h], [P, NT, FX], 2), ALU.mult))
    vector_block(k, name, body)


def gat2(k, w, carry, first, y):
    nc = k.nc
    F = C2 + 1
    edges = k.dram("edges2", [P, LANE * F])
    maxes, scans = k.dram("maxes2", [E + P, 1]), k.dram("scans2", [E + P, F])
    tab, stab = k.dram("tab2", [NP, F]), k.dram("stab2", [NP, 2])
    with ExitStack() as st:
        c = Ctx(nc, st)
        b2 = c.sb("g2_b2", [P, C2])
        wf = c.sb("g2_wf", [C2, D])
        bf = c.sb("g2_bf", [P, D])
        sv = c.sb("g2_sv", [P, NT, 2])
        pself = c.sb("g2_pself", [P, NT, 1])
        load_small(k, "g2l", [(b2[:, :], row_bc(w["L0_gnn_b2"])), (wf[:, :], w["L0_gnn_Wf"]),
                              (bf[:, :], row_bc(w["L0_gnn_bf"]))])
        store_nodes(k, "g2t", [k.h2[:, :, 0:F]], tab)
        gat_gather(k, "g2g", tab, F, 1, edges, maxes, carry, count_in_group)
        gat_between(k, "g2", 1, k.h2[:, :, C2:C2 + 2], sv, pself, maxes, stab, carry, first)
        gat_weigh(k, "g2w", F, 1, edges, scans, first, carry)
        lane_carries(k, "g2c", carry[:, 0:F], F, k.by_dst, ALU.add, scans)
        with ExitStack() as s3:
            c3 = Ctx(nc, s3)
            agg = c3.sb("g2_agg", [P, NT, F])
            extract(k, "g2x", scans, k.by_dst, agg, F, ALU.add)
            with ExitStack() as s4:
                gat_normalise(k, "g2n", agg, k.h2[:, :, 0:C2], pself, 1, C2, Ctx(nc, s4))
            with ExitStack() as s4:
                tmp = Ctx(nc, s4).sb("g2_tmp", [P, NT, C2])
                selu(k, "g2s", agg[:, :, 0:C2], tmp, b2[:, :])
            node_linear(k, "g2f", agg[:, :, 0:C2], wf[:, :], y, C2, D)

        def residual(v, ch):
            ch(v.tensor_tensor(y[:, :, :], y[:, :, :], bc(bf[:, :], [P, NT, D], 1), ALU.add))
            ch(v.tensor_tensor(y[:, :, :], y[:, :, :], k.x[:, :, :], ALU.add))
        vector_block(k, "g2r", residual)
        layer_norm(k, "g2y", y, k.x)


def root_inverse(k, name, src, out, floor):
    with ExitStack() as st:
        c = Ctx(k.nc, st)
        t = c.sb(name + "_t", [P, NT])
        ready, rooted, done = c.sem(name + "_ready"), c.sem(name + "_rooted"), c.sem(name + "_done")
        with k.nc.Block() as block:
            @block.vector
            def _(v):
                v.tensor_scalar(t[:, :], src, floor, None, ALU.max).then_inc(ready, 1)
                v.wait_ge(rooted, 1)
                v.reciprocal(out, t[:, :]).then_inc(done, 1)

            @block.scalar
            def _(a):
                a.wait_ge(ready, 1)
                a.activation(t[:, :], t[:, :], ACT.Sqrt).then_inc(rooted, 1)


def gcn(k, w, carry, y, scan16, tab16, tab16b):
    nc = k.nc
    HG = 32
    with ExitStack() as st:
        c = Ctx(nc, st)
        k.free_place = c.sb("c_free_place", [P, NT])
        w1, w2 = c.sb("c_w1", [D, HG]), c.sb("c_w2", [HG, D])
        b1, gamma, beta = (c.sb(n, [P, HG]) for n in ("c_b1", "c_gamma", "c_beta"))
        b2 = c.sb("c_b2", [P, D])
        dinv = c.sb("c_dinv", [P, NT])
        xs = c.sb("c_xs", [P, NT, D])
        agg = c.sb("c_agg", [P, NT, D])
        h = c.sb("c_h", [P, NT, HG])
        load_small(k, "cl", [(w1[:, :], w["L1_gnn_W1"]), (w2[:, :], w["L1_gnn_W2"]),
                             (b1[:, :], row_bc(w["L1_gnn_b1"])), (gamma[:, :], row_bc(w["L1_gnn_gamma"])),
                             (beta[:, :], row_bc(w["L1_gnn_beta"])), (b2[:, :], row_bc(w["L1_gnn_b2"]))])
        vector_block(k, "cd", lambda v, ch: ch(v.tensor_scalar(
            dinv[:, :], k.by_dst["count"][:, :], 1.0, None, ALU.add)))
        root_inverse(k, "cr", dinv[:, :], dinv[:, :], 1.0)

        def aggregate(name, values, table, side):
            vector_block(k, name + "a", lambda v, ch: ch(v.tensor_tensor(
                xs[:, :, :], values, bc(dinv[:, :], [P, NT, D], 2), ALU.mult)))
            store_nodes(k, name + "b", [xs[:, :, :]], table)
            gcn_gather(k, name + "c", table, scan16, carry, side)
            lane_carries(k, name + "d", carry[:, 0:D], D, k.by_dst, ALU.add, scan16)
            extract(k, name + "e", scan16, k.by_dst, agg, D, ALU.add)

            def finish(v, ch):
                ch(v.tensor_tensor(agg[:, :, :], agg[:, :, :], xs[:, :, :], ALU.add))
                ch(v.tensor_tensor(agg[:, :, :], agg[:, :, :], bc(dinv[:, :], [P, NT, D], 2), ALU.mult))
            vector_block(k, name + "f", finish)

        half = NG // 2 + 1
        aggregate("c1", k.x[:, :, :], tab16, lambda k, c, n: count_before_group(
            k, c, n, 0, half, k.by_src["start"]))
        node_linear(k, "ch", agg, w1[:, :], h, D, HG)
        batch_norm_relu(k, "cn", h, b1, gamma, beta, HG)
        node_linear(k, "co", h, w2[:, :], y, HG, D)
        aggregate("c2", y[:, :, :], tab16b, lambda k, c, n: count_before_group(
            k, c, n, half, NG - half, k.free_place))

        def residual(v, ch):
            ch(v.tensor_tensor(y[:, :, :], agg[:, :, :], bc(b2[:, :], [P, NT, D], 1), ALU.add))
            ch(v.tensor_tensor(y[:, :, :], y[:, :, :], k.x[:, :, :], ALU.add))
        vector_block(k, "cs", residual)
        layer_norm(k, "cy", y, k.x)


def batch_norm_relu(k, name, h, b1, gamma, beta, HG):
    with ExitStack() as st:
        c = Ctx(k.nc, st)
        t = c.sb(name + "_t", [P, NT, HG])
        part = c.sb(name + "_part", [P, HG])
        mean = c.sb(name + "_mean", [P, HG])
        var = c.sb(name + "_var", [P, HG])
        pS = c.ps(name + "_pS", [P, 512])
        step, ready, summed, rooted = (c.sem(name + s) for s in ("_step", "_ready", "_summed", "_rooted"))
        shape = [P, NT, HG]
        with k.nc.Block() as block:
            @block.tensor
            def _(pe):
                for n in range(2):
                    pe.wait_ge(ready, n + 1)
                    pe.matmul(pS[:, n * HG:(n + 1) * HG], k.ones[:, :], part[:, :],
                              start=True, stop=True).then_inc(summed, 1)

            @block.scalar
            def _(a):
                a.wait_ge(ready, 3)
                a.activation(var[:, :], var[:, :], ACT.Sqrt).then_inc(rooted, 1)

            @block.vector
            def _(v):
                ch = Chain(v, step)
                ch(v.tensor_tensor(h[:, :, :], h[:, :, :], bc(b1[:, :], shape, 1), ALU.add))
                ch(v.tensor_tensor(t[:, :, :], h[:, :, :], bc(k.node_mask[:, :], shape, 2), ALU.mult))
                v.tensor_reduce(part[:, :], t[:, :, :].rearrange("p t f -> p f t"), axis=AX.X,
                                op=ALU.add).then_inc(ready, 1)
                v.wait_ge(summed, 1)
                ch(v.tensor_scalar(mean[:, :], pS[:, 0:HG], 1.0 / N, None, ALU.mult))
                ch(v.tensor_tensor(h[:, :, :], h[:, :, :], bc(mean[:, :], shape, 1), ALU.subtract))
                ch(v.tensor_tensor(t[:, :, :], h[:, :, :], h[:, :, :], ALU.mult))
                ch(v.tensor_tensor(t[:, :, :], t[:, :, :], bc(k.node_mask[:, :], shape, 2), ALU.mult))
                v.tensor_reduce(part[:, :], t[:, :, :].rearrange("p t f -> p f t"), axis=AX.X,
                                op=ALU.add).then_inc(ready, 1)
                v.wait_ge(summed, 2)
                v.tensor_scalar(var[:, :], pS[:, HG:2 * HG], 1.0 / N, 1e-5, ALU.mult, ALU.add).then_inc(ready, 1)
                v.wait_ge(rooted, 1)
                ch(v.reciprocal(var[:, :], var[:, :]))
                ch(v.tensor_tensor(var[:, :], var[:, :], gamma[:, :], ALU.mult))
                ch(v.tensor_tensor(h[:, :, :], h[:, :, :], bc(var[:, :], shape, 1), ALU.mult))
                ch(v.tensor_tensor(h[:, :, :], h[:, :, :], bc(beta[:, :], shape, 1), ALU.add))
                ch(v.tensor_scalar(h[:, :, :], h[:, :, :], 0.0, None, ALU.max))


def sheaf(k, w, carry, first, y, scan16, messages):
    nc = k.nc
    tab = k.dram("tab5", [NP, D + 1])
    with ExitStack() as st:
        c = Ctx(nc, st)
        w1 = c.sb("s_w1", [2 * D, 2, HID])
        b1 = c.sb("s_b1", [2 * HID, 1])
        w2 = c.sb("s_w2", [2 * HID, 2, D])
        b2 = c.sb("s_b2", [P, 2 * D])
        xd = c.sb("s_xd", [P, NT, D + 1])
        agg = c.sb("s_agg", [P, NT, D])
        vector_block(k, "sz", lambda v, ch: ch(v.memset(w2[:, :, :], 0.0)))
        W1, W2 = w["L2_gnn_W1"], w["L2_gnn_W2"]
        load_small(k, "sl", [
            (w1[0:2 * D, 0, :], W1.rearrange("h i -> i h")),
            (w1[0:D, 1, :], W1[:, D:2 * D].rearrange("h i -> i h")),
            (w1[D:2 * D, 1, :], W1[:, 0:D].rearrange("h i -> i h")),
            (b1[0:HID, :], w["L2_gnn_b1"].rearrange("(h a) -> h a", a=1)),
            (b1[HID:2 * HID, :], w["L2_gnn_b1"].rearrange("(h a) -> h a", a=1)),
            (w2[0:HID, 0, :], W2.rearrange("o h -> h o")),
            (w2[HID:2 * HID, 1, :], W2.rearrange("o h -> h o")),
            (b2[:, 0:D], row_bc(w["L2_gnn_b2"])), (b2[:, D:2 * D], row_bc(w["L2_gnn_b2"]))])

        def degrees(v, ch):
            ch(v.tensor_copy(xd[:, :, 0:D], k.x[:, :, :]))
            ch(v.tensor_tensor(xd[:, :, D], k.by_dst["count"][:, :], k.by_src["count"][:, :], ALU.add))
        vector_block(k, "sd", degrees)
        root_inverse(k, "sr", xd[:, :, D], xd[:, :, D], 1e-5)
        store_nodes(k, "st", [xd[:, :, :]], tab)
        spread(k, "sp", xd, D + 1, tab, first[:, 0:D + 1])
        sheaf_edges(k, "se", tab, scan16, messages, first, carry,
                    w1[:, :, :].rearrange("p a h -> p (a h)"), b1, w2[:, :, :].rearrange("p a h -> p (a h)"), b2)
        lane_carries(k, "sc", carry[:, 0:D], D, k.by_dst, ALU.add, scan16)
        extract(k, "sx", scan16, k.by_dst, agg, D, ALU.add)
        first_src = c.sb("s_first_src", [P, 1], I32)
        first_src_f = c.sb("s_first_src_f", [P, 1])
        load_small(k, "sf", [(first_src_f[:, :], rows(messages)[:, 0, D:D + 1])])
        vector_block(k, "si", lambda v, ch: ch(v.tensor_copy(first_src[:, :], first_src_f[:, :])))
        mend_tables(k, "sm", k.by_src, first_src)
        src_order_scan(k, "ss", messages, scan16, carry, D + 1, True)
        lane_carries(k, "sq", carry[:, 0:D], D, k.by_src, ALU.add, scan16)
        extract(k, "sw", scan16, k.by_src, y, D, ALU.add)

        def residual(v, ch):
            ch(v.tensor_tensor(y[:, :, :], y[:, :, :], agg[:, :, :], ALU.add))
            ch(v.tensor_tensor(y[:, :, :], y[:, :, :], bc(xd[:, :, D], [P, NT, D], 2), ALU.mult))
            ch(v.tensor_tensor(y[:, :, :], y[:, :, :], k.x[:, :, :], ALU.add))
            ch(v.tensor_scalar(y[:, :, :], y[:, :, :], 0.0, None, ALU.max))
            ch(v.tensor_tensor(y[:, :, :], y[:, :, :], k.x[:, :, :], ALU.add))
        vector_block(k, "sv", residual)
        layer_norm(k, "sy", y, k.x)


def product(k, w, carry, first, y, scan16, messages, attr):
    nc = k.nc
    tab = k.dram("tab6", [NP, D])
    norm_lin = 1.0 / float(np.float32(np.sqrt(D)))
    norm_upd = 1.0 / float(np.float32(np.sqrt(D * D)))
    with ExitStack() as st:
        c = Ctx(nc, st)
        wm = c.sb("p_wm", [P, D])
        wl = c.sb("p_wl", [D, D])
        wu = c.sb("p_wu", [P, 2, D])
        wo = c.sb("p_wo", [D, D])
        agg = c.sb("p_agg", [P, NT, D])
        load_small(k, "pl", [
            (wm[:, :], w["L3_gnn_W_msg_tp"].rearrange("i j h -> (i j) h")), (wl[:, :], w["L3_gnn_W_msg_lin"]),
            (wu[:, 0, :], w["L3_gnn_W_upd_tp"][0:D // 2].rearrange("i j h -> (i j) h")),
            (wu[:, 1, :], w["L3_gnn_W_upd_tp"][D // 2:D].rearrange("i j h -> (i j) h")),
            (wo[:, :], w["L3_gnn_W_upd_lin"])])
        store_nodes(k, "pt", [k.x[:, :, :]], tab)
        spread(k, "pp", k.x, D, tab, first[:, 0:D])
        product_edges(k, "pe", attr, messages, first, wm)
        src_order_scan(k, "ps", messages, scan16, carry, D, False)
        lane_carries(k, "pc", carry[:, 0:D], D, k.by_src, ALU.add, scan16)
        extract(k, "px", scan16, k.by_src, y, D, ALU.add)
        node_linear(k, "pn", y, wl[:, :], agg, D, D)
        vector_block(k, "pq", lambda v, ch: ch(v.tensor_scalar(
            agg[:, :, :], agg[:, :, :], norm_lin, None, ALU.mult)))
        u = c.sb("p_u", [P, NT, D])
        for half in range(2):
            with ExitStack() as s3:
                o = Ctx(nc, s3).sb(f"p_o{half}", [P, NT, D // 2, D])

                def outer(v, ch):
                    for i in range(D // 2):
                        n = half * (D // 2) + i
                        ch(v.tensor_tensor(o[:, :, i, :], agg[:, :, :], bc(k.x[:, :, n], [P, NT, D], 2), ALU.mult))
                vector_block(k, f"po{half}", outer)
                node_linear(k, f"pm{half}", o[:, :, :, :].rearrange("p t i d -> p t (i d)"), wu[:, half, :],
                            u if half else y, P, D)
        with ExitStack() as s3:
            c3 = Ctx(nc, s3)
            summed, silued = c3.sem("pa_summed"), c3.sem("pa_silued")
            with nc.Block() as block:
                @block.vector
                def _(v):
                    v.tensor_tensor(u[:, :, :], u[:, :, :], y[:, :, :], ALU.add).then_inc(summed, 1)

                @block.scalar
                def _(a):
                    a.wait_ge(summed, 1)
                    a.activation(u[:, :, :], u[:, :, :], ACT.Silu, scale=norm_upd).then_inc(silued, 1)
        node_linear(k, "pw", u, wo[:, :], y, D, D)

        def residual(v, ch):
            ch(v.scalar_tensor_tensor(out=y[:, :, :], in0=y[:, :, :], scalar=norm_lin, in1=k.x[:, :, :],
                                      op0=ALU.mult, op1=ALU.add))
            ch(v.tensor_tensor(y[:, :, :], y[:, :, :], k.x[:, :, :], ALU.add))
        vector_block(k, "pr", residual)
        layer_norm(k, "py", y, k.x)


_EDGE = ["x", "src", "dst", "edge_attr_8"]
_WEIGHTS = ["L0_gnn_W1", "L0_gnn_a_src1", "L0_gnn_a_dst1", "L0_gnn_b1", "L0_gnn_W2", "L0_gnn_a_src2",
            "L0_gnn_a_dst2", "L0_gnn_b2", "L0_gnn_Wf", "L0_gnn_bf", "L1_gnn_W1", "L1_gnn_b1", "L1_gnn_gamma",
            "L1_gnn_beta", "L1_gnn_W2", "L1_gnn_b2", "L2_gnn_W1", "L2_gnn_b1", "L2_gnn_W2", "L2_gnn_b2",
            "L3_gnn_W_msg_tp", "L3_gnn_W_msg_lin", "L3_gnn_W_upd_tp", "L3_gnn_W_upd_lin"]


def kernel(**inputs):
    import numpy as _np
    import concourse.bacc as _bacc
    from concourse import mybir as _mybir
    from concourse.bass_utils import run_bass_kernel_spmd as _run

    nc = _bacc.Bacc("TRN2", target_bir_lowering=False, num_devices=1)
    arrays, args = {}, {}
    for name in _EDGE + _WEIGHTS:
        a = _np.ascontiguousarray(inputs[name])
        arrays[f"in_{name}_dram"] = a
        args[name] = nc.dram_tensor(f"in_{name}_dram", a.shape, _mybir.dt.from_np(a.dtype), kind="ExternalInput").ap()
    out = nc.dram_tensor("out_0_dram", (N, D), F32, kind="ExternalOutput").ap()
    program(nc, args["x"], args["src"], args["dst"], args["edge_attr_8"], args, out)
    r = _run(nc, [arrays], core_ids=[0])
    return r.results[0]["out_0_dram"]
```

```python
import numpy as np
import concourse.bass as bass
from concourse import mybir
from contextlib import ExitStack

F32 = mybir.dt.float32
BF16 = mybir.dt.bfloat16
I32 = mybir.dt.int32
ALU = mybir.AluOpType
ACT = mybir.ActivationFunctionType
AX = mybir.AxisListType

P = 128
N, E = 12500, 400000
LANE = E // P
CH = 125
NCH = LANE // CH
PAIRS = NCH // 2
GRP = 5
NG = CH // GRP
DG = 4
DC = DG * GRP
SG = NG - DG
SC = SG * GRP
LS = NCH * SC
NT = 100
NP = NT * P
XT = 25
FULL, REST = N // P, N % P
D = 16
H1, C1 = 3, 32
C2 = 32
HID = 64
DE = 8
BIG = 1e30
SELU_ALPHA, SELU_SCALE = 1.6732632423543772, 1.0507009873554805


class Chain:

    def __init__(self, eng, sem):
        self.eng, self.sem, self.n, self.base, self.starts = eng, sem, 0, [], []

    def loose(self, ins):
        self.n += 1
        ins.then_inc(self.sem, 1)

    def wait(self):
        self.eng.wait_ge(self.sem, sum(self.base[1:], self.base[0]) + self.n if self.base else self.n)

    def __call__(self, ins):
        self.loose(ins)
        self.wait()

    def enter(self, i, per):
        self.base.append(i * per)
        self.starts.append(self.n)

    def leave(self, count, per):
        assert self.n - self.starts[-1] == per, (self.n - self.starts[-1], per)
        self.n = self.starts.pop() + count * per
        self.base.pop()


def over_chunks(eng, body, chain=None, per=0):
    with eng.Fori(0, PAIRS) as j:
        if chain:
            chain.enter(j, 2 * per)
        body(2 * j, 0, j)
        body(2 * j + 1, 1, j)
        if chain:
            chain.leave(PAIRS, 2 * per)
    body(NCH - 1, 0, PAIRS)


def cols(i, n=CH):
    return bass.ds(i * n, n)


def rows(ap, lane=LANE):
    return ap[0:P * lane, :].rearrange("(p c) f -> p c f", p=P)


def bc(ap, shape, axis):
    return ap.unsqueeze(axis).to_broadcast(shape)


class Ctx:

    def __init__(self, nc, stack):
        self.nc, self.stack, self.count = nc, stack, 0

    def sb(self, name, shape, dt=F32):
        return self.stack.enter_context(self.nc.sbuf_tensor(name, shape, dt))[tuple(slice(None) for _ in shape)]

    def ps(self, name, shape, dt=F32):
        return self.stack.enter_context(self.nc.psum_tensor(name, shape, dt))[tuple(slice(None) for _ in shape)]

    def sem(self, name):
        sem = self.stack.enter_context(self.nc.semaphore(name))
        self.stack.callback(self.nc.sync.sem_clear, sem)
        return sem

    def pool_dma_sem(self, name):
        sem = self.stack.enter_context(self.nc.semaphore(name))
        self.stack.callback(self.nc.gpsimd.sem_clear, sem)
        self.stack.callback(self.nc.gpsimd.dma_reset, range(sem.num, sem.num + 1))
        return sem

    def dram(self, name, shape, dt=F32):
        return self.nc.dram_tensor(name, shape, dt).ap()


def scope(k):
    return Ctx(k.nc, k.stack.enter_context(ExitStack()))



def node_linear(k, name, src, w, out, K, M):
    groups = NT // GRP
    with ExitStack() as st:
        c = Ctx(k.nc, st)
        stage = [c.sb(f"{name}_stage{b}", [P, GRP, K]) for b in range(2)]
        tT = [c.sb(f"{name}_tT{b}", [K, GRP * P]) for b in range(2)]
        pT = [c.ps(f"{name}_pT{b}", [K, 1024]) for b in range(2)]
        pO = [c.ps(f"{name}_pO{b}", [P, 512]) for b in range(2)]
        staged, transposed, copied, product, evacuated = (
            c.sem(name + s) for s in ("_staged", "_transposed", "_copied", "_product", "_evacuated"))
        with k.nc.Block() as block:
            @block.vector
            def _(v):
                def stage_group(n, b, first=False):
                    if not first:
                        v.wait_ge(transposed, n - 1)
                    v.tensor_copy(stage[b][:, :, :], src[:, cols(n, GRP), :]).then_inc(staged, 1)

                def evacuate(n, b):
                    v.wait_ge(product, n + 1)
                    v.tensor_copy(out[:, cols(n, GRP), :],
                                  pO[b][:, 0:GRP * M].rearrange("p (g m) -> p g m", g=GRP)).then_inc(evacuated, 1)
                stage_group(0, 0, True)
                stage_group(1, 1, True)
                with v.Fori(0, groups // 2 - 1) as j:
                    stage_group(2 * j + 2, 0)
                    evacuate(2 * j, 0)
                    stage_group(2 * j + 3, 1)
                    evacuate(2 * j + 1, 1)
                evacuate(groups - 2, 0)
                evacuate(groups - 1, 1)

            @block.scalar
            def _(a):
                def copy(n, b):
                    a.wait_ge(transposed, n + 1)
                    a.activation(tT[b][:, :], pT[b][:, 0:GRP * P], ACT.Copy).then_inc(copied, 1)
                with a.Fori(0, groups // 2) as j:
                    copy(2 * j, 0)
                    copy(2 * j + 1, 1)

            @block.tensor
            def _(pe):
                def transpose(n, b):
                    pe.wait_ge(staged, n + 1)
                    pe.nop(nofuse=True)
                    for g in range(GRP):
                        mm = pe.transpose(pT[b][:, g * P:(g + 1) * P], stage[b][:, g, :], k.ident[:, :])
                    mm.then_inc(transposed, 1)

                def multiply(n, b, first=False):
                    pe.wait_ge(copied, n + 1)
                    if not first:
                        pe.wait_ge(evacuated, n - 1)
                    for g in range(GRP):
                        mm = pe.matmul(pO[b][:, g * M:(g + 1) * M], tT[b][:, g * P:(g + 1) * P], w,
                                       start=True, stop=True)
                    mm.then_inc(product, 1)
                transpose(0, 0)
                transpose(1, 1)
                multiply(0, 0, True)
                transpose(2, 0)
                multiply(1, 1, True)
                with pe.Fori(1, groups // 2 - 1) as j:
                    transpose(2 * j + 1, 1)
                    multiply(2 * j, 0)
                    transpose(2 * j + 2, 0)
                    multiply(2 * j + 1, 1)
                transpose(groups - 1, 1)
                multiply(groups - 2, 0)
                multiply(groups - 1, 1)


def layer_norm(k, name, x, out):
    with ExitStack() as st:
        c = Ctx(k.nc, st)
        sq = c.sb(name + "_sq", [P, NT, D])
        mean = c.sb(name + "_mean", [P, NT])
        var = c.sb(name + "_var", [P, NT])
        sd = c.sb(name + "_sd", [P, NT])
        step, var_ready, sd_ready = c.sem(name + "_step"), c.sem(name + "_var_ready"), c.sem(name + "_sd_ready")
        with k.nc.Block() as block:
            @block.vector
            def _(v):
                ch = Chain(v, step)
                ch(v.tensor_reduce(mean[:, :], x[:, :, :], axis=AX.X, op=ALU.add))
                ch(v.tensor_scalar(mean[:, :], mean[:, :], 1.0 / D, None, ALU.mult))
                ch(v.tensor_tensor(x[:, :, :], x[:, :, :], bc(mean[:, :], [P, NT, D], 2), ALU.subtract))
                ch(v.tensor_tensor(sq[:, :, :], x[:, :, :], x[:, :, :], ALU.mult))
                ch(v.tensor_reduce(var[:, :], sq[:, :, :], axis=AX.X, op=ALU.add))
                v.tensor_scalar(var[:, :], var[:, :], 1.0 / D, 1e-5, ALU.mult, ALU.add).then_inc(var_ready, 1)
                v.wait_ge(sd_ready, 1)
                ch(v.reciprocal(var[:, :], sd[:, :]))
                ch(v.tensor_tensor(out[:, :, :], x[:, :, :], bc(var[:, :], [P, NT, D], 2), ALU.mult))

            @block.scalar
            def _(a):
                a.wait_ge(var_ready, 1)
                a.activation(sd[:, :], var[:, :], ACT.Sqrt).then_inc(sd_ready, 1)


def selu(k, name, x, tmp, bias):
    with ExitStack() as st:
        c = Ctx(k.nc, st)
        step, neg, exps = c.sem(name + "_step"), c.sem(name + "_neg"), c.sem(name + "_exps")
        shape = [P, NT, x.shape[2]]
        with k.nc.Block() as block:
            @block.vector
            def _(v):
                ch = Chain(v, step)
                ch(v.tensor_tensor(x[:, :, :], x[:, :, :], bc(bias, shape, 1), ALU.add))
                v.tensor_scalar(tmp[:, :, :], x[:, :, :], 0.0, None, ALU.min).then_inc(neg, 1)
                ch(v.tensor_scalar(x[:, :, :], x[:, :, :], 0.0, SELU_SCALE, ALU.max, ALU.mult))
                v.wait_ge(exps, 1)
                ch(v.tensor_scalar(tmp[:, :, :], tmp[:, :, :], 1.0, SELU_ALPHA * SELU_SCALE,
                                   ALU.subtract, ALU.mult))
                ch(v.tensor_tensor(x[:, :, :], x[:, :, :], tmp[:, :, :], ALU.add))

            @block.scalar
            def _(a):
                a.wait_ge(neg, 1)
                a.activation(tmp[:, :, :], tmp[:, :, :], ACT.Exp).then_inc(exps, 1)


def store_nodes(k, name, parts, table):
    with ExitStack() as st:
        c = Ctx(k.nc, st)
        stored = c.sem(name + "_stored")
        with k.nc.Block() as block:
            @block.sync
            def _(s):
                at = 0
                view = table[0:NP, :].rearrange("(t p) f -> p t f", p=P)
                for part in parts:
                    w = part.shape[2]
                    s.dma_start(view[:, :, at:at + w], part).then_inc(stored, 16)
                    at += w
                s.wait_ge(stored, 16 * len(parts))


def vector_block(k, name, body):
    with ExitStack() as st:
        step = Ctx(k.nc, st).sem(name + "_step")
        with k.nc.Block() as block:
            @block.vector
            def _(v):
                body(v, Chain(v, step))



def lane_carries(k, name, last, F, order, op, scans):
    with ExitStack() as st:
        c = Ctx(k.nc, st)
        T = c.sb(name + "_T", [F, P])
        whole = c.sb(name + "_whole", [F, P])
        carried = c.sb(name + "_carried", [P, F])
        ends = c.sb(name + "_ends", [P, F])
        out_sem, in_sem, step, shifted, back = (
            c.sem(name + s) for s in ("_out", "_in", "_step", "_shifted", "_back"))
        got, sent = c.pool_dma_sem(name + "_got"), c.pool_dma_sem(name + "_sent")
        buf, table = k.lanes[0:P, 0:F], k.carried[0:P + 1, 0:F]
        scanned = 2 if op == ALU.add else 3
        with k.nc.Block() as block:
            @block.vector
            def _(v):
                ch = Chain(v, step)
                ch(v.memset(carried[:, :], 0.0))
                v.wait_ge(in_sem, 32)
                if op == ALU.add:
                    ch(v.tensor_tensor_scan(T[:, :], whole[:, :], T[:, :], 0.0, ALU.mult, ALU.add))
                else:
                    ch(v.tensor_scalar(whole[:, :], whole[:, :], 1.0, BIG, ALU.subtract, ALU.mult))
                    ch(v.tensor_tensor_scan(T[:, :], whole[:, :], T[:, :], -BIG, ALU.add, ALU.max))
                v.wait_ge(back, 16)
                v.wait_ge(got, 16)
                ch(v.tensor_tensor(ends[:, :], ends[:, :], carried[:, :], op))

            @block.gpsimd
            def _(g):
                g.indirect_dma_start(out=ends[:, :], out_offset=None, in_=scans[0:E, :],
                                     in_offset=bass.IndirectOffsetOnAxis(ap=order["mend_from"][:, 0:1], axis=0)
                                     ).then_inc(got, 16)
                g.wait_ge(step, scanned + 1)
                g.indirect_dma_start(out=scans, in_=ends[:, :], in_offset=None,
                                     out_offset=bass.IndirectOffsetOnAxis(ap=order["mend_to"][:, 0:1], axis=0)
                                     ).then_inc(sent, 16)
                g.wait_ge(sent, 16)

            @block.sync
            def _(s):
                with k.nc.allow_non_contiguous_dma("transpose of a small tile"):
                    s.dma_start(buf, last).then_inc(out_sem, 16)
                    s.wait_ge(out_sem, 16)
                    s.dma_start(T[:, :], buf.rearrange("p f -> f p")).then_inc(in_sem, 16)
                    s.dma_start(whole[:, :], order["whole_row"].to_broadcast([F, P])).then_inc(in_sem, 16)
                    s.wait_ge(step, scanned)
                    s.dma_start(table[0:P, :].rearrange("p f -> f p"), T[:, :]).then_inc(shifted, 16)
                    s.wait_ge(shifted, 16)
                    s.dma_start(carried[1:P, :], table[0:P - 1, :]).then_inc(back, 16)


def mend_tables(k, name, order, first_id):
    tab = k.dram(name + "_tab", [NP, 3])
    with ExitStack() as st:
        c = Ctx(k.nc, st)
        node = c.sb(name + "_node", [P, NT, 3])
        row = c.sb(name + "_row", [P, 3])
        to = c.sb(name + "_to", [P, 1])
        spare = c.sb(name + "_spare", [P, 1])

        def fields(v, ch):
            ch(v.tensor_copy(node[:, :, 0], order["end"][:, :]))
            ch(v.tensor_copy(node[:, :, 1], order["end_lane"][:, :]))
            ch(v.tensor_copy(node[:, :, 2], order["cross"][:, :]))
        vector_block(k, name + "f", fields)
        store_nodes(k, name + "s", [node[:, :, :]], tab)
        got, step = c.pool_dma_sem(name + "_got"), c.sem(name + "_step")
        with k.nc.Block() as block:
            @block.gpsimd
            def _(g):
                g.indirect_dma_start(out=row[:, :], out_offset=None, in_=tab,
                                     in_offset=bass.IndirectOffsetOnAxis(ap=first_id[:, 0:1], axis=0)
                                     ).then_inc(got, 16)

            @block.vector
            def _(v):
                ch = Chain(v, step)
                v.wait_ge(got, 16)
                ch(v.tensor_copy(order["mend_from"][:, :], row[:, 0:1]))
                ch(v.tensor_tensor(row[:, 1:2], row[:, 1:2], k.part[:, :], ALU.is_equal))
                ch(v.tensor_tensor(row[:, 1:2], row[:, 1:2], row[:, 2:3], ALU.mult))
                ch(v.tensor_scalar(spare[:, :], k.part[:, :], float(E), None, ALU.add))
                ch(v.tensor_tensor(to[:, :], row[:, 0:1], spare[:, :], ALU.subtract))
                ch(v.tensor_tensor(to[:, :], to[:, :], row[:, 1:2], ALU.mult))
                ch(v.tensor_tensor(to[:, :], to[:, :], spare[:, :], ALU.add))
                ch(v.tensor_copy(order["mend_to"][:, :], to[:, :]))


def extract(k, name, scans, order, out, F, op):
    with ExitStack() as st:
        c = Ctx(k.nc, st)
        si = [c.sb(f"{name}_si{b}", [P, XT], I32) for b in range(2)]
        gs = [c.sb(f"{name}_gs{b}", [P, XT, F]) for b in range(2)]
        staged, joined = ([c.sem(f"{name}_{s}{b}") for b in range(2)] for s in ("staged", "joined"))
        got = [c.pool_dma_sem(f"{name}_got{b}") for b in range(2)]
        shape = [P, XT, F]
        with k.nc.Block() as block:
            @block.gpsimd
            def _(g):
                def step(i, b, j):
                    g.wait_ge(joined[b], j + 1)
                    g.tensor_copy(si[b][:, :], order["end"][:, cols(i, XT)]).then_inc(staged[b], 1)
                    g.wait_ge(staged[b], j + 1)
                    g.nop(nofuse=True)
                    for t in range(XT):
                        g.indirect_dma_start(out=gs[b][:, t, :], out_offset=None, in_=scans[0:E, :],
                                             in_offset=bass.IndirectOffsetOnAxis(ap=si[b][:, t:t + 1], axis=0)
                                             ).then_inc(got[b], 16)
                with g.Fori(0, NT // XT // 2) as j:
                    step(2 * j, 0, j)
                    step(2 * j + 1, 1, j)

            @block.vector
            def _(v):
                for b in range(2):
                    v.sem_inc(joined[b], 1)

                def step(i, b, j):
                    v.wait_ge(got[b], (j + 1) * (16 * XT))
                    if op == ALU.add:
                        v.tensor_tensor(out[:, cols(i, XT), :], gs[b][:, :, :],
                                        bc(order["some"][:, cols(i, XT)], shape, 2), ALU.mult).then_inc(joined[b], 1)
                    else:
                        v.tensor_tensor(out[:, cols(i, XT), :], gs[b][:, :, :],
                                        bc(order["none_neg"][:, cols(i, XT)], shape, 2), ALU.add).then_inc(joined[b], 1)
                with v.Fori(0, NT // XT // 2) as j:
                    step(2 * j, 0, j)
                    step(2 * j + 1, 1, j)


def spread(k, name, values, F, table, first):
    view = table_view(k, F, E + NP)
    with ExitStack() as st:
        c = Ctx(k.nc, st)
        si = c.sb(name + "_si", [P, XT], I32)
        sv = c.sb(name + "_sv", [P, XT, F])
        staged = c.sem(name + "_staged")
        sent, got = c.pool_dma_sem(name + "_sent"), c.pool_dma_sem(name + "_got")
        with k.nc.Block() as block:
            @block.gpsimd
            def _(g):
                with g.Fori(0, NT // XT) as i:
                    g.tensor_copy(si[:, :], k.by_dst["begin"][:, cols(i, XT)]).then_inc(staged, 1)
                    g.tensor_copy(sv[:, :, :], values[:, cols(i, XT), :]).then_inc(staged, 1)
                    g.wait_ge(staged, 2 * i + 2)
                    g.nop(nofuse=True)
                    for t in range(XT):
                        g.indirect_dma_start(out=view, in_=sv[:, t, :], in_offset=None,
                                             out_offset=bass.IndirectOffsetOnAxis(ap=si[:, t:t + 1], axis=0)
                                             ).then_inc(sent, 16)
                    g.wait_ge(sent, (i + 1) * (16 * XT))
                    g.nop(nofuse=True)
                g.indirect_dma_start(out=first, out_offset=None, in_=table,
                                     in_offset=bass.IndirectOffsetOnAxis(ap=k.first_dst[:, 0:1], axis=0)
                                     ).then_inc(got, 16)
                g.wait_ge(got, 16)


def table_view(k, F, n):
    return k.spread_buf[0:n * F].rearrange("(r f) -> r f", f=F)


def gather_column_loop(g, k, i, j, b, table, G, stage, staged, freed, credit, got, index):
    g.wait_ge(freed[b], (j + 1) * credit)
    g.tensor_copy(stage[b][:, :], index[:, cols(i)]).then_inc(staged[b], 1)
    g.wait_ge(staged[b], j + 1)
    g.nop(nofuse=True)
    for t in range(CH):
        g.indirect_dma_start(out=G[b][:, t, :], out_offset=None, in_=table,
                             in_offset=bass.IndirectOffsetOnAxis(ap=stage[b][:, t:t + 1], axis=0)
                             ).then_inc(got[b], 16)



def setup(k, x, src, dst):
    c = k
    with ExitStack() as st:
        t = Ctx(k.nc, st)
        iota_i = t.sb("iota_i", [P, P], I32)
        part_i = t.sb("part_i", [P, 1], I32)
        part_one = t.sb("part_one", [P, P])
        lane_first = t.sb("lane_first", [P, 1], I32)
        loaded, made, step, whole_out = (t.sem(s) for s in ("su_loaded", "su_made", "su_step", "su_whole"))
        xclear = t.sem("su_xclear")
        with k.nc.Block() as block:
            @block.sync
            def _(s):
                s.dma_start(c.dst_i[:, :], dst.rearrange("(p c) -> p c", p=P)).then_inc(loaded, 16)
                s.dma_start(c.src_i[:, :], src.rearrange("(p c) -> p c", p=P)).then_inc(loaded, 16)
                s.wait_ge(xclear, 2)
                with k.nc.allow_non_contiguous_dma("one value of each lane"):
                    s.dma_start(lane_first[1:P, :],
                                dst.rearrange("(p c) -> p c", p=P)[0:P - 1, LANE - 1:LANE]).then_inc(loaded, 16)
                    s.dma_start(c.first_dst[:, :],
                                dst.rearrange("(p c) -> p c", p=P)[:, 0:1]).then_inc(loaded, 16)
                s.dma_start(c.x[:, 0:FULL, :],
                            x[0:FULL * P, :].rearrange("(t p) f -> p t f", p=P)).then_inc(loaded, 16)
                s.dma_start(c.x[0:REST, FULL, :], x[FULL * P:N, :]).then_inc(loaded, 16)
                s.wait_ge(made, 1)
                s.dma_start(c.by_dst["whole_row"].rearrange("a p -> p a"), c.whole[:, :]).then_inc(whole_out, 16)
                s.wait_ge(whole_out, 16)

            @block.gpsimd
            def _(g):
                g.iota(iota_i[:, :], pattern=[[1, P]], base=0, channel_multiplier=0).then_inc(step, 1)
                g.iota(part_i[:, :], pattern=[[0, 1]], base=0, channel_multiplier=1).then_inc(step, 1)

            @block.vector
            def _(v):
                v.memset(lane_first[:, :], -1).then_inc(xclear, 1)
                v.memset(c.x[:, FULL:NT, :], 0.0).then_inc(xclear, 1)
                v.wait_ge(step, 2)
                ch = Chain(v, step)
                ch.n = 2
                ch(v.tensor_copy(c.iota[:, :], iota_i[:, :]))
                ch(v.tensor_copy(c.part[:, :], part_i[:, :]))
                ch(v.tensor_scalar(c.ident[:, :], c.iota[:, :], c.part[:, 0:1], None, ALU.is_equal))
                ch(v.tensor_scalar(c.before[:, :], c.iota[:, :], c.part[:, 0:1], None, ALU.is_gt))
                ch(v.memset(c.ones[:, :], 1.0))
                ch(v.tensor_copy(c.ident_b[:, :], c.ident[:, :]))
                ch(v.tensor_scalar(c.ident128_b[:, :], c.ident[:, :], float(P), None, ALU.mult))
                ch(v.memset(c.earlier[:, 0:(GRP - 1) * P], 1.0))
                ch(v.tensor_scalar(c.earlier[:, (GRP - 1) * P:], c.iota[:, :], c.part[:, 0:1], None, ALU.is_lt))
                ch(v.memset(c.node_mask[:, :], 1.0))
                ch(v.memset(c.node_mask[:, FULL + 1:NT], 0.0))
                ch(v.tensor_scalar(c.node_mask[:, FULL:FULL + 1], c.part[:, 0:1], float(REST), None, ALU.is_lt))
                v.wait_ge(loaded, 96)
                ch(v.tensor_tensor(c.keep_d[:, 0:1], c.dst_i[:, 0:1], lane_first[:, :], ALU.is_equal))
                ch(v.tensor_tensor(c.keep_d[:, 1:LANE], c.dst_i[:, 1:LANE], c.dst_i[:, 0:LANE - 1], ALU.is_equal))
                v.tensor_reduce(c.whole[:, :], c.keep_d[:, :], axis=AX.X, op=ALU.min).then_inc(made, 1)
                v.wait_ge(made, 1)


SPREAD_F = 17
SPREAD_PIECE = 4250
SPREAD_PIECES = (E + NP) * SPREAD_F // (P * SPREAD_PIECE) + 1
SPREAD_SIZE = SPREAD_PIECES * P * SPREAD_PIECE


def digits(k, name, src_i, lo, hi):
    with ExitStack() as st:
        t = Ctx(k.nc, st).sb(name + "_t", [P, LANE], I32)

        def body(v, ch):
            ch(v.tensor_scalar(t[:, :], src_i[:, :], P - 1, None, ALU.bitwise_and))
            ch(v.tensor_copy(lo[:, :], t[:, :]))
            ch(v.tensor_scalar(t[:, :], src_i[:, :], 7, None, ALU.logical_shift_right))
            ch(v.tensor_copy(hi[:, :], t[:, :]))
        vector_block(k, name, body)


def order_tables(k, name, counts, order, lane_edges):
    with ExitStack() as st:
        c = Ctx(k.nc, st)
        pt = c.ps(name + "_pt", [P, 512])
        tot = c.sb(name + "_tot", [P, NT])
        run = c.sb(name + "_run", [P, NT])
        start = order["start"]
        endf = c.sb(name + "_endf", [P, NT])
        le = c.sb(name + "_le", [P, NT])
        ls = c.sb(name + "_ls", [P, NT])
        lane0 = c.sb(name + "_lane0", [P, P])
        ge = c.sb(name + "_ge", [P, NT, P])
        idx = c.sb(name + "_idx", [P, NT], I32)
        idf = c.sb(name + "_idf", [P, NT])
        summed, iotad, step = (c.sem(name + s) for s in ("_summed", "_iotad", "_step"))
        with k.nc.Block() as block:
            @block.tensor
            def _(pe):
                pe.matmul(pt[:, 0:NT], k.before[:, :], counts[:, :], start=True, stop=True)
                pe.matmul(pt[:, NT:2 * NT], k.ones[:, :], counts[:, :], start=True, stop=True).then_inc(summed, 1)

            @block.gpsimd
            def _(g):
                g.iota(idx[:, :], pattern=[[P, NT]], base=E, channel_multiplier=1).then_inc(iotad, 1)

            @block.vector
            def _(v):
                ch = Chain(v, step)
                ch(v.memset(ge[:, 0, 0:NT], 1.0))
                v.wait_ge(summed, 1)
                ch(v.tensor_copy(tot[:, :], pt[:, NT:2 * NT]))
                ch(v.tensor_tensor_scan(run[:, :], ge[:, 0, 0:NT], tot[:, :], 0.0, ALU.mult, ALU.add))
                ch(v.tensor_tensor(run[:, :], run[:, :], tot[:, :], ALU.subtract))
                ch(v.tensor_tensor(start[:, :], run[:, :], pt[:, 0:NT], ALU.add))
                ch(v.tensor_scalar(order["some"][:, :], counts[:, :], 0.5, None, ALU.is_gt))
                ch(v.tensor_scalar(order["none_neg"][:, :], order["some"][:, :], 1.0, BIG, ALU.subtract, ALU.mult))
                ch(v.tensor_tensor(endf[:, :], start[:, :], counts[:, :], ALU.add))
                ch(v.tensor_scalar(endf[:, :], endf[:, :], 1.0, 0.0, ALU.subtract, ALU.max))
                ch(v.tensor_copy(order["end"][:, :], endf[:, :]))
                ch(v.tensor_scalar(lane0[:, :], k.iota[:, :], float(lane_edges), float(lane_edges), ALU.mult, ALU.add))
                for pos, lane in ((endf, le), (start, ls)):
                    ch(v.tensor_tensor(ge[:, :, :], bc(pos[:, :], [P, NT, P], 2), bc(lane0[:, :], [P, NT, P], 1),
                                       ALU.is_ge))
                    ch(v.tensor_reduce(lane[:, :], ge[:, :, :], axis=AX.X, op=ALU.add))
                ch(v.tensor_copy(order["end_lane"][:, :], le[:, :]))
                ch(v.tensor_tensor(order["cross"][:, :], le[:, :], ls[:, :], ALU.is_gt))
                ch(v.tensor_tensor(order["cross"][:, :], order["cross"][:, :], order["some"][:, :], ALU.mult))
                v.wait_ge(iotad, 1)
                ch(v.tensor_copy(idf[:, :], idx[:, :]))
                ch(v.tensor_tensor(endf[:, :], start[:, :], idf[:, :], ALU.subtract))
                ch(v.tensor_tensor(endf[:, :], endf[:, :], order["some"][:, :], ALU.mult))
                ch(v.tensor_tensor(endf[:, :], endf[:, :], idf[:, :], ALU.add))
                ch(v.tensor_copy(order["begin"][:, :], endf[:, :]))


def new_order(k, name):
    o = {}
    for f in ("start", "some", "none_neg", "cross", "count"):
        o[f] = k.sb(f"{name}_{f}", [P, NT])
    for f in ("end", "end_lane", "begin"):
        o[f] = k.sb(f"{name}_{f}", [P, NT], I32)
    for f in ("mend_from", "mend_to"):
        o[f] = k.sb(f"{name}_{f}", [P, 1], I32)
    o["whole_row"] = k.dram(f"{name}_whole_row", [1, P])
    return o



def scan_chunk(v, ch, data, keep, carry, F, op=ALU.mult, op1=ALU.add, at=0):
    for f in range(F):
        ch.loose(v.tensor_tensor_scan(data[:, :, at + f], keep, data[:, :, at + f], carry[:, f:f + 1], op, op1))
    ch.wait()
    ch(v.tensor_copy(carry[:, 0:F], data[:, CH - 1, at:at + F]))


def histograms(k, c, name):
    digits_of = ((k.dst_lo, k.dst_hi), (k.src_lo, k.src_hi))
    counts = (k.by_dst["count"], k.by_src["count"], k.src_direct)
    oh_lo = [c.sb(f"{name}_oh_lo{o}", [P, GRP, P], BF16) for o in range(2)]
    oh_hi = [c.sb(f"{name}_oh_hi{o}", [P, GRP, NT], BF16) for o in range(2)]
    acc = [c.ps(f"{name}_acc{o}", [P, 512]) for o in range(3)]
    cleared, ready, used, counted, zero_made, zeroed = (
        c.sem(name + s) for s in ("_cleared", "_ready", "_used", "_counted", "_zero_made", "_zeroed"))
    zeros = c.sb(name + "_zeros", [P, SPREAD_PIECE])

    def scalar(a):
        a.wait_ge(zero_made, 1)
        flat = k.spread_buf[:].rearrange("(r p f) -> r p f", p=P, f=SPREAD_PIECE)
        for r in range(SPREAD_PIECES):
            a.dma_start(flat[r], zeros[:, :]).then_inc(zeroed, 16)
        a.wait_ge(zeroed, 16 * SPREAD_PIECES)

    def vector_first(v):
        v.memset(zeros[:, :], 0.0).then_inc(zero_made, 1)
        for o in range(2):
            v.memset(oh_lo[o][:, :, :], 0.0).then_inc(cleared, 1)
        v.wait_ge(cleared, 2)

    def vector(v, ch, i, q):
        at = bass.ds(i * CH + q * GRP, GRP)
        v.wait_ge(used, i * NG + q + 1)
        for o, (lo, hi) in enumerate(digits_of):
            v.tensor_tensor(oh_lo[o][:, :, :], bc(lo[:, at], [P, GRP, P], 2),
                            bc(k.iota[:, :], [P, GRP, P], 1), ALU.is_equal).then_inc(ready, 1)
            v.tensor_tensor(oh_hi[o][:, :, :], bc(hi[:, at], [P, GRP, NT], 2),
                            bc(k.iota[:, 0:NT], [P, GRP, NT], 1), ALU.is_equal).then_inc(ready, 1)

    def vector_last(v):
        v.wait_ge(used, NCH * NG + 1)
        for o in range(3):
            v.tensor_copy(counts[o][:, :], acc[o][:, 0:NT]).then_inc(counted, 1)

    def tensor_first(pe):
        pe.wait_ge(cleared, 2)
        for o in range(3):
            mm = pe.matmul(acc[o][:, 0:NT], oh_lo[0][:, 0, :], oh_lo[0][:, 1, 0:NT], start=True, stop=True,
                           skip_group_check=True)
        mm.then_inc(used, 1)

    def tensor(pe, i, q, direct):
        pe.wait_ge(ready, (i * NG + q) * 4 + 4)
        for o in range(2):
            for g in range(GRP):
                mm = pe.matmul(acc[2 if o and direct else o][:, 0:NT], oh_lo[o][:, g, :], oh_hi[o][:, g, :], start=False, stop=True,
                               skip_group_check=True)
        mm.then_inc(used, 1)

    return Side(vector, tensor, 0, [(0, DG, True), (DG, NG, False)], vector_first=vector_first, vector_last=vector_last, tensor_first=tensor_first,
                scalar=scalar)


class Side:

    def __init__(self, vector, tensor, steps, ranges, vector_first=None, vector_last=None, tensor_first=None,
                 scalar=None):
        none = lambda eng: None
        self.vector, self.tensor, self.steps, self.ranges = vector, tensor, steps, ranges
        self.groups = sum(end - start for start, end, _ in ranges)
        self.vector_first, self.vector_last = vector_first or none, vector_last or none
        self.tensor_first, self.scalar = tensor_first or none, scalar or none

    def vector_groups(self, v, ch, i):
        v.nop(nofuse=True)
        for start, end, _ in self.ranges:
            v.nop(nofuse=True)
            with v.Fori(0, end - start) as q:
                ch.enter(q, self.steps)
                self.vector(v, ch, i, q + start)
                ch.leave(end - start, self.steps)

    def tensor_groups(self, pe, i):
        for start, end, direct in self.ranges:
            with pe.Fori(start, end) as q:
                self.tensor(pe, i, q, direct)


def gat_gather(k, name, table, F, heads, edges, maxes, carry, side):
    FX = F - heads
    with ExitStack() as st:
        c = Ctx(k.nc, st)
        G = [c.sb(f"{name}_G{b}", [P, CH, F]) for b in range(2)]
        S = [c.sb(f"{name}_S{b}", [P, CH, heads]) for b in range(2)]
        stage = [c.sb(f"{name}_stage{b}", [P, CH], I32) for b in range(2)]
        neg = c.sb(name + "_neg", [P, CH])
        side = side(k, c, name + "h")
        staged = [c.sem(f"{name}_staged{b}") for b in range(2)]
        got = [c.pool_dma_sem(f"{name}_got{b}") for b in range(2)]
        stored = [c.sem(f"{name}_stored{b}") for b in range(2)]
        scanned, step = c.sem(name + "_scanned"), c.sem(name + "_step")
        with k.nc.Block() as block:
            @block.gpsimd
            def _(g):
                over_chunks(g, lambda i, b, j: gather_column_loop(
                    g, k, i, j, b, table, G, stage, staged, stored, 32, got, k.src_i))

            @block.vector
            def _(v):
                ch = Chain(v, step)
                ch(v.memset(carry[:, 0:heads], -BIG))
                side.vector_first(v)

                def chunk(i, b, j):
                    side.vector_groups(v, ch, i)
                    v.wait_ge(stored[b], (j + 1) * 32)
                    ch(v.tensor_scalar(neg[:, :], k.keep_d[:, cols(i)], 1.0, BIG, ALU.subtract, ALU.mult))
                    v.wait_ge(got[b], (j + 1) * (16 * CH))
                    for h in range(heads):
                        ch.loose(v.tensor_tensor_scan(S[b][:, :, h], neg[:, :], G[b][:, :, FX + h],
                                                      carry[:, h:h + 1], ALU.add, ALU.max))
                    ch.wait()
                    v.tensor_copy(carry[:, 0:heads], S[b][:, CH - 1, :]).then_inc(scanned, 1)
                    v.wait_ge(scanned, i + 1)
                over_chunks(v, chunk, ch, 1 + heads + side.groups * side.steps)
                side.vector_last(v)

            @block.tensor
            def _(pe):
                side.tensor_first(pe)
                over_chunks(pe, lambda i, b, j: side.tensor_groups(pe, i))

            @block.scalar
            def _(a):
                side.scalar(a)

            @block.sync
            def _(s):
                for b in range(2):
                    s.sem_inc(stored[b], 32)

                def chunk(i, b, j):
                    s.wait_ge(scanned, i + 1)
                    s.dma_start(edges.rearrange("p (c f) -> p c f", f=F)[:, cols(i), :],
                                G[b][:, :, :]).then_inc(stored[b], 16)
                    s.dma_start(rows(maxes)[:, cols(i), :], S[b][:, :, :]).then_inc(stored[b], 16)
                over_chunks(s, chunk)
                s.wait_ge(stored[0], 32 * (PAIRS + 2))
                s.wait_ge(stored[1], 32 * (PAIRS + 1))


def gat_weigh(k, name, F, heads, edges, scans, first, carry):
    FX = F - heads
    FO = heads * FX + heads
    with ExitStack() as st:
        c = Ctx(k.nc, st)
        G = [c.sb(f"{name}_G{b}", [P, CH, F]) for b in range(2)]
        X = [c.sb(f"{name}_X{b}", [P, CH, 2 * heads]) for b in range(2)]
        W = [c.sb(f"{name}_W{b}", [P, CH, FO]) for b in range(2)]
        begin = c.sb(name + "_begin", [P, CH])
        e1 = c.sb(name + "_e1", [P, CH, heads])
        loaded = [c.sem(f"{name}_loaded{b}") for b in range(2)]
        stored = [c.sem(f"{name}_stored{b}") for b in range(2)]
        scanned, step, logits, probs = (c.sem(name + s) for s in ("_scanned", "_step", "_logits", "_probs"))
        with k.nc.Block() as block:
            @block.sync
            def _(s):
                for b in range(2):
                    s.sem_inc(stored[b], 16)

                def load(i, b):
                    s.dma_start(G[b][:, :, :],
                                edges.rearrange("p (c f) -> p c f", f=F)[:, cols(i), :]).then_inc(loaded[b], 16)
                    s.dma_start(X[b][:, :, :],
                                rows(table_view(k, 2 * heads, E))[:, cols(i), :]).then_inc(loaded[b], 16)

                def chunk(i, b, j, more):
                    s.wait_ge(scanned, i + 1)
                    s.dma_start(rows(scans)[:, cols(i), :], W[b][:, :, :]).then_inc(stored[b], 16)
                    if more:
                        load(i + 2, b)
                load(0, 0)
                load(1, 1)
                with s.Fori(0, PAIRS - 1) as j:
                    chunk(2 * j, 0, j, True)
                    chunk(2 * j + 1, 1, j, True)
                chunk(NCH - 3, 0, PAIRS - 1, True)
                chunk(NCH - 2, 1, PAIRS - 1, False)
                chunk(NCH - 1, 0, PAIRS, False)
                s.wait_ge(stored[0], 16 * (PAIRS + 2))
                s.wait_ge(stored[1], 16 * (PAIRS + 1))

            @block.vector
            def _(v):
                ch = Chain(v, step)
                ch(v.memset(carry[:, 0:FO], 0.0))

                def chunk(i, b, j):
                    keep = k.keep_d[:, cols(i)]
                    v.wait_ge(loaded[b], (j + 1) * 32)
                    ch(v.tensor_scalar(begin[:, :], keep, -1.0, 1.0, ALU.mult, ALU.add))
                    ch(v.tensor_tensor(X[b][:, :, :], X[b][:, :, :], bc(begin[:, :], [P, CH, 2 * heads], 2),
                                       ALU.mult))
                    scan_chunk(v, ch, X[b], keep, first, 2 * heads)
                    ch(v.tensor_tensor(e1[:, :, :], G[b][:, :, FX:F], X[b][:, :, 0:heads], ALU.add))
                    ch(v.scalar_tensor_tensor(out=e1[:, :, :], in0=e1[:, :, :], scalar=0.2, in1=e1[:, :, :],
                                              op0=ALU.mult, op1=ALU.max))
                    v.wait_ge(stored[b], (j + 1) * 16)
                    v.tensor_tensor(W[b][:, :, heads * FX:FO], e1[:, :, :], X[b][:, :, heads:2 * heads],
                                    ALU.subtract).then_inc(logits, 1)
                    v.wait_ge(probs, i + 1)
                    for h in range(heads):
                        ch.loose(v.tensor_tensor(W[b][:, :, h * FX:(h + 1) * FX], G[b][:, :, 0:FX],
                                                 bc(W[b][:, :, heads * FX + h], [P, CH, FX], 2), ALU.mult))
                    ch.wait()
                    for f in range(FO):
                        ch.loose(v.tensor_tensor_scan(W[b][:, :, f], keep, W[b][:, :, f], carry[:, f:f + 1],
                                                      ALU.mult, ALU.add))
                    ch.wait()
                    v.tensor_copy(carry[:, 0:FO], W[b][:, CH - 1, :]).then_inc(scanned, 1)
                    v.wait_ge(scanned, i + 1)
                over_chunks(v, chunk, ch, 5 + 3 * heads + FO)

            @block.scalar
            def _(a):
                def chunk(i, b, j):
                    a.wait_ge(logits, i + 1)
                    a.activation(W[b][:, :, heads * FX:FO], W[b][:, :, heads * FX:FO], ACT.Exp).then_inc(probs, 1)
                over_chunks(a, chunk)


def gcn_gather(k, name, table, scans, carry, side):
    with ExitStack() as st:
        c = Ctx(k.nc, st)
        G = [c.sb(f"{name}_G{b}", [P, CH, D]) for b in range(2)]
        stage = [c.sb(f"{name}_stage{b}", [P, CH], I32) for b in range(2)]
        staged = [c.sem(f"{name}_staged{b}") for b in range(2)]
        got = [c.pool_dma_sem(f"{name}_got{b}") for b in range(2)]
        stored = [c.sem(f"{name}_stored{b}") for b in range(2)]
        scanned, step = c.sem(name + "_scanned"), c.sem(name + "_step")
        side = side(k, c, name + "h")
        with k.nc.Block() as block:
            @block.gpsimd
            def _(g):
                over_chunks(g, lambda i, b, j: gather_column_loop(
                    g, k, i, j, b, table, G, stage, staged, stored, 16, got, k.src_i))

            @block.vector
            def _(v):
                ch = Chain(v, step)
                ch(v.memset(carry[:, 0:D], 0.0))
                side.vector_first(v)

                def chunk(i, b, j):
                    side.vector_groups(v, ch, i)
                    v.wait_ge(got[b], (j + 1) * (16 * CH))
                    for f in range(D):
                        ch.loose(v.tensor_tensor_scan(G[b][:, :, f], k.keep_d[:, cols(i)], G[b][:, :, f],
                                                      carry[:, f:f + 1], ALU.mult, ALU.add))
                    ch.wait()
                    v.tensor_copy(carry[:, 0:D], G[b][:, CH - 1, :]).then_inc(scanned, 1)
                    v.wait_ge(scanned, i + 1)
                over_chunks(v, chunk, ch, D + side.groups * side.steps)
                side.vector_last(v)

            @block.tensor
            def _(pe):
                side.tensor_first(pe)
                over_chunks(pe, lambda i, b, j: side.tensor_groups(pe, i))

            @block.scalar
            def _(a):
                side.scalar(a)

            @block.sync
            def _(s):
                for b in range(2):
                    s.sem_inc(stored[b], 16)

                def chunk(i, b, j):
                    s.wait_ge(scanned, i + 1)
                    s.dma_start(rows(scans)[:, cols(i), :], G[b][:, :, :]).then_inc(stored[b], 16)
                over_chunks(s, chunk)
                s.wait_ge(stored[0], 16 * (PAIRS + 2))
                s.wait_ge(stored[1], 16 * (PAIRS + 1))


def count_in_group(k, c, name):
    pB = c.ps(name + "_pB", [P, 1024])
    junk = [c.sb(f"{name}_junk{g}", [P, (g + 1) * P]) for g in range(GRP)]
    src_f = c.sb(name + "_src_f", [P, GRP])
    rowed, used = c.sem(name + "_rowed"), c.sem(name + "_used")

    def vector(v, ch, i, q):
        at = bass.ds(i * CH + q * GRP, GRP)
        ch(v.tensor_copy(src_f[:, :], k.src_i[:, at]))
        n = i * SG + (q - DG)
        v.wait_ge(rowed, n + 1)
        for g in range(GRP):
            ins = v.scalar_tensor_tensor(out=junk[g][:, :], in0=pB[:, 0:(g + 1) * P],
                                         scalar=src_f[:, g:g + 1], in1=k.earlier[:, (GRP - 1 - g) * P:],
                                         op0=ALU.is_equal, op1=ALU.mult, accum_out=k.cnt5[:, g:g + 1])
            ch.loose(ins)
        ch.wait()
        v.tensor_copy(k.cnt[:, at], k.cnt5[:, :]).then_inc(used, 1)
        v.wait_ge(used, n + 2)

    def tensor(pe, i, q, direct):
        pe.wait_ge(used, i * SG + (q - DG) + 1)
        for g in range(GRP):
            at = bass.ds(i * CH + q * GRP + g, 1)
            pe.matmul(pB[:, g * P:(g + 1) * P], k.src_lo[:, at].to_broadcast([P, P]), k.ident_b[:, :],
                      start=True, stop=False)
            mm = pe.matmul(pB[:, g * P:(g + 1) * P], k.src_hi[:, at].to_broadcast([P, P]), k.ident128_b[:, :],
                           start=False, stop=True)
        mm.then_inc(rowed, 1)

    return Side(vector, tensor, 1 + GRP, [(DG, NG, False)], tensor_first=lambda pe: pe.sem_inc(used, 1))


def count_before_group(k, c, name, q0, groups, table_in):
    pB = c.ps(name + "_pB", [P, 1024])
    pT = c.ps(name + "_pT", [P, 512])
    pR = c.ps(name + "_pR", [P, 512])
    table = k.free_place
    oh_lo = c.sb(name + "_oh_lo", [P, GRP, P], BF16)
    oh_hi = c.sb(name + "_oh_hi", [P, GRP, NT], BF16)
    loT = c.sb(name + "_loT", [P, GRP, P])
    prod = c.sb(name + "_prod", [P, GRP, NT])
    r5 = c.sb(name + "_r5", [P, GRP])
    rowed, hot, hotT, looked, added, copied, ranked = (
        c.sem(name + s) for s in ("_rowed", "_hot", "_hotT", "_looked", "_added", "_copied", "_ranked"))

    def vector(v, ch, i, q):
        n = i * groups + (q - q0)
        at = bass.ds(i * CH + q * GRP, GRP)
        v.wait_ge(added, n + 1)
        v.tensor_tensor(oh_lo[:, :, :], bc(k.src_lo[:, at], [P, GRP, P], 2), bc(k.iota[:, :], [P, GRP, P], 1),
                        ALU.is_equal).then_inc(hot, 1)
        ch(v.tensor_tensor(oh_hi[:, :, :], bc(k.src_hi[:, at], [P, GRP, NT], 2),
                           bc(k.iota[:, 0:NT], [P, GRP, NT], 1), ALU.is_equal))
        v.wait_ge(rowed, n + 1)
        v.tensor_scalar(loT[:, :, :], pB[:, 0:GRP * P].rearrange("p (g q) -> p g q", g=GRP), k.part[:, 0:1], None,
                        ALU.is_equal).then_inc(hotT, 1)
        v.wait_ge(looked, n + 1)
        ch(v.tensor_tensor(prod[:, :, :], pR[:, 0:GRP * NT].rearrange("p (g t) -> p g t", g=GRP), oh_hi[:, :, :],
                           ALU.mult))
        ch(v.tensor_reduce(r5[:, :], prod[:, :, :], axis=AX.X, op=ALU.add))
        v.tensor_tensor(k.rank[:, at], r5[:, :], k.cnt[:, at], ALU.add).then_inc(ranked, 1)
        v.wait_ge(ranked, n + 1)

    def tensor_first(pe):
        pe.matmul(pT[:, 0:NT], k.ident[:, :], table_in[:, :], start=True, stop=True,
                  skip_group_check=True).then_inc(added, 1)

    def tensor(pe, i, q, direct):
        n = i * groups + (q - q0)
        for g in range(GRP):
            at = bass.ds(i * CH + q * GRP + g, 1)
            mm = pe.matmul(pB[:, g * P:(g + 1) * P], k.src_lo[:, at].to_broadcast([P, P]), k.ident_b[:, :],
                           start=True, stop=True)
        mm.then_inc(rowed, 1)
        pe.wait_ge(hotT, n + 1)
        pe.wait_ge(copied, n + 1)
        for g in range(GRP):
            mm = pe.matmul(pR[:, g * NT:(g + 1) * NT], loT[:, g, :], table[:, :], start=True, stop=True)
        mm.then_inc(looked, 1)
        for g in range(GRP):
            mm = pe.matmul(pT[:, 0:NT], oh_lo[:, g, :], oh_hi[:, g, :], start=False, stop=True,
                           skip_group_check=True)
        mm.then_inc(added, 1)

    def scalar(a):
        with a.Fori(0, NCH * groups + 1) as n:
            a.wait_ge(added, n + 1)
            a.activation(table[:, :], pT[:, 0:NT], ACT.Copy).then_inc(copied, 1)

    return Side(vector, tensor, 3, [(q0, q0 + groups, False)], tensor_first=tensor_first, scalar=scalar)


def scatter_column_loop(g, k, i, j, b, view, M, stage, staged, ready, sent, parts=1):
    g.tensor_copy(stage[b][:, :], k.rank[:, bass.ds(i * CH + DC, SC)]).then_inc(staged[b], 1)
    g.wait_ge(staged[b], j + 1)
    for t in range(SC):
        if parts == 1 and t == 0 or parts > 1 and t % GRP == 0:
            g.wait_ge(ready, i + 1 if parts == 1 else i * NG + (DG + t // GRP + 1))
            g.nop(nofuse=True)
        g.indirect_dma_start(out=view, in_=M[b][:, DC + t, :], in_offset=None,
                             out_offset=bass.IndirectOffsetOnAxis(ap=stage[b][:, t:t + 1], axis=0)
                             ).then_inc(sent[b], 16)


class DirectSums:
    BANKS = 4

    def __init__(self, c, name, wide):
        self.wide = wide
        self.oh_lo = [c.sb(f"{name}_ohl{b}", [P, P]) for b in range(2)]
        self.oh_hi = [c.sb(f"{name}_ohh{b}", [P, NT]) for b in range(2)]
        self.acc = c.ps(name + "_acc", [P, self.BANKS, 512])
        self.made, self.added, self.hot, self.out_sem = (
            c.sem(name + s) for s in ("_made", "_added", "_hot", "_outs"))
        self.w = NT // self.BANKS

    def vector_first(self, v):
        for b in range(2):
            v.memset(self.wide[b][:, :, :], 0.0).then_inc(self.hot, 1)
            v.memset(self.oh_lo[b][:, :], 0.0).then_inc(self.hot, 1)
        v.wait_ge(self.hot, 4)

    def tensor_first(self, pe):
        pe.wait_ge(self.hot, 4)
        for b in range(2):
            self.products(pe, b, b == 0)

    def products(self, pe, b, start):
        for q in range(self.BANKS):
            mm = pe.matmul(self.acc[:, q, 0:self.w * D], self.oh_lo[b][:, :],
                           self.wide[b][:, q * self.w:(q + 1) * self.w, :].rearrange("p t d -> p (t d)"),
                           start=start, stop=True, skip_group_check=True)
        mm.then_inc(self.added, 1)

    def vector(self, v, k, M, i, d, b):
        m = i * DC + d
        at = bass.ds(i * CH + d, 1)
        v.wait_ge(self.added, m + 1)
        v.tensor_tensor(self.oh_lo[b][:, :], k.iota[:, :], k.src_lo[:, at].to_broadcast([P, P]),
                        ALU.is_equal).then_inc(self.made, 1)
        v.tensor_tensor(self.oh_hi[b][:, :], k.iota[:, 0:NT], k.src_hi[:, at].to_broadcast([P, NT]),
                        ALU.is_equal).then_inc(self.hot, 1)
        v.wait_ge(self.hot, m + 5)
        v.tensor_tensor(self.wide[b][:, :, :], bc(self.oh_hi[b][:, :], [P, NT, D], 2),
                        M[:, bass.ds(d, 1), 0:D].to_broadcast([P, NT, D]), ALU.mult).then_inc(self.made, 1)

    def tensor(self, pe, i, d, b):
        pe.wait_ge(self.made, (i * DC + d) * 2 + 2)
        self.products(pe, b, False)

    def vector_last(self, v, out):
        v.wait_ge(self.added, NCH * DC + 2)
        for q in range(self.BANKS):
            v.tensor_copy(out[:, q * self.w:(q + 1) * self.w, :],
                          self.acc[:, q, 0:self.w * D].rearrange("p (t d) -> p t d", d=D)).then_inc(self.out_sem, 1)


def release_messages(g, b, j, sent, mfree):
    g.wait_ge(sent[b], (j + 1) * (16 * SC))
    g.nop(nofuse=True).then_inc(mfree[b], 1)


def sheaf_edges(k, name, table, scans, messages, first, carry, w1, b1, w2, b2, direct, wide):
    F = D + 1
    with ExitStack() as st:
        c = Ctx(k.nc, st)
        G = [c.sb(f"{name}_G{b}", [P, CH, F]) for b in range(2)]
        X = [c.sb(f"{name}_X{b}", [P, CH, F]) for b in range(2)]
        M = [c.sb(f"{name}_M{b}", [P, CH, F]) for b in range(2)]
        O = c.sb(name + "_O", [P, CH, D])
        stage = [c.sb(f"{name}_stage{b}", [P, CH], I32) for b in range(2)]
        rstage = [c.sb(f"{name}_rstage{b}", [P, SC], I32) for b in range(2)]
        V = c.sb(name + "_V", [P, CH, 2, D])
        T = c.sb(name + "_T", [P, CH, 2, D])
        dots = c.sb(name + "_dots", [P, CH, 4])
        sq = c.sb(name + "_sq", [P, GRP, 4, D])
        dot = c.sb(name + "_dot", [P, CH])
        begin = c.sb(name + "_begin", [P, CH])
        pair = c.sb(name + "_pair", [P, GRP, 2, D])
        pairT = c.sb(name + "_pairT", [2 * D, 2, GRP * P // 2])
        hid = c.sb(name + "_hid", [P, 2, GRP * P // 2])
        both = c.ps(name + "_pTV", [P, 1024])
        pT, pV = both[0:2 * D, 0:GRP * P], both[:, GRP * P:GRP * P + GRP * 2 * D]
        pH = c.ps(name + "_pH", [P, 2, 512])
        sums = DirectSums(c, name + "d", wide)
        staged = [c.sem(f"{name}_staged{b}") for b in range(2)]
        rstaged = [c.sem(f"{name}_rstaged{b}") for b in range(2)]
        got = [c.pool_dma_sem(f"{name}_got{b}") for b in range(2)]
        free = [c.sem(f"{name}_free{b}") for b in range(2)]
        sent = [c.pool_dma_sem(f"{name}_sent{b}") for b in range(2)]
        mfree = [c.sem(f"{name}_mfree{b}") for b in range(2)]
        loaded = [c.sem(f"{name}_loaded{b}") for b in range(2)]
        stored = c.sem(name + "_stored")
        messaged, scanned, step, paired, transposed, copied, hidden, relued, vectored, evacuated = (
            c.sem(name + s) for s in ("_messaged", "_scanned", "_step", "_paired", "_transposed", "_copied",
                                      "_hidden", "_relued", "_vectored", "_evacuated"))
        HALF = GRP * P // 2
        with k.nc.Block() as block:
            @block.gpsimd
            def _(g):
                def gather(i, b, j):
                    gather_column_loop(g, k, i, j, b, table, G, stage, staged, free, 1, got, k.src_i)

                def scatter(i, b, j):
                    scatter_column_loop(g, k, i, j, b, messages, M, rstage, rstaged, messaged, sent)
                for b in range(2):
                    g.sem_inc(mfree[b], 1)
                gather(0, 0, 0)
                with g.Fori(0, PAIRS) as j:
                    gather(2 * j + 1, 1, j)
                    scatter(2 * j, 0, j)
                    gather(2 * j + 2, 0, j + 1)
                    release_messages(g, 0, j, sent, mfree)
                    scatter(2 * j + 1, 1, j)
                    release_messages(g, 1, j, sent, mfree)
                scatter(NCH - 1, 0, PAIRS)
                g.wait_ge(sent[0], 16 * SC * (PAIRS + 1))

            @block.vector
            def _(v):
                for b in range(2):
                    v.sem_inc(free[b], 1)
                ch = Chain(v, step)
                ch(v.memset(carry[:, 0:D], 0.0))
                sums.vector_first(v)

                def take_off(out, y, n, part):
                    ch(v.tensor_tensor(T[:, :, 1, :], V[:, :, n, :], bc(part, [P, CH, D], 2), ALU.mult))
                    ch(v.tensor_tensor(out, y, T[:, :, 1, :], ALU.subtract))

                def reflect(out, y, n):
                    tmp = T[:, :, 1, :]
                    ch(v.tensor_tensor(tmp, y, V[:, :, n, :], ALU.mult))
                    ch(v.tensor_reduce(dot[:, :], tmp, axis=AX.X, op=ALU.add))
                    ch(v.tensor_tensor(dot[:, :], dot[:, :], dots[:, :, n], ALU.mult))
                    take_off(out, y, n, dot[:, :])

                def chunk(i, b, j, direct_before):
                    keep = k.keep_d[:, cols(i)]
                    v.wait_ge(loaded[b], (j + 1) * 16)
                    ch(v.tensor_scalar(begin[:, :], keep, -1.0, 1.0, ALU.mult, ALU.add))
                    ch(v.tensor_tensor(X[b][:, :, :], X[b][:, :, :], bc(begin[:, :], [P, CH, F], 2), ALU.mult))
                    scan_chunk(v, ch, X[b], keep, first, F)
                    v.wait_ge(got[b], (j + 1) * (16 * CH))

                    def pair_group(q):
                        at = bass.ds(q * GRP, GRP)
                        ch(v.tensor_copy(pair[:, :, 0, :], G[b][:, at, 0:D]))
                        v.tensor_copy(pair[:, :, 1, :], X[b][:, at, 0:D]).then_inc(paired, 1)

                    def evacuate(q):
                        v.wait_ge(vectored, i * NG + q + 1)
                        v.tensor_tensor(V[:, bass.ds(q * GRP, GRP), :, :].rearrange("p c n d -> p c (n d)"),
                                        pV[:, 0:GRP * 2 * D].rearrange("p (c n) -> p c n", c=GRP),
                                        bc(b2[:, :], [P, GRP, 2 * D], 1), ALU.add).then_inc(evacuated, 1)
                    def group_dots(q):
                        at = bass.ds(q * GRP, GRP)
                        ch.loose(v.tensor_tensor(sq[:, :, 0:2, :], V[:, at, :, :], V[:, at, :, :], ALU.mult))
                        ch.loose(v.tensor_tensor(sq[:, :, 2, :], V[:, at, 0, :], G[b][:, at, 0:D], ALU.mult))
                        ch(v.tensor_tensor(sq[:, :, 3, :], V[:, at, 1, :], X[b][:, at, 0:D], ALU.mult))
                        ch(v.tensor_reduce(dots[:, at, :], sq[:, :, :, :], axis=AX.X, op=ALU.add))

                    def spread_column(d, half):
                        if direct_before:
                            sums.vector(v, k, M[1 - b], i - 1, d, half)

                    def group_step(q, half=None):
                        v.wait_ge(transposed, i * NG + q + 1)
                        pair_group(q + 1)
                        v.wait_ge(evacuated, i * NG + q)
                        group_dots(q - 1)
                        if half is not None:
                            spread_column(q, half)
                        evacuate(q)
                    pair_group(0)
                    v.wait_ge(transposed, i * NG + 1)
                    pair_group(1)
                    spread_column(0, 0)
                    evacuate(0)
                    with v.Fori(0, DC // 2 - 1) as m:
                        ch.enter(m, 10)
                        group_step(2 * m + 1, 1)
                        group_step(2 * m + 2, 0)
                        ch.leave(DC // 2 - 1, 10)
                    group_step(DC - 1, 1)
                    with v.Fori(DC, NG - 1) as q:
                        ch.enter(q - DC, 5)
                        group_step(q)
                        ch.leave(NG - 1 - DC, 5)
                    v.wait_ge(evacuated, i * NG + (NG - 1))
                    group_dots(NG - 2)
                    evacuate(NG - 1)
                    v.wait_ge(evacuated, (i + 1) * NG)
                    group_dots(NG - 1)
                    lengths = dots[:, :, 0:2]
                    ch(v.tensor_scalar(lengths, lengths, 1e-24, None, ALU.max))
                    ch(v.reciprocal(lengths, lengths))
                    ch(v.tensor_scalar(lengths, lengths, 2.0, None, ALU.mult))
                    ch(v.tensor_tensor(dots[:, :, 2:4], dots[:, :, 2:4], lengths, ALU.mult))
                    if direct_before:
                        v.wait_ge(sums.made, i * (2 * DC))
                    A = T[:, :, 0, :]
                    v.wait_ge(mfree[b], j + 1)
                    take_off(A, X[b][:, :, 0:D], 1, dots[:, :, 3])
                    reflect(A, A, 0)
                    ch(v.tensor_tensor(M[b][:, :, 0:D], A, bc(X[b][:, :, D], [P, CH, D], 2), ALU.mult))
                    v.tensor_copy(M[b][:, :, D], k.src_i[:, cols(i)]).then_inc(messaged, 1)
                    v.wait_ge(stored, (i + 1) * 16)
                    take_off(A, G[b][:, :, 0:D], 0, dots[:, :, 2])
                    reflect(A, A, 1)
                    v.tensor_tensor(O[:, :, :], A, bc(G[b][:, :, D], [P, CH, D], 2),
                                    ALU.mult).then_inc(free[b], 1)
                    v.wait_ge(free[b], j + 2)
                    for f in range(D):
                        ch.loose(v.tensor_tensor_scan(O[:, :, f], keep, O[:, :, f], carry[:, f:f + 1],
                                                      ALU.mult, ALU.add))
                    ch.wait()
                    v.tensor_copy(carry[:, 0:D], O[:, CH - 1, :]).then_inc(scanned, 1)
                    v.wait_ge(scanned, i + 1)
                per = 2 + F + 1 + 5 * NG + 4 + 2 * (2 + 5) + 1 + D
                chunk(0, 0, 0, False)
                with v.Fori(0, PAIRS) as j:
                    ch.enter(j, 2 * per)
                    chunk(2 * j + 1, 1, j, True)
                    chunk(2 * j + 2, 0, j + 1, True)
                    ch.leave(PAIRS, 2 * per)
                v.nop(nofuse=True)
                with v.Fori(0, DC // 2) as m:
                    sums.vector(v, k, M[0], NCH - 1, 2 * m, 0)
                    sums.vector(v, k, M[0], NCH - 1, 2 * m + 1, 1)
                sums.vector_last(v, direct)

            @block.tensor
            def _(pe):
                def chunk(i, direct_before):
                    def transpose(n):
                        pe.wait_ge(paired, n + 1)
                        pe.nop(nofuse=True)
                        for g in range(GRP):
                            mm = pe.transpose(pT[:, g * P:(g + 1) * P],
                                              pair[:, g, :, :].rearrange("p n d -> p (n d)"), k.ident[:, :])
                        mm.then_inc(transposed, 1)

                    def hidden_layer(n):
                        pe.wait_ge(copied, n + 1)
                        for h in range(2):
                            mm = pe.matmul(pH[:, h, 0:HALF], w1[:, :], pairT[:, h, :], start=True, stop=True)
                        mm.then_inc(hidden, 1)

                    def vectors(n):
                        pe.wait_ge(relued, n + 1)
                        flat = hid[:, :, :].rearrange("p a q -> p (a q)")
                        for g in range(GRP):
                            mm = pe.matmul(pV[:, g * 2 * D:(g + 1) * 2 * D], flat[:, g * P:(g + 1) * P], w2[:, :],
                                           start=True, stop=True)
                        mm.then_inc(vectored, 1)
                    def group_step(q, d=None, half=0):
                        hidden_layer(i * NG + q)
                        transpose(i * NG + q + 1)
                        if d is not None:
                            sums.tensor(pe, i - 1, d, half)
                        pe.wait_ge(copied, i * NG + q + 2)
                        vectors(i * NG + q)
                    transpose(i * NG)
                    group_step(0)
                    with pe.Fori(0, DC // 2) as m:
                        for half in range(2):
                            group_step(2 * m + (1 + half), 2 * m + half if direct_before else None, half)
                    with pe.Fori(DC + 1, NG - 1) as q:
                        group_step(q)
                    hidden_layer(i * NG + (NG - 1))
                    pe.wait_ge(evacuated, i * NG + (NG - 1))
                    vectors(i * NG + (NG - 1))
                sums.tensor_first(pe)
                chunk(0, False)
                with pe.Fori(0, PAIRS) as j:
                    chunk(2 * j + 1, True)
                    chunk(2 * j + 2, True)
                with pe.Fori(0, DC // 2) as m:
                    sums.tensor(pe, NCH - 1, 2 * m, 0)
                    sums.tensor(pe, NCH - 1, 2 * m + 1, 1)

            @block.scalar
            def _(a):
                def copy(n):
                    a.wait_ge(transposed, n + 1)
                    a.activation(pairT[:, :, :].rearrange("p a q -> p (a q)"), pT[:, 0:GRP * P],
                                 ACT.Copy).then_inc(copied, 1)

                def relu(n):
                    a.wait_ge(hidden, n + 1)
                    a.activation(hid[:, :, :], pH[:, :, 0:HALF], ACT.Relu, bias=b1[:, 0:1]).then_inc(relued, 1)

                def chunk(i, b, j):
                    copy(i * NG)
                    with a.Fori(0, NG - 1) as q:
                        relu(i * NG + q)
                        copy(i * NG + q + 1)
                    relu(i * NG + (NG - 1))
                over_chunks(a, chunk)

            @block.sync
            def _(s):
                s.sem_inc(stored, 16)

                def load(i, b):
                    s.dma_start(X[b][:, :, :], rows(table_view(k, F, E))[:, cols(i), :]).then_inc(loaded[b], 16)

                def chunk(i, b, j, more):
                    s.wait_ge(scanned, i + 1)
                    s.dma_start(rows(scans)[:, cols(i), :], O[:, :, :]).then_inc(stored, 16)
                    if more:
                        load(i + 2, b)
                load(0, 0)
                load(1, 1)
                with s.Fori(0, PAIRS - 1) as j:
                    chunk(2 * j, 0, j, True)
                    chunk(2 * j + 1, 1, j, True)
                chunk(NCH - 3, 0, PAIRS - 1, True)
                chunk(NCH - 2, 1, PAIRS - 1, False)
                chunk(NCH - 1, 0, PAIRS, False)
                s.wait_ge(stored, 16 * (NCH + 1))


def src_order_scan(k, name, messages, scans, carry, F, find_keep):
    with ExitStack() as st:
        c = Ctx(k.nc, st)
        G = [c.sb(f"{name}_G{b}", [P, SC, F]) for b in range(2)]
        O = [c.sb(f"{name}_O{b}", [P, SC, D]) for b in range(2)]
        prev = c.sb(name + "_prev", [P, 1])
        loaded = [c.sem(f"{name}_loaded{b}") for b in range(2)]
        stored = [c.sem(f"{name}_stored{b}") for b in range(2)]
        cleared, scanned, step, prevd, whole = (
            c.sem(name + s) for s in ("_cleared", "_scanned", "_step", "_prevd", "_whole"))
        extra = 3 if find_keep else 0
        with k.nc.Block() as block:
            @block.sync
            def _(s):
                for b in range(2):
                    s.sem_inc(stored[b], 16)
                if find_keep:
                    s.wait_ge(cleared, 1)
                    with k.nc.allow_non_contiguous_dma("one value of each lane"):
                        s.dma_start(prev[1:P, :], rows(messages, LS)[0:P - 1, LS - 1, D:D + 1]).then_inc(prevd, 16)

                def load(i, b):
                    s.dma_start(G[b][:, :, :], rows(messages, LS)[:, cols(i, SC), :]).then_inc(loaded[b], 16)

                def chunk(i, b, j, more):
                    s.wait_ge(scanned, i + 1)
                    s.dma_start(rows(scans, LS)[:, cols(i, SC), :], O[b][:, :, :]).then_inc(stored[b], 16)
                    if more:
                        load(i + 2, b)
                load(0, 0)
                load(1, 1)
                with s.Fori(0, PAIRS - 1) as j:
                    chunk(2 * j, 0, j, True)
                    chunk(2 * j + 1, 1, j, True)
                chunk(NCH - 3, 0, PAIRS - 1, True)
                chunk(NCH - 2, 1, PAIRS - 1, False)
                chunk(NCH - 1, 0, PAIRS, False)
                if find_keep:
                    s.wait_ge(whole, 1)
                    s.dma_start(k.by_src["whole_row"].rearrange("a p -> p a"), k.whole[:, :]).then_inc(whole, 16)
                    s.wait_ge(whole, 17)
                s.wait_ge(stored[0], 16 * (PAIRS + 2))
                s.wait_ge(stored[1], 16 * (PAIRS + 1))

            @block.vector
            def _(v):
                ch = Chain(v, step)
                ch(v.memset(carry[:, 0:D], 0.0))
                if find_keep:
                    v.memset(prev[:, :], -1.0).then_inc(cleared, 1)
                    v.wait_ge(prevd, 16)

                def chunk(i, b, j):
                    v.wait_ge(loaded[b], (j + 1) * 16)
                    if find_keep:
                        ids = G[b][:, :, D]
                        ch(v.tensor_tensor(k.keep_s[:, bass.ds(i * SC, 1)], ids[:, 0:1], prev[:, :], ALU.is_equal))
                        ch(v.tensor_tensor(k.keep_s[:, bass.ds(i * SC + 1, SC - 1)], ids[:, 1:SC], ids[:, 0:SC - 1],
                                           ALU.is_equal))
                        ch(v.tensor_copy(prev[:, :], ids[:, SC - 1:SC]))
                    v.wait_ge(stored[b], (j + 1) * 16)
                    for f in range(D):
                        ch.loose(v.tensor_tensor_scan(O[b][:, :, f], k.keep_s[:, cols(i, SC)], G[b][:, :, f],
                                                      carry[:, f:f + 1], ALU.mult, ALU.add))
                    ch.wait()
                    v.tensor_copy(carry[:, 0:D], O[b][:, SC - 1, :]).then_inc(scanned, 1)
                    v.wait_ge(scanned, i + 1)
                over_chunks(v, chunk, ch, D + extra)
                if find_keep:
                    v.tensor_reduce(k.whole[:, :], k.keep_s[:, :], axis=AX.X, op=ALU.min).then_inc(whole, 1)


def product_edges(k, name, attr, messages, first, w, direct, wide):
    with ExitStack() as st:
        c = Ctx(k.nc, st)
        X = [c.sb(f"{name}_X{b}", [P, CH, D]) for b in range(2)]
        A = [c.sb(f"{name}_A{b}", [P, CH, DE]) for b in range(2)]
        M = [c.sb(f"{name}_M{b}", [P, CH, D]) for b in range(2)]
        rstage = [c.sb(f"{name}_rstage{b}", [P, SC], I32) for b in range(2)]
        begin = c.sb(name + "_begin", [P, CH])
        outer = c.sb(name + "_outer", [P, GRP, D, DE])
        outT = c.sb(name + "_outT", [P, GRP * P])
        pT = c.ps(name + "_pT", [P, 1024])
        pM = c.ps(name + "_pM", [P, 512])
        sums = DirectSums(c, name + "d", wide)
        rstaged = [c.sem(f"{name}_rstaged{b}") for b in range(2)]
        sent = [c.pool_dma_sem(f"{name}_sent{b}") for b in range(2)]
        mfree = [c.sem(f"{name}_mfree{b}") for b in range(2)]
        loaded = [c.sem(f"{name}_loaded{b}") for b in range(2)]
        dfree, used, step, outered, transposed, copied, product, silued = (
            c.sem(name + s) for s in ("_dfree", "_used", "_step", "_outered", "_transposed", "_copied",
                                      "_product", "_silued"))
        norm = 1.0 / float(np.float32(np.sqrt(D * DE)))
        with k.nc.Block() as block:
            @block.gpsimd
            def _(g):
                for b in range(2):
                    g.sem_inc(mfree[b], 1)

                def scatter(i, b, j):
                    scatter_column_loop(g, k, i, j, b, messages, M, rstage, rstaged, silued, sent, NG)
                with g.Fori(0, PAIRS) as j:
                    scatter(2 * j, 0, j)
                    release_messages(g, 0, j, sent, mfree)
                    scatter(2 * j + 1, 1, j)
                    release_messages(g, 1, j, sent, mfree)
                scatter(NCH - 1, 0, PAIRS)
                g.wait_ge(sent[0], 16 * SC * (PAIRS + 1))

            @block.vector
            def _(v):
                ch = Chain(v, step)
                ch(v.memset(begin[:, :], 0.0))

                def chunk(i, b, j):
                    keep = k.keep_d[:, cols(i)]
                    v.wait_ge(loaded[b], (j + 1) * 32)
                    ch(v.tensor_scalar(begin[:, :], keep, -1.0, 1.0, ALU.mult, ALU.add))
                    ch(v.tensor_tensor(X[b][:, :, :], X[b][:, :, :], bc(begin[:, :], [P, CH, D], 2), ALU.mult))
                    scan_chunk(v, ch, X[b], keep, first, D)

                    def outer_products(q):
                        at = bass.ds(q * GRP, GRP)
                        v.wait_ge(transposed, i * NG + q + 1)
                        v.tensor_tensor(outer[:, :, :, :], bc(X[b][:, at, :], [P, GRP, D, DE], 3),
                                        bc(A[b][:, at, :], [P, GRP, D, DE], 2), ALU.mult).then_inc(outered, 1)
                    v.nop(nofuse=True)
                    with v.Fori(0, DG + 1) as q:
                        outer_products(q)
                    v.wait_ge(silued, i * NG + DG)
                    v.nop(nofuse=True)
                    with v.Fori(0, DC // 2) as m:
                        outer_products(2 * m + (DG + 1))
                        sums.vector(v, k, M[b], i, 2 * m, 0)
                        outer_products(2 * m + (DG + 2))
                        sums.vector(v, k, M[b], i, 2 * m + 1, 1)
                    v.wait_ge(sums.made, (i + 1) * (2 * DC))
                    v.wait_ge(outered, (i + 1) * NG)
                    v.sem_inc(dfree, 1)
                    v.sem_inc(used, 1)
                v.sem_inc(dfree, 2)
                sums.vector_first(v)
                over_chunks(v, chunk, ch, 2 + D + 1)
                sums.vector_last(v, direct)

            @block.tensor
            def _(pe):
                pe.sem_inc(transposed, 1)

                def transpose(n):
                    pe.wait_ge(outered, n + 1)
                    for g in range(GRP):
                        mm = pe.transpose(pT[:, g * P:(g + 1) * P],
                                          outer[:, g, :, :].rearrange("p i j -> p (i j)"), k.ident[:, :])
                    mm.then_inc(transposed, 1)

                def multiply(n):
                    pe.wait_ge(copied, n + 1)
                    for g in range(GRP):
                        mm = pe.matmul(pM[:, g * D:(g + 1) * D], outT[:, g * P:(g + 1) * P], w[:, :],
                                       start=True, stop=True)
                    mm.then_inc(product, 1)

                def chunk(i, b, j):
                    with pe.Fori(0, DG + 1) as q:
                        transpose(i * NG + q)
                        multiply(i * NG + q)
                    with pe.Fori(0, DC // 2) as m:
                        for half in range(2):
                            n = i * NG + 2 * m + (DG + 1 + half)
                            transpose(n)
                            sums.tensor(pe, i, 2 * m + half, half)
                            multiply(n)
                sums.tensor_first(pe)
                over_chunks(pe, chunk)

            @block.scalar
            def _(a):
                def chunk(i, b, j):
                    a.wait_ge(mfree[b], j + 1)
                    a.wait_ge(dfree, i + 1)
                    a.nop(nofuse=True)
                    with a.Fori(0, NG) as q:
                        n = i * NG + q
                        a.wait_ge(transposed, n + 2)
                        a.activation(outT[:, :], pT[:, 0:GRP * P], ACT.Copy).then_inc(copied, 1)
                        a.wait_ge(product, n + 1)
                        a.activation(M[b][:, bass.ds(q * GRP, GRP), :],
                                     pM[:, 0:GRP * D].rearrange("p (g d) -> p g d", g=GRP), ACT.Silu,
                                     scale=norm).then_inc(silued, 1)
                over_chunks(a, chunk)

            @block.sync
            def _(s):
                def load(i, b):
                    s.dma_start(X[b][:, :, :], rows(table_view(k, D, E))[:, cols(i), :]).then_inc(loaded[b], 16)
                    s.dma_start(A[b][:, :, :], rows(attr)[:, cols(i), :]).then_inc(loaded[b], 16)

                def next_load(i, b):
                    s.wait_ge(used, i + 1)
                    load(i + 2, b)
                load(0, 0)
                load(1, 1)
                with s.Fori(0, PAIRS - 1) as j:
                    next_load(2 * j, 0)
                    next_load(2 * j + 1, 1)
                next_load(NCH - 3, 0)



def program(nc, x, src, dst, attr, w, out):
    with ExitStack() as st:
        k = Ctx(nc, st)
        k.src_i = k.sb("src_i", [P, LANE], I32)
        k.keep_d = k.sb("keep_d", [P, LANE])
        k.ident = k.sb("ident", [P, P])
        k.iota = k.sb("iota", [P, P])
        k.part = k.sb("part", [P, 1])
        k.before = k.sb("before", [P, P])
        k.ones = k.sb("ones", [P, P])
        k.ident_b = k.sb("ident_b", [P, P], BF16)
        k.ident128_b = k.sb("ident128_b", [P, P], BF16)
        k.earlier = k.sb("earlier", [P, GRP * P])
        k.node_mask = k.sb("node_mask", [P, NT])
        k.whole = k.sb("whole", [P, 1])
        k.first_dst = k.sb("first_dst", [P, 1], I32)
        k.cnt5 = k.sb("cnt5", [P, GRP])
        k.x = k.sb("x", [P, NT, D])
        y = k.sb("y", [P, NT, D])
        carry = k.sb("carry", [P, 51])
        first = k.sb("first", [P, SPREAD_F])
        k.by_dst = new_order(k, "by_dst")
        k.by_src = new_order(k, "by_src")
        k.lanes = k.dram("lanes", [P, 51])
        k.spread_buf = k.dram("spread_buf", [SPREAD_SIZE])
        scan16 = k.dram("scan16", [E + P, D])
        k.carried = k.dram("carried", [P + 1, 51])
        tab16 = k.dram("tab16", [NP, D])
        tab16b = k.dram("tab16b", [NP, D])
        messages = k.dram("messages", [P * LS, D + 1])
        messages2 = k.dram("messages2", [P * LS, D])

        k.rank = k.sb("rank", [P, LANE], I32)
        k.keep_s = k.sb("keep_s", [P, LS])
        k.src_lo, k.src_hi = (k.sb(n, [P, LANE], BF16) for n in ("src_lo", "src_hi"))
        k.src_direct = k.sb("src_direct", [P, NT])
        with ExitStack() as s12:
            c = Ctx(nc, s12)
            k.h2 = c.sb("h2", [P, NT, C2 + 2])
            with ExitStack() as s0:
                k.dst_i = Ctx(nc, s0).sb("dst_i", [P, LANE], I32)
                setup(k, x, src, dst)
                digits(k, "ds", k.src_i, k.src_lo, k.src_hi)
            gat1(k, w, dst, carry, first, y)
            with ExitStack() as s2:
                k.cnt = Ctx(nc, s2).sb("cnt", [P, LANE])
                gat2(k, w, carry, first, y)
                gcn(k, w, carry, y, scan16, tab16, tab16b)
        sheaf(k, w, carry, first, y, scan16, messages)
        product(k, w, carry, first, y, scan16, messages2, attr)

        stored = k.sem("out_stored")
        with nc.Block() as block:
            @block.sync
            def _(s):
                s.dma_start(out[0:FULL * P, :].rearrange("(t p) f -> p t f", p=P),
                            k.x[:, 0:FULL, :]).then_inc(stored, 16)
                s.dma_start(out[FULL * P:N, :], k.x[0:REST, FULL, :]).then_inc(stored, 16)
                s.wait_ge(stored, 32)


def load_small(k, name, copies):
    with ExitStack() as st:
        loaded = Ctx(k.nc, st).sem(name + "_loaded")
        with k.nc.Block() as block:
            @block.sync
            def _(s):
                with k.nc.allow_non_contiguous_dma("small weights"):
                    for dst, src in copies:
                        s.dma_start(dst, src).then_inc(loaded, 16)
                s.wait_ge(loaded, 16 * len(copies))


def row_bc(ap, n=P):
    return ap.rearrange("(a f) -> a f", a=1).to_broadcast([n, ap.shape[0]])


def gat1(k, w, dst, carry, first, y):
    nc = k.nc
    F = D + H1
    edges = k.dram("edges1", [P, LANE * F])
    maxes, scans = k.dram("maxes1", [E + P, H1]), k.dram("scans1", [E + P, H1 * D + H1])
    tab, stab = k.dram("tab1", [NP, F]), k.dram("stab1", [NP, 2 * H1])
    h2 = k.h2
    with ExitStack() as st:
        c = Ctx(nc, st)
        w1 = c.sb("g1_w1", [D, H1 * C1])
        a1 = c.sb("g1_a1", [D, 2, H1 * C1])
        wa = c.sb("g1_wa", [D, 2, H1])
        w1d = c.sb("g1_w1d", [H1 * D, H1 * C1])
        b1 = c.sb("g1_b1", [P, H1 * C1])
        w2 = c.sb("g1_w2", [H1 * C1, C2 + 2])
        a2 = c.sb("g1_a2", [H1 * C1, 2, C2])
        t2 = c.sb("g1_t2", [H1 * C1, 2, C2])
        al = c.sb("g1_al", [P, NT, 2 * H1])
        sv = c.sb("g1_sv", [P, NT, 2 * H1])
        pself = c.sb("g1_pself", [P, NT, H1])
        vector_block(k, "g1z", lambda v, ch: ch(v.memset(w1d[:, :], 0.0)))
        load_small(k, "g1l", [
            (w1[:, :], w["L0_gnn_W1"]),
            (a1[:, 0, :], row_bc(w["L0_gnn_a_src1"].rearrange("h c -> (h c)"), D)),
            (a1[:, 1, :], row_bc(w["L0_gnn_a_dst1"].rearrange("h c -> (h c)"), D)),
            (b1[:, :], row_bc(w["L0_gnn_b1"])),
            (w2[:, 0:C2], w["L0_gnn_W2"]),
            (a2[:, 0, :], row_bc(w["L0_gnn_a_src2"].rearrange("h c -> (h c)"), H1 * C1)),
            (a2[:, 1, :], row_bc(w["L0_gnn_a_dst2"].rearrange("h c -> (h c)"), H1 * C1)),
        ] + [(w1d[D * h:D * h + D, C1 * h:C1 * h + C1], w["L0_gnn_W1"][:, C1 * h:C1 * h + C1]) for h in range(H1)])

        def fold(v, ch):
            for s in range(2):
                ch(v.tensor_tensor(a1[:, s, :], a1[:, s, :], w1[:, :], ALU.mult))
                ch(v.tensor_reduce(wa[:, s, :], a1[:, s, :].rearrange("p (h c) -> p h c", h=H1), axis=AX.X,
                                   op=ALU.add))
                ch(v.tensor_tensor(t2[:, s, :], a2[:, s, :], w2[:, 0:C2], ALU.mult))
                ch(v.tensor_reduce(w2[:, C2 + s:C2 + s + 1], t2[:, s, :], axis=AX.X, op=ALU.add))
        vector_block(k, "g1f", fold)
        node_linear(k, "g1a", k.x, wa[:, :, :].rearrange("p s h -> p (s h)"), al, D, 2 * H1)
        store_nodes(k, "g1t", [k.x[:, :, :], al[:, :, 0:H1]], tab)
        with ExitStack() as s1:
            c1 = Ctx(nc, s1)
            k.dst_lo, k.dst_hi = (c1.sb(n, [P, LANE], BF16) for n in ("dst_lo", "dst_hi"))
            with ExitStack() as s0:
                dst_i = Ctx(nc, s0).sb("dst_again", [P, LANE], I32)
                load_small(k, "dl", [(dst_i[:, :], dst.rearrange("(p c) -> p c", p=P))])
                digits(k, "dd", dst_i, k.dst_lo, k.dst_hi)
            gat_gather(k, "g1g", tab, F, H1, edges, maxes, carry, histograms)
        for name, order, lane_edges in (("g1o", k.by_dst, LANE), ("g1q", k.by_src, LS)):
            order_tables(k, name, order["count"], order, lane_edges)
        mend_tables(k, "g1m", k.by_dst, k.first_dst)
        gat_between(k, "g1", H1, al, sv, pself, maxes, stab, carry, first)
        gat_weigh(k, "g1w", F, H1, edges, scans, first, carry)
        FO = H1 * D + H1
        lane_carries(k, "g1c", carry[:, 0:FO], FO, k.by_dst, ALU.add, scans)
        with ExitStack() as s3:
            c3 = Ctx(nc, s3)
            agg = c3.sb("g1_agg", [P, NT, FO])
            h1 = c3.sb("g1_h1", [P, NT, H1 * C1])
            extract(k, "g1x", scans, k.by_dst, agg, FO, ALU.add)
            with ExitStack() as s4:
                gat_normalise(k, "g1n", agg, k.x, pself, H1, D, Ctx(nc, s4))
            node_linear(k, "g1b", agg[:, :, 0:H1 * D], w1d[:, :], h1, H1 * D, H1 * C1)
            with ExitStack() as s4:
                tmp = Ctx(nc, s4).sb("g1_tmp", [P, NT, H1 * C1])
                selu(k, "g1s", h1, tmp, b1[:, :])
            node_linear(k, "g1c2", h1, w2[:, :], h2, H1 * C1, C2 + 2)


def gat_between(k, name, heads, al, sv, pself, maxes, stab, carry, first):
    lane_carries(k, name + "m", carry[:, 0:heads], heads, k.by_dst, ALU.max, maxes)
    extract(k, name + "e", maxes, k.by_dst, pself, heads, ALU.max)
    with ExitStack() as st:
        c = Ctx(k.nc, st)
        step, logits, probs = c.sem(name + "b_step"), c.sem(name + "b_logits"), c.sem(name + "b_probs")
        with k.nc.Block() as block:
            @block.vector
            def _(v):
                ch = Chain(v, step)
                a_src, a_dst, m = al[:, :, 0:heads], al[:, :, heads:2 * heads], sv[:, :, heads:2 * heads]
                ch(v.tensor_copy(sv[:, :, 0:heads], a_dst))
                ch(v.tensor_tensor(m, pself[:, :, :], a_src, ALU.max))
                ch(v.tensor_tensor(m, m, a_dst, ALU.add))
                ch(v.scalar_tensor_tensor(out=m, in0=m, scalar=0.2, in1=m, op0=ALU.mult, op1=ALU.max))
                ch(v.tensor_tensor(pself[:, :, :], a_src, a_dst, ALU.add))
                ch(v.scalar_tensor_tensor(out=pself[:, :, :], in0=pself[:, :, :], scalar=0.2, in1=pself[:, :, :],
                                          op0=ALU.mult, op1=ALU.max))
                v.tensor_tensor(pself[:, :, :], pself[:, :, :], m, ALU.subtract).then_inc(logits, 1)

            @block.scalar
            def _(a):
                a.wait_ge(logits, 1)
                a.activation(pself[:, :, :], pself[:, :, :], ACT.Exp).then_inc(probs, 1)
    store_nodes(k, name + "u", [sv[:, :, :]], stab)
    spread(k, name + "p", sv, 2 * heads, stab, first[:, 0:2 * heads])


def gat_normalise(k, name, agg, x, pself, heads, FX, c):
    tmp = c.sb(name + "_tmp", [P, NT, FX])
    inv = c.sb(name + "_inv", [P, NT, heads])

    def body(v, ch):
        z = agg[:, :, heads * FX:heads * FX + heads]
        ch(v.tensor_tensor(inv[:, :, :], z, pself[:, :, :], ALU.add))
        ch(v.tensor_scalar(inv[:, :, :], inv[:, :, :], 1e-16, None, ALU.add))
        ch(v.reciprocal(inv[:, :, :], inv[:, :, :]))
        for h in range(heads):
            part = agg[:, :, h * FX:(h + 1) * FX]
            ch(v.tensor_tensor(tmp[:, :, :], x, bc(pself[:, :, h], [P, NT, FX], 2), ALU.mult))
            ch(v.tensor_tensor(part, part, tmp[:, :, :], ALU.add))
            ch(v.tensor_tensor(part, part, bc(inv[:, :, h], [P, NT, FX], 2), ALU.mult))
    vector_block(k, name, body)


def gat2(k, w, carry, first, y):
    nc = k.nc
    F = C2 + 1
    edges = k.dram("edges2", [P, LANE * F])
    maxes, scans = k.dram("maxes2", [E + P, 1]), k.dram("scans2", [E + P, F])
    tab, stab = k.dram("tab2", [NP, F]), k.dram("stab2", [NP, 2])
    with ExitStack() as st:
        c = Ctx(nc, st)
        b2 = c.sb("g2_b2", [P, C2])
        wf = c.sb("g2_wf", [C2, D])
        bf = c.sb("g2_bf", [P, D])
        sv = c.sb("g2_sv", [P, NT, 2])
        pself = c.sb("g2_pself", [P, NT, 1])
        load_small(k, "g2l", [(b2[:, :], row_bc(w["L0_gnn_b2"])), (wf[:, :], w["L0_gnn_Wf"]),
                              (bf[:, :], row_bc(w["L0_gnn_bf"]))])
        store_nodes(k, "g2t", [k.h2[:, :, 0:F]], tab)
        gat_gather(k, "g2g", tab, F, 1, edges, maxes, carry, count_in_group)
        gat_between(k, "g2", 1, k.h2[:, :, C2:C2 + 2], sv, pself, maxes, stab, carry, first)
        gat_weigh(k, "g2w", F, 1, edges, scans, first, carry)
        lane_carries(k, "g2c", carry[:, 0:F], F, k.by_dst, ALU.add, scans)
        with ExitStack() as s3:
            c3 = Ctx(nc, s3)
            agg = c3.sb("g2_agg", [P, NT, F])
            extract(k, "g2x", scans, k.by_dst, agg, F, ALU.add)
            with ExitStack() as s4:
                gat_normalise(k, "g2n", agg, k.h2[:, :, 0:C2], pself, 1, C2, Ctx(nc, s4))
            with ExitStack() as s4:
                tmp = Ctx(nc, s4).sb("g2_tmp", [P, NT, C2])
                selu(k, "g2s", agg[:, :, 0:C2], tmp, b2[:, :])
            node_linear(k, "g2f", agg[:, :, 0:C2], wf[:, :], y, C2, D)

        def residual(v, ch):
            ch(v.tensor_tensor(y[:, :, :], y[:, :, :], bc(bf[:, :], [P, NT, D], 1), ALU.add))
            ch(v.tensor_tensor(y[:, :, :], y[:, :, :], k.x[:, :, :], ALU.add))
        vector_block(k, "g2r", residual)
        layer_norm(k, "g2y", y, k.x)


def root_inverse(k, name, src, out, floor):
    with ExitStack() as st:
        c = Ctx(k.nc, st)
        t = c.sb(name + "_t", [P, NT])
        ready, rooted, done = c.sem(name + "_ready"), c.sem(name + "_rooted"), c.sem(name + "_done")
        with k.nc.Block() as block:
            @block.vector
            def _(v):
                v.tensor_scalar(t[:, :], src, floor, None, ALU.max).then_inc(ready, 1)
                v.wait_ge(rooted, 1)
                v.reciprocal(out, t[:, :]).then_inc(done, 1)

            @block.scalar
            def _(a):
                a.wait_ge(ready, 1)
                a.activation(t[:, :], t[:, :], ACT.Sqrt).then_inc(rooted, 1)


def gcn(k, w, carry, y, scan16, tab16, tab16b):
    nc = k.nc
    HG = 32
    with ExitStack() as st:
        c = Ctx(nc, st)
        k.free_place = c.sb("c_free_place", [P, NT])
        w1, w2 = c.sb("c_w1", [D, HG]), c.sb("c_w2", [HG, D])
        b1, gamma, beta = (c.sb(n, [P, HG]) for n in ("c_b1", "c_gamma", "c_beta"))
        b2 = c.sb("c_b2", [P, D])
        dinv = c.sb("c_dinv", [P, NT])
        xs = c.sb("c_xs", [P, NT, D])
        agg = c.sb("c_agg", [P, NT, D])
        h = c.sb("c_h", [P, NT, HG])
        load_small(k, "cl", [(w1[:, :], w["L1_gnn_W1"]), (w2[:, :], w["L1_gnn_W2"]),
                             (b1[:, :], row_bc(w["L1_gnn_b1"])), (gamma[:, :], row_bc(w["L1_gnn_gamma"])),
                             (beta[:, :], row_bc(w["L1_gnn_beta"])), (b2[:, :], row_bc(w["L1_gnn_b2"]))])
        vector_block(k, "cd", lambda v, ch: ch(v.tensor_scalar(
            dinv[:, :], k.by_dst["count"][:, :], 1.0, None, ALU.add)))
        root_inverse(k, "cr", dinv[:, :], dinv[:, :], 1.0)

        def aggregate(name, values, table, side):
            vector_block(k, name + "a", lambda v, ch: ch(v.tensor_tensor(
                xs[:, :, :], values, bc(dinv[:, :], [P, NT, D], 2), ALU.mult)))
            store_nodes(k, name + "b", [xs[:, :, :]], table)
            gcn_gather(k, name + "c", table, scan16, carry, side)
            lane_carries(k, name + "d", carry[:, 0:D], D, k.by_dst, ALU.add, scan16)
            extract(k, name + "e", scan16, k.by_dst, agg, D, ALU.add)

            def finish(v, ch):
                ch(v.tensor_tensor(agg[:, :, :], agg[:, :, :], xs[:, :, :], ALU.add))
                ch(v.tensor_tensor(agg[:, :, :], agg[:, :, :], bc(dinv[:, :], [P, NT, D], 2), ALU.mult))
            vector_block(k, name + "f", finish)

        half = SG // 2 + 1
        aggregate("c1", k.x[:, :, :], tab16, lambda k, c, n: count_before_group(
            k, c, n, DG, half, k.by_src["start"]))
        node_linear(k, "ch", agg, w1[:, :], h, D, HG)
        batch_norm_relu(k, "cn", h, b1, gamma, beta, HG)
        node_linear(k, "co", h, w2[:, :], y, HG, D)
        aggregate("c2", y[:, :, :], tab16b, lambda k, c, n: count_before_group(
            k, c, n, DG + half, SG - half, k.free_place))

        def residual(v, ch):
            ch(v.tensor_tensor(y[:, :, :], agg[:, :, :], bc(b2[:, :], [P, NT, D], 1), ALU.add))
            ch(v.tensor_tensor(y[:, :, :], y[:, :, :], k.x[:, :, :], ALU.add))
        vector_block(k, "cs", residual)
        layer_norm(k, "cy", y, k.x)


def batch_norm_relu(k, name, h, b1, gamma, beta, HG):
    with ExitStack() as st:
        c = Ctx(k.nc, st)
        t = c.sb(name + "_t", [P, NT, HG])
        part = c.sb(name + "_part", [P, HG])
        mean = c.sb(name + "_mean", [P, HG])
        var = c.sb(name + "_var", [P, HG])
        pS = c.ps(name + "_pS", [P, 512])
        step, ready, summed, rooted = (c.sem(name + s) for s in ("_step", "_ready", "_summed", "_rooted"))
        shape = [P, NT, HG]
        with k.nc.Block() as block:
            @block.tensor
            def _(pe):
                for n in range(2):
                    pe.wait_ge(ready, n + 1)
                    pe.matmul(pS[:, n * HG:(n + 1) * HG], k.ones[:, :], part[:, :],
                              start=True, stop=True).then_inc(summed, 1)

            @block.scalar
            def _(a):
                a.wait_ge(ready, 3)
                a.activation(var[:, :], var[:, :], ACT.Sqrt).then_inc(rooted, 1)

            @block.vector
            def _(v):
                ch = Chain(v, step)
                ch(v.tensor_tensor(h[:, :, :], h[:, :, :], bc(b1[:, :], shape, 1), ALU.add))
                ch(v.tensor_tensor(t[:, :, :], h[:, :, :], bc(k.node_mask[:, :], shape, 2), ALU.mult))
                v.tensor_reduce(part[:, :], t[:, :, :].rearrange("p t f -> p f t"), axis=AX.X,
                                op=ALU.add).then_inc(ready, 1)
                v.wait_ge(summed, 1)
                ch(v.tensor_scalar(mean[:, :], pS[:, 0:HG], 1.0 / N, None, ALU.mult))
                ch(v.tensor_tensor(h[:, :, :], h[:, :, :], bc(mean[:, :], shape, 1), ALU.subtract))
                ch(v.tensor_tensor(t[:, :, :], h[:, :, :], h[:, :, :], ALU.mult))
                ch(v.tensor_tensor(t[:, :, :], t[:, :, :], bc(k.node_mask[:, :], shape, 2), ALU.mult))
                v.tensor_reduce(part[:, :], t[:, :, :].rearrange("p t f -> p f t"), axis=AX.X,
                                op=ALU.add).then_inc(ready, 1)
                v.wait_ge(summed, 2)
                v.tensor_scalar(var[:, :], pS[:, HG:2 * HG], 1.0 / N, 1e-5, ALU.mult, ALU.add).then_inc(ready, 1)
                v.wait_ge(rooted, 1)
                ch(v.reciprocal(var[:, :], var[:, :]))
                ch(v.tensor_tensor(var[:, :], var[:, :], gamma[:, :], ALU.mult))
                ch(v.tensor_tensor(h[:, :, :], h[:, :, :], bc(var[:, :], shape, 1), ALU.mult))
                ch(v.tensor_tensor(h[:, :, :], h[:, :, :], bc(beta[:, :], shape, 1), ALU.add))
                ch(v.tensor_scalar(h[:, :, :], h[:, :, :], 0.0, None, ALU.max))


def sheaf(k, w, carry, first, y, scan16, messages):
    nc = k.nc
    tab = k.dram("tab5", [NP, D + 1])
    with ExitStack() as st:
        c = Ctx(nc, st)
        w1 = c.sb("s_w1", [2 * D, 2, HID])
        b1 = c.sb("s_b1", [2 * HID, 1])
        w2 = c.sb("s_w2", [2 * HID, 2, D])
        b2 = c.sb("s_b2", [P, 2 * D])
        xd = c.sb("s_xd", [P, NT, D + 1])
        direct = c.sb("s_direct", [P, NT, D])
        agg = c.sb("s_agg", [P, NT, D])
        vector_block(k, "sz", lambda v, ch: ch(v.memset(w2[:, :, :], 0.0)))
        W1, W2 = w["L2_gnn_W1"], w["L2_gnn_W2"]
        load_small(k, "sl", [
            (w1[0:2 * D, 0, :], W1.rearrange("h i -> i h")),
            (w1[0:D, 1, :], W1[:, D:2 * D].rearrange("h i -> i h")),
            (w1[D:2 * D, 1, :], W1[:, 0:D].rearrange("h i -> i h")),
            (b1[0:HID, :], w["L2_gnn_b1"].rearrange("(h a) -> h a", a=1)),
            (b1[HID:2 * HID, :], w["L2_gnn_b1"].rearrange("(h a) -> h a", a=1)),
            (w2[0:HID, 0, :], W2.rearrange("o h -> h o")),
            (w2[HID:2 * HID, 1, :], W2.rearrange("o h -> h o")),
            (b2[:, 0:D], row_bc(w["L2_gnn_b2"])), (b2[:, D:2 * D], row_bc(w["L2_gnn_b2"]))])

        def degrees(v, ch):
            ch(v.tensor_copy(xd[:, :, 0:D], k.x[:, :, :]))
            ch(v.tensor_tensor(xd[:, :, D], k.by_dst["count"][:, :], k.by_src["count"][:, :], ALU.add))
            ch(v.tensor_tensor(xd[:, :, D], xd[:, :, D], k.src_direct[:, :], ALU.add))
        vector_block(k, "sd", degrees)
        root_inverse(k, "sr", xd[:, :, D], xd[:, :, D], 1e-5)
        store_nodes(k, "st", [xd[:, :, :]], tab)
        spread(k, "sp", xd, D + 1, tab, first[:, 0:D + 1])
        sheaf_edges(k, "se", tab, scan16, messages, first, carry,
                    w1[:, :, :].rearrange("p a h -> p (a h)"), b1, w2[:, :, :].rearrange("p a h -> p (a h)"), b2,
                    direct, (y, agg))
        lane_carries(k, "sc", carry[:, 0:D], D, k.by_dst, ALU.add, scan16)
        extract(k, "sx", scan16, k.by_dst, agg, D, ALU.add)
        first_src = c.sb("s_first_src", [P, 1], I32)
        first_src_f = c.sb("s_first_src_f", [P, 1])
        load_small(k, "sf", [(first_src_f[:, :], rows(messages, LS)[:, 0, D:D + 1])])
        vector_block(k, "si", lambda v, ch: ch(v.tensor_copy(first_src[:, :], first_src_f[:, :])))
        mend_tables(k, "sm", k.by_src, first_src)
        src_order_scan(k, "ss", messages, scan16, carry, D + 1, True)
        lane_carries(k, "sq", carry[:, 0:D], D, k.by_src, ALU.add, scan16)
        extract(k, "sw", scan16, k.by_src, y, D, ALU.add)

        def residual(v, ch):
            ch(v.tensor_tensor(y[:, :, :], y[:, :, :], agg[:, :, :], ALU.add))
            ch(v.tensor_tensor(y[:, :, :], y[:, :, :], direct[:, :, :], ALU.add))
            ch(v.tensor_tensor(y[:, :, :], y[:, :, :], bc(xd[:, :, D], [P, NT, D], 2), ALU.mult))
            ch(v.tensor_tensor(y[:, :, :], y[:, :, :], k.x[:, :, :], ALU.add))
            ch(v.tensor_scalar(y[:, :, :], y[:, :, :], 0.0, None, ALU.max))
            ch(v.tensor_tensor(y[:, :, :], y[:, :, :], k.x[:, :, :], ALU.add))
        vector_block(k, "sv", residual)
        layer_norm(k, "sy", y, k.x)


def product(k, w, carry, first, y, scan16, messages, attr):
    nc = k.nc
    tab = k.dram("tab6", [NP, D])
    norm_lin = 1.0 / float(np.float32(np.sqrt(D)))
    norm_upd = 1.0 / float(np.float32(np.sqrt(D * D)))
    with ExitStack() as st:
        c = Ctx(nc, st)
        wm = c.sb("p_wm", [P, D])
        wl = c.sb("p_wl", [D, D])
        wu = c.sb("p_wu", [P, 2, D])
        wo = c.sb("p_wo", [D, D])
        agg = c.sb("p_agg", [P, NT, D])
        direct = c.sb("p_direct", [P, NT, D])
        load_small(k, "pl", [
            (wm[:, :], w["L3_gnn_W_msg_tp"].rearrange("i j h -> (i j) h")), (wl[:, :], w["L3_gnn_W_msg_lin"]),
            (wu[:, 0, :], w["L3_gnn_W_upd_tp"][0:D // 2].rearrange("i j h -> (i j) h")),
            (wu[:, 1, :], w["L3_gnn_W_upd_tp"][D // 2:D].rearrange("i j h -> (i j) h")),
            (wo[:, :], w["L3_gnn_W_upd_lin"])])
        store_nodes(k, "pt", [k.x[:, :, :]], tab)
        spread(k, "pp", k.x, D, tab, first[:, 0:D])
        product_edges(k, "pe", attr, messages, first, wm, direct, (y, agg))
        src_order_scan(k, "ps", messages, scan16, carry, D, False)
        lane_carries(k, "pc", carry[:, 0:D], D, k.by_src, ALU.add, scan16)
        extract(k, "px", scan16, k.by_src, y, D, ALU.add)
        vector_block(k, "pj", lambda v, ch: ch(v.tensor_tensor(y[:, :, :], y[:, :, :], direct[:, :, :], ALU.add)))
        node_linear(k, "pn", y, wl[:, :], agg, D, D)
        vector_block(k, "pq", lambda v, ch: ch(v.tensor_scalar(
            agg[:, :, :], agg[:, :, :], norm_lin, None, ALU.mult)))
        u = c.sb("p_u", [P, NT, D])
        for half in range(2):
            with ExitStack() as s3:
                o = Ctx(nc, s3).sb(f"p_o{half}", [P, NT, D // 2, D])

                def outer(v, ch):
                    for i in range(D // 2):
                        n = half * (D // 2) + i
                        ch(v.tensor_tensor(o[:, :, i, :], agg[:, :, :], bc(k.x[:, :, n], [P, NT, D], 2), ALU.mult))
                vector_block(k, f"po{half}", outer)
                node_linear(k, f"pm{half}", o[:, :, :, :].rearrange("p t i d -> p t (i d)"), wu[:, half, :],
                            u if half else y, P, D)
        with ExitStack() as s3:
            c3 = Ctx(nc, s3)
            summed, silued = c3.sem("pa_summed"), c3.sem("pa_silued")
            with nc.Block() as block:
                @block.vector
                def _(v):
                    v.tensor_tensor(u[:, :, :], u[:, :, :], y[:, :, :], ALU.add).then_inc(summed, 1)

                @block.scalar
                def _(a):
                    a.wait_ge(summed, 1)
                    a.activation(u[:, :, :], u[:, :, :], ACT.Silu, scale=norm_upd).then_inc(silued, 1)
        node_linear(k, "pw", u, wo[:, :], y, D, D)

        def residual(v, ch):
            ch(v.scalar_tensor_tensor(out=y[:, :, :], in0=y[:, :, :], scalar=norm_lin, in1=k.x[:, :, :],
                                      op0=ALU.mult, op1=ALU.add))
            ch(v.tensor_tensor(y[:, :, :], y[:, :, :], k.x[:, :, :], ALU.add))
        vector_block(k, "pr", residual)
        layer_norm(k, "py", y, k.x)


_EDGE = ["x", "src", "dst", "edge_attr_8"]
_WEIGHTS = ["L0_gnn_W1", "L0_gnn_a_src1", "L0_gnn_a_dst1", "L0_gnn_b1", "L0_gnn_W2", "L0_gnn_a_src2",
            "L0_gnn_a_dst2", "L0_gnn_b2", "L0_gnn_Wf", "L0_gnn_bf", "L1_gnn_W1", "L1_gnn_b1", "L1_gnn_gamma",
            "L1_gnn_beta", "L1_gnn_W2", "L1_gnn_b2", "L2_gnn_W1", "L2_gnn_b1", "L2_gnn_W2", "L2_gnn_b2",
            "L3_gnn_W_msg_tp", "L3_gnn_W_msg_lin", "L3_gnn_W_upd_tp", "L3_gnn_W_upd_lin"]


def kernel(**inputs):
    import numpy as _np
    import concourse.bacc as _bacc
    from concourse import mybir as _mybir
    from concourse.bass_utils import run_bass_kernel_spmd as _run

    nc = _bacc.Bacc("TRN2", target_bir_lowering=False, num_devices=1)
    arrays, args = {}, {}
    for name in _EDGE + _WEIGHTS:
        a = _np.ascontiguousarray(inputs[name])
        arrays[f"in_{name}_dram"] = a
        args[name] = nc.dram_tensor(f"in_{name}_dram", a.shape, _mybir.dt.from_np(a.dtype), kind="ExternalInput").ap()
    out = nc.dram_tensor("out_0_dram", (N, D), F32, kind="ExternalOutput").ap()
    program(nc, args["x"], args["src"], args["dst"], args["edge_attr_8"], args, out)
    r = _run(nc, [arrays], core_ids=[0])
    return r.results[0]["out_0_dram"]
```
